# Optimizing a Trainium2 kernel written in Bass

```python
import numpy as np
import jax
import jax.numpy as jnp

def _softmax(x, axis=-1):
    return jax.nn.softmax(x, axis=axis)

def _gelu(x):
    return jax.nn.gelu(x, approximate=True)

def _silu(x):
    return jax.nn.silu(x)

def _sigmoid(x):
    return jax.nn.sigmoid(x)

def _layernorm(x, axis=-1, eps=1e-05):
    m = jnp.mean(x, axis=axis, keepdims=True)
    v = jnp.var(x, axis=axis, keepdims=True)
    return (x - m) / jnp.sqrt(v + eps)

def _scatter_add(tgt, idx, src, axis=0):
    return tgt.at[idx].add(src)

def _segment_sum(src, seg, n):
    return jax.ops.segment_sum(src, seg, n)
kernel_name = 'mk_metaformer_d2_conv_nchw1024_r4_d5f992'

def setup_inputs(seed: int=0):
    np.random.seed(seed)
    _w = jnp.asarray

    def _rec_inputs():
        import jax
        import jax.numpy as jnp
        _gk = jax.random.key(seed)
        x = -0.0006537 + 1.001 * jax.random.normal(jax.random.fold_in(_gk, 1), (4, 256, 24, 24), jnp.float32)
        return x
    x = _rec_inputs()

    def _L0_conv_setup():
        import jax, jax.numpy as jnp
        import numpy as np
        DIM = 256
        R = 2
        D_MODEL = DIM // (R * R)
        D_INNER = 2 * D_MODEL
        D_STATE = 16
        D_CONV = 4
        DT_RANK = (D_MODEL + 15) // 16
        NUM_TOKENS = 1

        def pixel_shuffle(x, r):
            B, C, H, W = x.shape
            c = C // (r * r)
            x = x.reshape(B, c, r, r, H, W)
            x = x.transpose(0, 1, 4, 2, 5, 3)
            return x.reshape(B, c, H * r, W * r)

        def pixel_unshuffle(x, r):
            B, C, Hr, Wr = x.shape
            H, W = (Hr // r, Wr // r)
            x = x.reshape(B, C, H, r, W, r)
            x = x.transpose(0, 1, 3, 5, 2, 4)
            return x.reshape(B, C * r * r, H, W)

        def mamba_block(seq, in_proj_w, conv_w, conv_b, x_proj_w, dt_proj_w, dt_proj_b, A_log, D, out_proj_w):
            B, L, _ = seq.shape
            xz = jnp.einsum('bld,ed->ble', seq, in_proj_w)
            u, z = jnp.split(xz, 2, axis=-1)
            up = jnp.pad(u, ((0, 0), (D_CONV - 1, 0), (0, 0)))
            u = sum((up[:, k:k + L, :] * conv_w[:, k] for k in range(D_CONV))) + conv_b
            u = jax.nn.silu(u)
            x_dbl = jnp.einsum('bld,ed->ble', u, x_proj_w)
            dt, Bm, Cm = jnp.split(x_dbl, [DT_RANK, DT_RANK + D_STATE], axis=-1)
            dt = jax.nn.softplus(jnp.einsum('blr,dr->bld', dt, dt_proj_w) + dt_proj_b)
            A = -jnp.exp(A_log)

            def step(h, inputs):
                dt_t, B_t, C_t, u_t = inputs
                dA = jnp.exp(dt_t[:, :, None] * A)
                h = dA * h + (dt_t * u_t)[:, :, None] * B_t[:, None, :]
                y = jnp.einsum('bdn,bn->bd', h, C_t)
                return (h, y)
            h0 = jnp.zeros((B, D_INNER, D_STATE), dtype=seq.dtype)
            xs = (dt.transpose(1, 0, 2), Bm.transpose(1, 0, 2), Cm.transpose(1, 0, 2), u.transpose(1, 0, 2))
            _, ys = jax.lax.scan(step, h0, xs)
            y = ys.transpose(1, 0, 2) + u * D
            y = y * jax.nn.silu(z)
            return jnp.einsum('bld,ed->ble', y, out_proj_w)
        key = jax.random.key(seed)
        ks = jax.random.split(key, 12)
        s = lambda k, shape, scale=0.02: jax.random.normal(k, shape, dtype=jnp.float32) * scale
        inp = {'x': jax.random.normal(ks[0], (4, DIM, 24, 24), dtype=jnp.float32), 'global_token': jnp.zeros((1, NUM_TOKENS, D_MODEL), dtype=jnp.float32), 'in_proj_w': s(ks[1], (2 * D_INNER, D_MODEL)), 'conv_w': s(ks[2], (D_INNER, D_CONV), 0.1), 'conv_b': jnp.zeros((D_INNER,), dtype=jnp.float32), 'x_proj_w': s(ks[3], (DT_RANK + 2 * D_STATE, D_INNER)), 'dt_proj_w': s(ks[4], (D_INNER, DT_RANK), 0.1), 'dt_proj_b': jax.random.uniform(ks[5], (D_INNER,), dtype=jnp.float32, minval=-4.0, maxval=-2.0), 'A_log': jnp.log(jnp.broadcast_to(jnp.arange(1, D_STATE + 1, dtype=jnp.float32), (D_INNER, D_STATE))), 'D': jnp.ones((D_INNER,), dtype=jnp.float32), 'out_proj_w': s(ks[6], (D_MODEL, D_INNER))}
        return inp
    _L0_conv_all = _L0_conv_setup()
    _L0_conv_in = {k: v for k, v in _L0_conv_all.items() if k in ('global_token', 'in_proj_w', 'conv_w', 'conv_b', 'x_proj_w', 'dt_proj_w', 'dt_proj_b', 'A_log', 'D', 'out_proj_w')}
    del _L0_conv_all

    def _L0_ffn_setup():
        import jax, jax.numpy as jnp
        import numpy as np
        NUM_EXPERTS = 8
        TOP_K = 2
        key = jax.random.key(seed)
        k1, k2, k3, k4 = jax.random.split(key, 4)
        B, S, D, E, F = (2, 512, 256, NUM_EXPERTS, 4 * 256)
        scale = 0.02
        return {'x': jax.random.normal(k1, (B, S, D), dtype=jnp.float32), 'gate_w': jax.random.normal(k2, (E, D), dtype=jnp.float32) * scale, 'w1': jax.random.normal(k3, (E, F, D), dtype=jnp.float32) * scale, 'w2': jax.random.normal(k4, (E, D, F), dtype=jnp.float32) * scale}
    _L0_ffn_all = _L0_ffn_setup()
    _L0_ffn_in = {k: v for k, v in _L0_ffn_all.items() if k in ('gate_w', 'w1', 'w2')}
    del _L0_ffn_all

    def _L1_conv_setup():
        import jax, jax.numpy as jnp
        import numpy as np
        DIM = 256
        R = 2
        D_MODEL = DIM // (R * R)
        D_INNER = 2 * D_MODEL
        D_STATE = 16
        D_CONV = 4
        DT_RANK = (D_MODEL + 15) // 16
        NUM_TOKENS = 1

        def pixel_shuffle(x, r):
            B, C, H, W = x.shape
            c = C // (r * r)
            x = x.reshape(B, c, r, r, H, W)
            x = x.transpose(0, 1, 4, 2, 5, 3)
            return x.reshape(B, c, H * r, W * r)

        def pixel_unshuffle(x, r):
            B, C, Hr, Wr = x.shape
            H, W = (Hr // r, Wr // r)
            x = x.reshape(B, C, H, r, W, r)
            x = x.transpose(0, 1, 3, 5, 2, 4)
            return x.reshape(B, C * r * r, H, W)

        def mamba_block(seq, in_proj_w, conv_w, conv_b, x_proj_w, dt_proj_w, dt_proj_b, A_log, D, out_proj_w):
            B, L, _ = seq.shape
            xz = jnp.einsum('bld,ed->ble', seq, in_proj_w)
            u, z = jnp.split(xz, 2, axis=-1)
            up = jnp.pad(u, ((0, 0), (D_CONV - 1, 0), (0, 0)))
            u = sum((up[:, k:k + L, :] * conv_w[:, k] for k in range(D_CONV))) + conv_b
            u = jax.nn.silu(u)
            x_dbl = jnp.einsum('bld,ed->ble', u, x_proj_w)
            dt, Bm, Cm = jnp.split(x_dbl, [DT_RANK, DT_RANK + D_STATE], axis=-1)
            dt = jax.nn.softplus(jnp.einsum('blr,dr->bld', dt, dt_proj_w) + dt_proj_b)
            A = -jnp.exp(A_log)

            def step(h, inputs):
                dt_t, B_t, C_t, u_t = inputs
                dA = jnp.exp(dt_t[:, :, None] * A)
                h = dA * h + (dt_t * u_t)[:, :, None] * B_t[:, None, :]
                y = jnp.einsum('bdn,bn->bd', h, C_t)
                return (h, y)
            h0 = jnp.zeros((B, D_INNER, D_STATE), dtype=seq.dtype)
            xs = (dt.transpose(1, 0, 2), Bm.transpose(1, 0, 2), Cm.transpose(1, 0, 2), u.transpose(1, 0, 2))
            _, ys = jax.lax.scan(step, h0, xs)
            y = ys.transpose(1, 0, 2) + u * D
            y = y * jax.nn.silu(z)
            return jnp.einsum('bld,ed->ble', y, out_proj_w)
        key = jax.random.key(seed)
        ks = jax.random.split(key, 12)
        s = lambda k, shape, scale=0.02: jax.random.normal(k, shape, dtype=jnp.float32) * scale
        inp = {'x': jax.random.normal(ks[0], (4, DIM, 24, 24), dtype=jnp.float32), 'global_token': jnp.zeros((1, NUM_TOKENS, D_MODEL), dtype=jnp.float32), 'in_proj_w': s(ks[1], (2 * D_INNER, D_MODEL)), 'conv_w': s(ks[2], (D_INNER, D_CONV), 0.1), 'conv_b': jnp.zeros((D_INNER,), dtype=jnp.float32), 'x_proj_w': s(ks[3], (DT_RANK + 2 * D_STATE, D_INNER)), 'dt_proj_w': s(ks[4], (D_INNER, DT_RANK), 0.1), 'dt_proj_b': jax.random.uniform(ks[5], (D_INNER,), dtype=jnp.float32, minval=-4.0, maxval=-2.0), 'A_log': jnp.log(jnp.broadcast_to(jnp.arange(1, D_STATE + 1, dtype=jnp.float32), (D_INNER, D_STATE))), 'D': jnp.ones((D_INNER,), dtype=jnp.float32), 'out_proj_w': s(ks[6], (D_MODEL, D_INNER))}
        return inp
    _L1_conv_all = _L1_conv_setup()
    _L1_conv_in = {k: v for k, v in _L1_conv_all.items() if k in ('global_token', 'in_proj_w', 'conv_w', 'conv_b', 'x_proj_w', 'dt_proj_w', 'dt_proj_b', 'A_log', 'D', 'out_proj_w')}
    del _L1_conv_all

    def _L1_ffn_setup():
        import jax, jax.numpy as jnp
        import numpy as np
        N_EXPERTS = 8
        N_GROUP = 4
        TOPK_GROUP = 2
        TOP_K = 2
        HIDDEN = 256
        INTER = 512
        B, S = (1, 256)

        def _grouped_topk(scores):
            T, E = scores.shape
            per_group = E // N_GROUP
            group_scores = scores.reshape(T, N_GROUP, per_group).max(-1)
            _, gidx = jax.lax.top_k(group_scores, TOPK_GROUP)
            gmask = jnp.zeros((T, N_GROUP), scores.dtype).at[jnp.arange(T)[:, None], gidx].set(1.0)
            smask = jnp.repeat(gmask, per_group, axis=1)
            masked = jnp.where(smask > 0, scores, 0.0)
            topk_w, topk_ids = jax.lax.top_k(masked, TOP_K)
            topk_w = topk_w / topk_w.sum(-1, keepdims=True)
            return (topk_ids, topk_w)
        key = jax.random.key(seed)
        k1, k2, k3, k4 = jax.random.split(key, 4)
        return {'hidden_states': jax.random.normal(k1, (B, S, HIDDEN), jnp.float32), 'gate_w': jax.random.normal(k2, (N_EXPERTS, HIDDEN), jnp.float32) * 0.02, 'w13_weight': jax.random.normal(k3, (N_EXPERTS, 2 * INTER, HIDDEN), jnp.float32) * 0.02, 'w2_weight': jax.random.normal(k4, (N_EXPERTS, HIDDEN, INTER), jnp.float32) * 0.02}
    _L1_ffn_all = _L1_ffn_setup()
    _L1_ffn_in = {k: v for k, v in _L1_ffn_all.items() if k in ('gate_w', 'w13_weight', 'w2_weight')}
    del _L1_ffn_all
    return {'x': x, 'L0_conv_global_token': _L0_conv_in['global_token'], 'L0_conv_in_proj_w': _L0_conv_in['in_proj_w'], 'L0_conv_conv_w': _L0_conv_in['conv_w'], 'L0_conv_conv_b': _L0_conv_in['conv_b'], 'L0_conv_x_proj_w': _L0_conv_in['x_proj_w'], 'L0_conv_dt_proj_w': _L0_conv_in['dt_proj_w'], 'L0_conv_dt_proj_b': _L0_conv_in['dt_proj_b'], 'L0_conv_A_log': _L0_conv_in['A_log'], 'L0_conv_D': _L0_conv_in['D'], 'L0_conv_out_proj_w': _L0_conv_in['out_proj_w'], 'L0_ffn_gate_w': _L0_ffn_in['gate_w'], 'L0_ffn_w1': _L0_ffn_in['w1'], 'L0_ffn_w2': _L0_ffn_in['w2'], 'L1_conv_global_token': _L1_conv_in['global_token'], 'L1_conv_in_proj_w': _L1_conv_in['in_proj_w'], 'L1_conv_conv_w': _L1_conv_in['conv_w'], 'L1_conv_conv_b': _L1_conv_in['conv_b'], 'L1_conv_x_proj_w': _L1_conv_in['x_proj_w'], 'L1_conv_dt_proj_w': _L1_conv_in['dt_proj_w'], 'L1_conv_dt_proj_b': _L1_conv_in['dt_proj_b'], 'L1_conv_A_log': _L1_conv_in['A_log'], 'L1_conv_D': _L1_conv_in['D'], 'L1_conv_out_proj_w': _L1_conv_in['out_proj_w'], 'L1_ffn_gate_w': _L1_ffn_in['gate_w'], 'L1_ffn_w13_weight': _L1_ffn_in['w13_weight'], 'L1_ffn_w2_weight': _L1_ffn_in['w2_weight']}

def reference(x, L0_conv_global_token, L0_conv_in_proj_w, L0_conv_conv_w, L0_conv_conv_b, L0_conv_x_proj_w, L0_conv_dt_proj_w, L0_conv_dt_proj_b, L0_conv_A_log, L0_conv_D, L0_conv_out_proj_w, L0_ffn_gate_w, L0_ffn_w1, L0_ffn_w2, L1_conv_global_token, L1_conv_in_proj_w, L1_conv_conv_w, L1_conv_conv_b, L1_conv_x_proj_w, L1_conv_dt_proj_w, L1_conv_dt_proj_b, L1_conv_A_log, L1_conv_D, L1_conv_out_proj_w, L1_ffn_gate_w, L1_ffn_w13_weight, L1_ffn_w2_weight):
    import jax
    import jax.numpy as jnp

    def _L0_conv_ref(x, global_token, in_proj_w, conv_w, conv_b, x_proj_w, dt_proj_w, dt_proj_b, A_log, D, out_proj_w):
        import jax, jax.numpy as jnp
        import numpy as np
        DIM = 256
        R = 2
        D_MODEL = DIM // (R * R)
        D_INNER = 2 * D_MODEL
        D_STATE = 16
        D_CONV = 4
        DT_RANK = (D_MODEL + 15) // 16
        NUM_TOKENS = 1

        def pixel_shuffle(x, r):
            B, C, H, W = x.shape
            c = C // (r * r)
            x = x.reshape(B, c, r, r, H, W)
            x = x.transpose(0, 1, 4, 2, 5, 3)
            return x.reshape(B, c, H * r, W * r)

        def pixel_unshuffle(x, r):
            B, C, Hr, Wr = x.shape
            H, W = (Hr // r, Wr // r)
            x = x.reshape(B, C, H, r, W, r)
            x = x.transpose(0, 1, 3, 5, 2, 4)
            return x.reshape(B, C * r * r, H, W)

        def mamba_block(seq, in_proj_w, conv_w, conv_b, x_proj_w, dt_proj_w, dt_proj_b, A_log, D, out_proj_w):
            B, L, _ = seq.shape
            xz = jnp.einsum('bld,ed->ble', seq, in_proj_w)
            u, z = jnp.split(xz, 2, axis=-1)
            up = jnp.pad(u, ((0, 0), (D_CONV - 1, 0), (0, 0)))
            u = sum((up[:, k:k + L, :] * conv_w[:, k] for k in range(D_CONV))) + conv_b
            u = jax.nn.silu(u)
            x_dbl = jnp.einsum('bld,ed->ble', u, x_proj_w)
            dt, Bm, Cm = jnp.split(x_dbl, [DT_RANK, DT_RANK + D_STATE], axis=-1)
            dt = jax.nn.softplus(jnp.einsum('blr,dr->bld', dt, dt_proj_w) + dt_proj_b)
            A = -jnp.exp(A_log)

            def step(h, inputs):
                dt_t, B_t, C_t, u_t = inputs
                dA = jnp.exp(dt_t[:, :, None] * A)
                h = dA * h + (dt_t * u_t)[:, :, None] * B_t[:, None, :]
                y = jnp.einsum('bdn,bn->bd', h, C_t)
                return (h, y)
            h0 = jnp.zeros((B, D_INNER, D_STATE), dtype=seq.dtype)
            xs = (dt.transpose(1, 0, 2), Bm.transpose(1, 0, 2), Cm.transpose(1, 0, 2), u.transpose(1, 0, 2))
            _, ys = jax.lax.scan(step, h0, xs)
            y = ys.transpose(1, 0, 2) + u * D
            y = y * jax.nn.silu(z)
            return jnp.einsum('bld,ed->ble', y, out_proj_w)
        B, C, H, W = x.shape
        xs = pixel_shuffle(x, R)
        seq = xs.reshape(B, D_MODEL, -1).transpose(0, 2, 1)
        tok = jnp.broadcast_to(global_token, (B, NUM_TOKENS, D_MODEL))
        seq = jnp.concatenate([tok, seq], axis=1)
        seq = mamba_block(seq, in_proj_w, conv_w, conv_b, x_proj_w, dt_proj_w, dt_proj_b, A_log, D, out_proj_w)
        seq = seq[:, -H * W * R * R:, :]
        out = seq.reshape(B, H * R, W * R, D_MODEL).transpose(0, 3, 1, 2)
        return pixel_unshuffle(out, R)

    def _L0_ffn_ref(x, gate_w, w1, w2):
        import jax, jax.numpy as jnp
        import numpy as np
        NUM_EXPERTS = 8
        TOP_K = 2
        B, S, D = x.shape
        E = gate_w.shape[0]
        gate_logits = jnp.einsum('bsd,ed->bse', x, gate_w)
        top_vals, top_idx = jax.lax.top_k(gate_logits, TOP_K)
        top_w = jax.nn.softmax(top_vals, axis=-1)
        comb = jnp.sum(jax.nn.one_hot(top_idx, E, dtype=x.dtype) * top_w[..., None], axis=-2)
        xf = x.reshape(-1, D)
        comb_f = comb.reshape(-1, E)
        out = jnp.zeros_like(xf)
        for e in range(E):
            h = jax.nn.gelu(xf @ w1[e].T, approximate=False)
            out = out + comb_f[:, e:e + 1] * (h @ w2[e].T)
        return out.reshape(B, S, D)

    def _L1_conv_ref(x, global_token, in_proj_w, conv_w, conv_b, x_proj_w, dt_proj_w, dt_proj_b, A_log, D, out_proj_w):
        import jax, jax.numpy as jnp
        import numpy as np
        DIM = 256
        R = 2
        D_MODEL = DIM // (R * R)
        D_INNER = 2 * D_MODEL
        D_STATE = 16
        D_CONV = 4
        DT_RANK = (D_MODEL + 15) // 16
        NUM_TOKENS = 1

        def pixel_shuffle(x, r):
            B, C, H, W = x.shape
            c = C // (r * r)
            x = x.reshape(B, c, r, r, H, W)
            x = x.transpose(0, 1, 4, 2, 5, 3)
            return x.reshape(B, c, H * r, W * r)

        def pixel_unshuffle(x, r):
            B, C, Hr, Wr = x.shape
            H, W = (Hr // r, Wr // r)
            x = x.reshape(B, C, H, r, W, r)
            x = x.transpose(0, 1, 3, 5, 2, 4)
            return x.reshape(B, C * r * r, H, W)

        def mamba_block(seq, in_proj_w, conv_w, conv_b, x_proj_w, dt_proj_w, dt_proj_b, A_log, D, out_proj_w):
            B, L, _ = seq.shape
            xz = jnp.einsum('bld,ed->ble', seq, in_proj_w)
            u, z = jnp.split(xz, 2, axis=-1)
            up = jnp.pad(u, ((0, 0), (D_CONV - 1, 0), (0, 0)))
            u = sum((up[:, k:k + L, :] * conv_w[:, k] for k in range(D_CONV))) + conv_b
            u = jax.nn.silu(u)
            x_dbl = jnp.einsum('bld,ed->ble', u, x_proj_w)
            dt, Bm, Cm = jnp.split(x_dbl, [DT_RANK, DT_RANK + D_STATE], axis=-1)
            dt = jax.nn.softplus(jnp.einsum('blr,dr->bld', dt, dt_proj_w) + dt_proj_b)
            A = -jnp.exp(A_log)

            def step(h, inputs):
                dt_t, B_t, C_t, u_t = inputs
                dA = jnp.exp(dt_t[:, :, None] * A)
                h = dA * h + (dt_t * u_t)[:, :, None] * B_t[:, None, :]
                y = jnp.einsum('bdn,bn->bd', h, C_t)
                return (h, y)
            h0 = jnp.zeros((B, D_INNER, D_STATE), dtype=seq.dtype)
            xs = (dt.transpose(1, 0, 2), Bm.transpose(1, 0, 2), Cm.transpose(1, 0, 2), u.transpose(1, 0, 2))
            _, ys = jax.lax.scan(step, h0, xs)
            y = ys.transpose(1, 0, 2) + u * D
            y = y * jax.nn.silu(z)
            return jnp.einsum('bld,ed->ble', y, out_proj_w)
        B, C, H, W = x.shape
        xs = pixel_shuffle(x, R)
        seq = xs.reshape(B, D_MODEL, -1).transpose(0, 2, 1)
        tok = jnp.broadcast_to(global_token, (B, NUM_TOKENS, D_MODEL))
        seq = jnp.concatenate([tok, seq], axis=1)
        seq = mamba_block(seq, in_proj_w, conv_w, conv_b, x_proj_w, dt_proj_w, dt_proj_b, A_log, D, out_proj_w)
        seq = seq[:, -H * W * R * R:, :]
        out = seq.reshape(B, H * R, W * R, D_MODEL).transpose(0, 3, 1, 2)
        return pixel_unshuffle(out, R)

    def _L1_ffn_ref(hidden_states, gate_w, w13_weight, w2_weight):
        import jax, jax.numpy as jnp
        import numpy as np
        N_EXPERTS = 8
        N_GROUP = 4
        TOPK_GROUP = 2
        TOP_K = 2
        HIDDEN = 256
        INTER = 512
        B, S = (1, 256)

        def _grouped_topk(scores):
            T, E = scores.shape
            per_group = E // N_GROUP
            group_scores = scores.reshape(T, N_GROUP, per_group).max(-1)
            _, gidx = jax.lax.top_k(group_scores, TOPK_GROUP)
            gmask = jnp.zeros((T, N_GROUP), scores.dtype).at[jnp.arange(T)[:, None], gidx].set(1.0)
            smask = jnp.repeat(gmask, per_group, axis=1)
            masked = jnp.where(smask > 0, scores, 0.0)
            topk_w, topk_ids = jax.lax.top_k(masked, TOP_K)
            topk_w = topk_w / topk_w.sum(-1, keepdims=True)
            return (topk_ids, topk_w)
        Bm, Sm, H = hidden_states.shape
        x = hidden_states.reshape(-1, H)
        T = x.shape[0]
        scores = jax.nn.softmax(x @ gate_w.T, axis=-1)
        topk_ids, topk_w = _grouped_topk(scores)
        combine = jnp.zeros((T, N_EXPERTS), x.dtype).at[jnp.arange(T)[:, None], topk_ids].add(topk_w)
        gu = jnp.einsum('th,eih->tei', x, w13_weight)
        gate, up = (gu[..., :INTER], gu[..., INTER:])
        act = jax.nn.silu(gate) * up
        act = act * combine[:, :, None]
        out = jnp.einsum('tei,ehi->th', act, w2_weight)
        return out.reshape(Bm, Sm, H)

    def _gn(v, G=32, eps=1e-05):
        B_, C_, H_, W_ = v.shape
        g = v.reshape(B_, G, C_ // G, H_, W_)
        m = jnp.mean(g, axis=(2, 3, 4), keepdims=True)
        s = jnp.var(g, axis=(2, 3, 4), keepdims=True)
        return ((g - m) / jnp.sqrt(s + eps)).reshape(v.shape)

    def _ln_c(v, eps=1e-06):
        m = jnp.mean(v, axis=1, keepdims=True)
        s = jnp.var(v, axis=1, keepdims=True)
        return (v - m) / jnp.sqrt(s + eps)

    def _ln_t(v, eps=1e-05):
        m = jnp.mean(v, axis=-1, keepdims=True)
        s = jnp.var(v, axis=-1, keepdims=True)
        return (v - m) / jnp.sqrt(s + eps)

    def _to_tokens(v):
        B_, C_, H_, W_ = v.shape
        return v.reshape(B_, C_, H_ * W_).transpose(0, 2, 1)

    def _from_tokens(t, like):
        B_, C_, H_, W_ = like.shape
        return t.transpose(0, 2, 1).reshape(B_, C_, H_, W_)
    x = x + _L0_conv_ref(_ln_c(x), L0_conv_global_token, L0_conv_in_proj_w, L0_conv_conv_w, L0_conv_conv_b, L0_conv_x_proj_w, L0_conv_dt_proj_w, L0_conv_dt_proj_b, L0_conv_A_log, L0_conv_D, L0_conv_out_proj_w)
    t = _to_tokens(x)
    t = t + _L0_ffn_ref(_ln_t(t), L0_ffn_gate_w, L0_ffn_w1, L0_ffn_w2)
    x = _from_tokens(t, x)
    x = x + _L1_conv_ref(_ln_c(x), L1_conv_global_token, L1_conv_in_proj_w, L1_conv_conv_w, L1_conv_conv_b, L1_conv_x_proj_w, L1_conv_dt_proj_w, L1_conv_dt_proj_b, L1_conv_A_log, L1_conv_D, L1_conv_out_proj_w)
    t = _to_tokens(x)
    t = t + _L1_ffn_ref(_ln_t(t), L1_ffn_gate_w, L1_ffn_w13_weight, L1_ffn_w2_weight)
    x = _from_tokens(t, x)
    return x

_drawn_inputs = setup_inputs


def setup_inputs(seed=0):
    import zlib

    import numpy as np

    out = dict(_drawn_inputs(seed))
    spreads = {'L0_conv_global_token': (0.0, 2.0),
     'L0_conv_conv_b': (0.0, 0.8),
     'L0_conv_D': (1.0, 0.6),
     'L1_conv_global_token': (0.0, 2.0),
     'L1_conv_conv_b': (0.0, 0.8),
     'L1_conv_D': (1.0, 0.6)}
    factors = {'L0_conv_in_proj_w': 8.0,
     'L0_conv_conv_w': 8.0,
     'L0_conv_x_proj_w': 8.0,
     'L0_conv_dt_proj_w': 8.0,
     'L0_conv_dt_proj_b': 8.0,
     'L0_conv_A_log': 8.0,
     'L0_conv_out_proj_w': 8.0,
     'L1_conv_in_proj_w': 8.0,
     'L1_conv_conv_w': 8.0,
     'L1_conv_x_proj_w': 8.0,
     'L1_conv_dt_proj_w': 8.0,
     'L1_conv_dt_proj_b': 8.0,
     'L1_conv_A_log': 8.0,
     'L1_conv_out_proj_w': 8.0,
     'L1_ffn_gate_w': 3.843,
     'L1_ffn_w13_weight': 3.32,
     'L1_ffn_w2_weight': 3.323}
    for name, (base, spread) in spreads.items():
        noise = np.random.default_rng([zlib.crc32(name.encode()), seed]).standard_normal(out[name].shape)
        drawn = base * np.exp(spread * noise) if base else spread * noise
        out[name] = jnp.asarray(drawn.astype(out[name].dtype))
    for name, factor in factors.items():
        out[name] = (out[name] * factor).astype(out[name].dtype)
    return out
```

```python
from contextlib import ExitStack, contextmanager

import concourse.bass as bass
from concourse import mybir

F32 = mybir.dt.float32
BF16 = mybir.dt.bfloat16
U32 = mybir.dt.uint32
ALU = mybir.AluOpType
ACT = mybir.ActivationFunctionType
AX = mybir.AxisListType.X

P = 128
BATCH, SIDE = 4, 24
PIX = SIDE * SIDE
TOK = BATCH * PIX
ROWS = 4
PT = ROWS * SIDE
T = 4 * PT
NT = TOK // PT
TPB = PIX // PT
N = 16
TAPS = 4
E = 8
NDBU, NCREP, NHC = 4, 4, 8
BC = 96

PACK = {}
_at = 0
for _name, _w in (("in", 512), ("bc", BC), ("out", 256), ("conv_w", 4), ("conv_b", 1), ("dt_b", 1), ("D", 1),
                  ("A", N), ("tok", 1), ("xdt", 128), ("dtw", 128)):
    PACK[_name] = (_at, _at + _w)
    _at += _w
PACKW = _at


@contextmanager
def semaphores(nc):
    made = []

    def new(name):
        made.append(nc.alloc_semaphore(name))
        return made[-1]

    yield new
    nc.clear_and_free_semaphores(made)
    nc.all_engine_barrier()


def wait(eng, sem, count):
    if isinstance(count, int) and count <= 0:
        return
    eng.wait_ge(sem, count)


def tile_pairs(eng, body):
    body(0)
    with eng.Fori(1, NT // 2 - 1) as p:
        body(p)
    body(NT // 2 - 1)


def layer_norm(nc, m, L, eps):
    X, Xn, ps, ones = m["X"], m["Xn"], m["ps"], m["ones_c"]
    W, NB = 384, TOK // 384
    with ExitStack() as ctx:
        new = ctx.enter_context(semaphores(nc))
        sem = {k: new(f"{L}_{k}") for k in
               ("mean", "cent", "sq", "var", "ln", "rstd", "norm")}
        sq = ctx.enter_context(nc.sbuf_tensor(f"{L}_sq", [P, 2, 2, W], F32))
        rs = ctx.enter_context(nc.sbuf_tensor(f"{L}_rs", [P, 2, 2, W], F32))
        block = ctx.enter_context(nc.Block())

        @block.tensor
        def _(pe):
            for q in range(NB + 1):
                if q < NB:
                    wait(pe, sem["cent"], q - 1)
                    for i in range(2):
                        mm = nc.tensor.matmul(ps[:, q % 2, 0:W], ones[:], X[:, i, q * W:(q + 1) * W],
                                              start=(i == 0), stop=(i == 1))
                    mm.then_inc(sem["mean"], 1)
                if q > 0:
                    b = q - 1
                    pe.wait_ge(sem["sq"], b + 1)
                    wait(pe, sem["ln"], b - 1)
                    for i in range(2):
                        mm = nc.tensor.matmul(ps[:, 2 + b % 2, 0:W], ones[:], sq[:, b % 2, i, :],
                                              start=(i == 0), stop=(i == 1))
                    mm.then_inc(sem["var"], 1)

        @block.vector
        def _(dve):
            for q in range(NB + 1):
                if q < NB:
                    dve.wait_ge(sem["mean"], q + 1)
                    nc.vector.tensor_tensor(Xn[:, :, q * W:(q + 1) * W], X[:, :, q * W:(q + 1) * W],
                                            ps[:, q % 2, 0:W].unsqueeze(1).to_broadcast([P, 2, W]),
                                            ALU.subtract).then_inc(sem["cent"], 1)
                if q > 0:
                    b = q - 1
                    dve.wait_ge(sem["rstd"], b + 1)
                    nc.vector.tensor_tensor(Xn[:, :, b * W:(b + 1) * W], Xn[:, :, b * W:(b + 1) * W],
                                            rs[:, b % 2, 0, :].unsqueeze(1).to_broadcast([P, 2, W]),
                                            ALU.mult).then_inc(sem["norm"], 1)

        @block.scalar
        def _(act):
            for q in range(NB):
                act.wait_ge(sem["cent"], q + 1)
                wait(act, sem["var"], q - 1)
                nc.scalar.activation(sq[:, q % 2, :, :], Xn[:, :, q * W:(q + 1) * W], ACT.Square
                                     ).then_inc(sem["sq"], 1)
                act.wait_ge(sem["var"], q + 1)
                wait(act, sem["norm"], q - 1)
                nc.scalar.activation(rs[:, q % 2, 1, :], ps[:, 2 + q % 2, 0:W], ACT.Ln, bias=eps
                                     ).then_inc(sem["ln"], 1)
                act.wait_ge(sem["ln"], q + 1)
                nc.scalar.activation(rs[:, q % 2, 0, :], rs[:, q % 2, 1, :], ACT.Exp, scale=-0.5
                                     ).then_inc(sem["rstd"], 1)


def softplus_steps(nc, act, pool, sem, s, one, ps, bias, u, dt, w, k):
    def a0():
        nc.scalar.activation(s["a"], ps, ACT.Abs, bias=bias).then_inc(sem["abs"], 1)

    def a1():
        nc.scalar.activation(s["r"], ps, ACT.Relu, bias=bias).then_inc(sem["relu"], 1)

    def a2():
        act.wait_ge(sem["abs"], k + 1)
        nc.scalar.activation(s["e"], s["a"], ACT.Exp, scale=-1.0).then_inc(sem["e"], 1)

    def a3():
        act.wait_ge(sem["f"], k + 1)
        nc.scalar.activation(s["l"], s["f"], ACT.Ln).then_inc(sem["l"], 1)

    def p0():
        pool.wait_ge(sem["e"], k + 1)
        nc.gpsimd.tensor_tensor(s["f"], s["e"], one, ALU.add).then_inc(sem["f"], 1)
        pool.wait_ge(sem["f"], k + 1)
        nc.gpsimd.tensor_tensor(s["g"], s["f"], one, ALU.subtract).then_inc(sem["g"], 1)

    def p1():
        pool.wait_ge(sem["g"], 4 * k + 1)
        nc.gpsimd.tensor_tensor(s["g"], s["e"], s["g"], ALU.subtract).then_inc(sem["g"], 1)
        pool.wait_ge(sem["relu"], k + 1)
        pool.wait_ge(sem["g"], 4 * k + 2)
        nc.gpsimd.tensor_tensor(s["g"], s["g"], s["r"], ALU.add).then_inc(sem["g"], 1)

    def p2():
        pool.wait_ge(sem["l"], k + 1)
        pool.wait_ge(sem["g"], 4 * k + 3)
        nc.gpsimd.tensor_tensor(dt, s["g"], s["l"], ALU.add).then_inc(sem["g"], 1)
        pool.wait_ge(sem["g"], 4 * k + 4)
        nc.gpsimd.tensor_tensor(w, dt, u, ALU.mult).then_inc(sem["w"], 1)

    return (a0, a1, a2, a3), (p0, p1, p2)


def mamba(nc, m, L, wp):
    X, Xn, ps, ident = m["X"], m["Xn"], m["ps"], m["ident"]

    def par(name, rows=P):
        a, b = PACK[name]
        return wp[0:rows, a:b]

    w_in = par("in").rearrange("p (g d) -> p g d", g=4)
    w_out = par("out").rearrange("p (j c) -> p j c", j=2)

    with ExitStack() as ctx:
        new = ctx.enter_context(semaphores(nc))
        def sb(name, shape, dt=F32):
            return ctx.enter_context(nc.sbuf_tensor(f"{L}_{name}", shape, dt))

        NAMES = ("u_in z_in upre hist conv u zs xp abs relu e f l g w hi r1 mid parts b c dbu da scan carry "
                 "crep hc y yz out res const cred").split()
        sem = {k: new(f"{L}_{k}") for k in NAMES}
        tsem = {k: new(f"{L}_tok_{k}") for k in
                ("abs", "relu", "e", "f", "l", "g", "w")}
        s_tok = new(f"{L}_tok")
        s_diag = new(f"{L}_diag")
        s_negA = new(f"{L}_negA")

        diag = sb("diag", [P, TAPS + 1, P])
        negA = sb("negA", [P, 2, N])
        w_dt = sb("w_dt", [P, P])
        hist = sb("hist", [P, 2, TAPS - 1])
        carry = sb("carry", [P, 2, N])
        tok = sb("tok", [P, 16])
        ubc = sb("ubc", [P, P])
        upre = sb("upre", [P, TAPS - 1 + T])
        u = sb("u", [P, 2, T])
        zs = sb("zs", [P, T])
        sp = {k: sb("sp_" + k, [P, T]) for k in "arefgl"}
        dt = sb("dt", [P, 2, T])
        w = sb("w", [P, 2, T])
        hi = sb("hi", [P, T], BF16)
        mid = sb("mid", [P, T], BF16)
        r1 = sb("r1", [P, T])
        parts = sb("parts", [P, 2, T], BF16)
        dbu = sb("dbu", [P, NDBU, T])
        h = sb("h", [P, N, T])
        crep = sb("crep", [P, NCREP, T])
        hc = sb("hc", [P, NHC, T])
        yz = sb("yz", [P, T])

        one_t = m["ones"][:, 0:1].to_broadcast([P, T])

        def bank(k, w=T):
            return ps[:, k, 0:w]

        def b_ps(n):
            return bank(n % 2)

        c_ps, y_ps, ua_ps, zb_ps = bank(2), bank(5), bank(6), bank(7)

        def da_ps(n):
            return bank(3 + n % 2)

        seq = [v.rearrange("p (h i w j) -> p h i w j", i=2, w=SIDE, j=2) for v in (upre[:, TAPS - 1:], zs[:], yz[:])]

        def quarters(v):
            return v.rearrange("p (j h w) -> p j h w", j=2, w=SIDE)

        block = ctx.enter_context(nc.Block())

        @block.tensor
        def _(pe):
            def project_in(out, g, t, sem_out):
                for i in range(2):
                    for j in range(2):
                        mm = nc.tensor.matmul(out[:, (2 * i + j) * PT:(2 * i + j + 1) * PT], w_in[:, g + j, :],
                                              Xn[:, i, bass.ds(t * PT, PT)], start=True, stop=True)
                mm.then_inc(sem_out, 1)

            def u_in(t):
                wait(pe, sem["relu"], t)
                wait(pe, sem["abs"], t)
                project_in(ua_ps, 0, t, sem["u_in"])

            def z_in(t):
                wait(pe, sem["res"], t - 1)
                wait(pe, sem["r1"], t + 1)
                project_in(zb_ps, 2, t, sem["z_in"])

            def conv(t, taps):
                pe.wait_ge(sem["upre"], 2 * t + 2)
                for k in taps:
                    mm = nc.tensor.matmul(ua_ps, diag[:, k, :], upre[:, k:k + T], start=(k == 0), stop=(k == TAPS - 1))
                if TAPS - 1 in taps:
                    mm.then_inc(sem["conv"], 1)

            def project_x(t, r):
                pe.wait_ge(sem["u"], t + 1)
                wait(pe, sem["zs"], 2 * t)
                nc.tensor.matmul(zb_ps[0:BC, :], par("bc"), u[:, r, :], start=True, stop=True).then_inc(sem["xp"], 1)
                nc.tensor.matmul(ua_ps, w_dt[:], u[:, r, :], start=True, stop=True).then_inc(sem["xp"], 1)

            def spread_b(t, r, n):
                g = t * N + n
                wait(pe, sem["dbu"], g - 1)
                if n == 0:
                    pe.wait_ge(sem["parts"], t + 1)
                nc.tensor.matmul(b_ps(n), m["sel"][:, n, :], parts[0:BC, r, :], start=True, stop=True
                                 ).then_inc(sem["b"], 1)

            def spread_c(t, r, n):
                wait(pe, sem["crep"], t * N + n)
                nc.tensor.matmul(c_ps, m["sel"][:, N + n, :], parts[0:BC, r, :], start=True, stop=True
                                 ).then_inc(sem["c"], 1)

            def skip(t, r):
                wait(pe, sem["yz"], t)
                nc.tensor.matmul(y_ps, diag[:, TAPS, :], u[:, r, :], start=True, stop=False)

            def sum_y(t, n):
                pe.wait_ge(sem["hc"], t * N + n + 1)
                nc.tensor.matmul(y_ps, ident[:], hc[:, n % NHC, :], start=False, stop=(n == N - 1)
                                 ).then_inc(sem["y"], 1)

            def project_out(t):
                pe.wait_ge(sem["yz"], t + 1)
                for i in range(2):
                    for j in range(2):
                        mm = nc.tensor.matmul(zb_ps[:, i * PT:(i + 1) * PT], w_out[:, j, :], seq[2][:, :, i, :, j],
                                              start=(j == 0), stop=(j == 1))
                mm.then_inc(sem["out"], 1)

            pe.wait_ge(s_diag, TAPS + 2)
            nc.tensor.matmul(bank(0, P), par("xdt", 4), par("dtw", 4), start=True, stop=True).then_inc(s_tok, 1)
            nc.tensor.matmul(bank(1, 1), w_in[:, 0, :], par("tok"), start=True, stop=True).then_inc(s_tok, 1)
            pe.wait_ge(s_tok, 6)
            nc.tensor.matmul(bank(3, 1), w_dt[:], tok[:, 0:1], start=True, stop=True).then_inc(s_tok, 1)
            nc.tensor.matmul(bank(4, N), ubc[:], par("bc")[:, 0:N], start=True, stop=True).then_inc(s_tok, 1)
            u_in(0)
            conv(0, range(TAPS))
            project_x(0, 0)
            pe.wait_ge(s_tok, 9)
            spread_b(0, 0, 0)
            spread_b(0, 0, 1)
            spread_c(0, 0, 0)

            def tile(t, r, last):
                first = isinstance(t, int) and t == 0
                for n in range(N):
                    if n + 2 < N:
                        spread_b(t, r, n + 2)
                    elif not last:
                        spread_b(t + 1, 1 - r, n + 2 - N)
                    if n + 1 < N:
                        spread_c(t, r, n + 1)
                    elif not last:
                        spread_c(t + 1, 1 - r, 0)
                    if n == 0:
                        if not first:
                            sum_y(t - 1, N - 1)
                        if not last:
                            u_in(t + 1)
                    if n == 1:
                        z_in(t)
                    if n == 2 and not last:
                        conv(t + 1, (0, 1))
                    if n == 3 and not last:
                        conv(t + 1, (2, 3))
                    if n == 4:
                        skip(t, r)
                        sum_y(t, 0)
                    if 5 <= n < 8:
                        sum_y(t, 2 * n - 9)
                        sum_y(t, 2 * n - 8)
                    if n >= 8:
                        sum_y(t, n - 1)
                    if n == 6 and not last:
                        project_x(t + 1, 1 - r)
                    if n == 10 and not first:
                        if not last:
                            pe.wait_ge(sem["r1"], t + 2)
                        wait(pe, sem["zs"], 2 * t + 2)
                        project_out(t - 1)

            def pair(p):
                tile(2 * p, 0, False)
                tile(2 * p + 1, 1, isinstance(p, int) and p == NT // 2 - 1)

            tile_pairs(pe, pair)
            sum_y(NT - 1, N - 1)
            pe.wait_ge(sem["res"], NT - 1)
            project_out(NT - 1)

        @block.scalar
        def _(act):
            def steps(t, r):
                return softplus_steps(nc, act, None, sem, {k: v[:] for k, v in sp.items()}, one_t, ua_ps, par("dt_b"),
                                      None, None, None, t)[0]

            def u_out(t, slot):
                act.wait_ge(sem["u_in"], t + 1)
                wait(act, sem["conv"], t)
                wait(act, sem["hist"], t)
                nc.scalar.copy(upre[:, 0:TAPS - 1], hist[:, slot, :]).then_inc(sem["const"], 1)
                for i in range(2):
                    nc.scalar.copy(seq[0][:, :, i, :, :].rearrange("p h w j -> p j h w"),
                                   quarters(ua_ps[:, i * 2 * PT:(i + 1) * 2 * PT])).then_inc(sem["upre"], 1)
                act.wait_ge(sem["upre"], 2 * t + 2)
                act.wait_ge(sem["const"], t + 1)
                nc.scalar.copy(hist[:, 1, :], upre[:, T:T + TAPS - 1]).then_inc(sem["hist"], 1)

            def silu_z(t):
                act.wait_ge(sem["z_in"], t + 1)
                wait(act, sem["yz"], t)
                for i in range(2):
                    nc.scalar.activation(seq[1][:, :, i, :, :].rearrange("p h w j -> p j h w"),
                                         quarters(zb_ps[:, i * 2 * PT:(i + 1) * 2 * PT]), ACT.Silu
                                         ).then_inc(sem["zs"], 1)

            def silu_u(t, r):
                act.wait_ge(sem["conv"], t + 1)
                wait(act, sem["y"], (t - 2) * N + 1)
                nc.scalar.activation(u[:, r, :], ua_ps, ACT.Silu, bias=par("conv_b")).then_inc(sem["u"], 1)

            def dt_head(t, r):
                act.wait_ge(sem["xp"], 2 * t + 2)
                wait(act, sem["w"], t)
                steps(t, r)[0]()
                steps(t, r)[1]()

            def b_high(t):
                act.wait_ge(sem["xp"], 2 * t + 1)
                wait(act, sem["r1"], t)
                nc.scalar.copy(hi[0:BC, :], zb_ps[0:BC, :]).then_inc(sem["hi"], 1)

            def b_mid(t):
                act.wait_ge(sem["r1"], t + 1)
                wait(act, sem["parts"], t)
                nc.scalar.copy(mid[0:BC, :], r1[0:BC, :]).then_inc(sem["mid"], 1)

            def decay(t, r, n):
                g = t * N + n
                if n == 0:
                    act.wait_ge(sem["w"], t + 1)
                wait(act, sem["scan"], g - 1)
                nc.scalar.activation(da_ps(n), dt[:, r, :], ACT.Exp, scale=negA[:, 0, n:n + 1]
                                     ).then_inc(sem["da"], 1)

            def copy_c(t, n):
                g = t * N + n
                act.wait_ge(sem["c"], g + 1)
                wait(act, sem["hc"], g + 1 - NCREP)
                nc.scalar.copy(crep[:, n % NCREP, :], c_ps).then_inc(sem["crep"], 1)

            nc.scalar.activation(negA[:, 1, :], par("A"), ACT.Exp).then_inc(s_negA, 1)
            act.wait_ge(s_negA, 1)
            nc.scalar.mul(negA[:, 0, :], negA[:, 1, :], -1.0).then_inc(s_negA, 1)
            act.wait_ge(s_tok, 2)
            nc.scalar.copy(w_dt[:], bank(0, P)).then_inc(s_tok, 1)
            act.wait_ge(s_diag, TAPS + 2)
            nc.scalar.copy(hist[:, 0, TAPS - 2:TAPS - 1], bank(1, 1)).then_inc(s_tok, 1)
            nc.scalar.activation(tok[:, 0:1], bank(1, 1), ACT.Silu, bias=par("conv_b"),
                                 scale=par("conv_w")[:, TAPS - 1:TAPS]).then_inc(s_tok, 1)
            act.wait_ge(s_tok, 8)
            tsteps = softplus_steps(nc, act, None, tsem, {k: tok[:, 2 + q:3 + q] for q, k in enumerate("arefgl")}, m["ones"][:, 0:1],
                                    bank(3, 1), par("dt_b"), None, None, None, 0)[0]
            for step in tsteps:
                step()
            act.wait_ge(s_negA, 2)
            u_out(0, 0)
            silu_u(0, 0)
            b_high(0)
            dt_head(0, 0)
            steps(0, 0)[2]()
            b_mid(0)
            steps(0, 0)[3]()

            def tile(t, r, slot, last):
                for n in range(N):
                    decay(t, r, n)
                    copy_c(t, n)
                    if n == 1 and not last:
                        u_out(t + 1, slot)
                    if n == 4:
                        silu_z(t)
                        if not last:
                            silu_u(t + 1, 1 - r)
                    if not last:
                        if n == 7:
                            b_high(t + 1)
                            dt_head(t + 1, 1 - r)
                        if n == 8:
                            steps(t + 1, r)[2]()
                        if n == 9:
                            b_mid(t + 1)
                        if n == 10:
                            steps(t + 1, r)[3]()

            def pair(p):
                tile(2 * p, 0, 1, False)
                tile(2 * p + 1, 1, ((p + 1) % (TPB // 2) + 1) // 2, isinstance(p, int) and p == NT // 2 - 1)

            tile_pairs(act, pair)

        @block.vector
        def _(dve):
            def split_one(t):
                dve.wait_ge(sem["hi"], t + 1)
                wait(dve, sem["parts"], t)
                nc.vector.scalar_tensor_tensor(out=r1[0:BC, :], in0=hi[0:BC, :], scalar=m["mask"][0:BC, 0:1],
                                               in1=zb_ps[0:BC, :], op0=ALU.mult, op1=ALU.add
                                               ).then_inc(sem["r1"], 1)

            def split_two(t, r):
                dve.wait_ge(sem["mid"], t + 1)
                wait(dve, sem["c"], (t - 1) * N)
                nc.vector.scalar_tensor_tensor(out=parts[0:BC, r, :], in0=mid[0:BC, :], scalar=m["mask"][0:BC, 1:2],
                                               in1=r1[0:BC, :], op0=ALU.mult, op1=ALU.add
                                               ).then_inc(sem["parts"], 1)

            def times_b(t, r, n):
                g = t * N + n
                dve.wait_ge(sem["b"], g + 1)
                if n == 0:
                    dve.wait_ge(sem["w"], t + 1)
                wait(dve, sem["scan"], g - NDBU + 1)
                nc.vector.tensor_tensor(dbu[:, n % NDBU, :], w[:, r, :], b_ps(n), ALU.mult).then_inc(sem["dbu"], 1)

            def scan(t, n, slot):
                g = t * N + n
                dve.wait_ge(sem["da"], g + 1)
                dve.wait_ge(sem["dbu"], g + 1)
                wait(dve, sem["hc"], g - N + 1)
                first = h[:, n, T - 1:T] if slot is None else carry[:, slot, n:n + 1] if isinstance(slot, int) \
                    else carry[:, bass.ds(slot, 1), n:n + 1].rearrange("p a n -> p (a n)")
                nc.vector.tensor_tensor_scan(h[:, n, :], da_ps(n), dbu[:, n % NDBU, :], first, ALU.mult, ALU.add
                                             ).then_inc(sem["scan"], 1)

            def gate(t):
                dve.wait_ge(sem["y"], t * N + N)
                dve.wait_ge(sem["zs"], 2 * t + 2)
                wait(dve, sem["out"], t)
                nc.vector.tensor_tensor(yz[:], zs[:], y_ps, ALU.mult).then_inc(sem["yz"], 1)

            def residual(t):
                dve.wait_ge(sem["out"], t + 1)
                x = X[:, :, bass.ds(t * PT, PT)]
                nc.vector.tensor_tensor(x, x, zb_ps[:, 0:2 * PT].rearrange("p (i t) -> p i t", i=2), ALU.add
                                        ).then_inc(sem["res"], 1)

            for k in range(TAPS):
                nc.vector.tensor_scalar(diag[:, k, :], ident[:], par("conv_w")[:, k:k + 1], None, ALU.mult
                                        ).then_inc(s_diag, 1)
            nc.vector.tensor_scalar(diag[:, TAPS, :], ident[:], par("D"), None, ALU.mult).then_inc(s_diag, 1)
            nc.vector.memset(hist[:, 0, :], 0.0).then_inc(s_diag, 1)
            dve.wait_ge(s_tok, 5)
            nc.vector.tensor_scalar(ubc[:], m["ones"][:], tok[:, 0:1], None, ALU.mult).then_inc(s_tok, 1)
            dve.wait_ge(s_tok, 8)
            dve.wait_ge(tsem["w"], 1)
            nc.vector.tensor_scalar(carry[:, 0, :], bank(4, N), tok[:, 9:10], None, ALU.mult).then_inc(s_tok, 1)
            dve.wait_ge(s_tok, 9)
            split_one(0)
            split_two(0, 0)
            times_b(0, 0, 0)

            def tile(t, r, slot, last):
                for n in range(N):
                    if n + 1 < N:
                        times_b(t, r, n + 1)
                    elif not last:
                        times_b(t + 1, 1 - r, 0)
                    scan(t, n, slot)
                    if n == 2 and not (isinstance(t, int) and t == 0):
                        gate(t - 1)
                    if n == 8 and not last:
                        split_one(t + 1)
                    if n == 10 and not last:
                        split_two(t + 1, 1 - r)
                    if n == 12 and not (isinstance(t, int) and t == 0):
                        residual(t - 1)

            def pair(p):
                tile(2 * p, 0, (p % (TPB // 2) + 1) // 2, False)
                last = isinstance(p, int) and p == NT // 2 - 1
                tile(2 * p + 1, 1, None, last)
                if not last:
                    dve.wait_ge(sem["scan"], (2 * p + 2) * N)
                    nc.vector.tensor_copy(carry[:, 1, :], h[:, :, T - 1]).then_inc(sem["carry"], 1)
                    dve.wait_ge(sem["carry"], p + 1)

            tile_pairs(dve, pair)
            gate(NT - 1)
            residual(NT - 1)

        @block.gpsimd
        def _(pool):
            def steps(t, r):
                return softplus_steps(nc, None, pool, sem, {k: v[:] for k, v in sp.items()}, one_t, None, None,
                                      u[:, r, :], dt[:, r, :], w[:, r, :], t)[1]

            def times_c(t, n):
                g = t * N + n
                pool.wait_ge(sem["scan"], g + 1)
                pool.wait_ge(sem["crep"], g + 1)
                wait(pool, sem["y"], g - NHC + 1)
                nc.gpsimd.tensor_tensor(hc[:, n % NHC, :], h[:, n, :], crep[:, n % NCREP, :], ALU.mult
                                        ).then_inc(sem["hc"], 1)

            tsteps = softplus_steps(nc, None, pool, tsem, {k: tok[:, 2 + q:3 + q] for q, k in enumerate("arefgl")}, m["ones"][:, 0:1],
                                    None, None, tok[:, 0:1], tok[:, 8:9], tok[:, 9:10], 0)[1]
            for step in tsteps:
                step()
            for step in steps(0, 0):
                step()

            def tile(t, r, last):
                for n in range(N):
                    times_c(t, n)
                    if not last:
                        if n == 8:
                            steps(t + 1, 1 - r)[0]()
                        if n == 9:
                            steps(t + 1, 1 - r)[1]()
                        if n == 11:
                            wait(pool, sem["da"], t * N)
                            wait(pool, sem["dbu"], t * N)
                            steps(t + 1, 1 - r)[2]()

            def pair(p):
                tile(2 * p, 0, False)
                tile(2 * p + 1, 1, isinstance(p, int) and p == NT // 2 - 1)

            tile_pairs(pool, pair)


TS = 256
KT = (2 * TOK + E * (TS - 1)) // TS
NQ = TOK // P
D = 256
HALVES = TS // P


class Chain:

    def __init__(self, eng, sem):
        self.eng, self.sem, self.n = eng, sem, 0

    def __call__(self, ins):
        self.n += 1
        ins.then_inc(self.sem, 1)
        self.eng.wait_ge(self.sem, self.n)


def route(nc, m, L, gate, grouped):
    Xn, ps, iota = m["Xn"], m["ps"], m["iota"]
    with ExitStack() as ctx:
        new = ctx.enter_context(semaphores(nc))
        def sb(name, shape, dt=F32):
            return ctx.enter_context(nc.sbuf_tensor(f"{L}_{name}", shape, dt))

        sem = {k: new(f"{L}_{k}") for k in
               "logit turned rows_a rows_d expo ask_e marks rank chain slots".split()}
        s_sent = [new(f"{L}_sent{k}") for k in range(2)]
        rows = sb("rows", [P, NQ, D])
        lg, mx, ixf, ma, mb, sc, mp, tmp = (sb(k, [P, NQ, E]) for k in ("lg", "mx", "ixf", "ma", "mb", "sc", "mp", "tmp"))
        ix = sb("ix", [P, NQ, E], U32)
        g8 = sb("g8", [P, NQ, E])
        one = sb("one", [P, 4, NQ])
        cnt = sb("cnt", [P, 4, E])
        steps = sb("steps", [P, 16])
        big = sb("big", [P, KT * E])
        tef = sb("tef", [P, KT])
        ones_row = m["ones"][:, 0:NQ]
        block = ctx.enter_context(nc.Block())

        def per_token(v):
            return v.unsqueeze(2).to_broadcast([P, NQ, E])

        def per_expert(v):
            return v.unsqueeze(1).to_broadcast([P, NQ, E])

        flat = "p q e -> p (q e)"

        @block.tensor
        def _(pe):
            for q in range(NQ):
                for i in range(2):
                    mm = nc.tensor.matmul(ps[:, 0, q * E:(q + 1) * E], Xn[:, i, q * P:(q + 1) * P],
                                          gate[:, i * E:(i + 1) * E], start=(i == 0), stop=(i == 1))
            mm.then_inc(sem["logit"], 1)
            for q in range(NQ):
                b = 1 + q % 4
                wait(pe, sem["rows_d"] if q % 2 else sem["rows_a"], (q - 4) // 2 + 1 if q >= 4 else 0)
                for i in range(2):
                    mm = nc.tensor.transpose(ps[:, b, i * P:(i + 1) * P], Xn[:, i, q * P:(q + 1) * P], m["ident"][:])
                mm.then_inc(sem["turned"], 1)
            pe.wait_ge(sem["marks"], 1)
            nc.tensor.matmul(ps[:, 5, 0:NQ * E], m["tri"][:], ma[:].rearrange(flat), start=True, stop=False)
            nc.tensor.matmul(ps[:, 5, 0:NQ * E], m["ones"][:], mp[:].rearrange(flat), start=False, stop=True)
            nc.tensor.matmul(ps[:, 6, 0:E], m["ones"][:], cnt[:, 3, :], start=True, stop=True).then_inc(sem["rank"], 1)

        @block.scalar
        def _(act):
            for q in range(0, NQ, 2):
                act.wait_ge(sem["turned"], q + 1)
                nc.scalar.copy(rows[:, q, :], ps[:, 1 + q % 4, 0:D]).then_inc(sem["rows_a"], 1)
            act.wait_ge(sem["ask_e"], 1)
            if grouped:
                nc.scalar.activation(sc[:], sc[:], ACT.Exp).then_inc(sem["expo"], 1)
            else:
                nc.scalar.activation(one[:, 1, :], one[:, 0, :], ACT.Exp).then_inc(sem["expo"], 1)

        @block.vector
        def _(dve):
            link = Chain(dve, sem["chain"])
            for q in range(1, NQ, 2):
                dve.wait_ge(sem["turned"], q + 1)
                nc.vector.tensor_copy(rows[:, q, :], ps[:, 1 + q % 4, 0:D]).then_inc(sem["rows_d"], 1)
            dve.wait_ge(sem["logit"], 1)
            link(nc.vector.tensor_copy(lg[:].rearrange(flat), ps[:, 0, 0:NQ * E]))

            def top(values):
                for q in range(NQ):
                    ins = nc.vector.max(mx[:, q, :], values[:, q, :])
                link(ins)
                for q in range(NQ):
                    ins = nc.vector.max_index(ix[:, q, :], mx[:, q, :], values[:, q, :])
                link(ins)
                link(nc.vector.tensor_copy(ixf[:], ix[:]))

            if not grouped:
                top(lg)
                nc.vector.tensor_tensor(one[:, 0, :], mx[:, :, 1], mx[:, :, 0], ALU.subtract).then_inc(sem["ask_e"], 1)
                dve.wait_ge(sem["expo"], 1)
                link(nc.vector.tensor_scalar(one[:, 2, :], one[:, 1, :], 1.0, None, ALU.add))
                link(nc.vector.reciprocal(m["p01"][:, 0, :], one[:, 2, :]))
                link(nc.vector.tensor_tensor(m["p01"][:, 1, :], one[:, 1, :], m["p01"][:, 0, :], ALU.mult))
            else:
                link(nc.vector.tensor_reduce(one[:, 0, :], lg[:], AX, ALU.max))
                nc.vector.tensor_tensor(sc[:], lg[:], per_token(one[:, 0, :]), ALU.subtract).then_inc(sem["ask_e"], 1)
                dve.wait_ge(sem["expo"], 1)
                link(nc.vector.tensor_reduce(one[:, 1, :], sc[:], AX, ALU.add))
                link(nc.vector.reciprocal(one[:, 2, :], one[:, 1, :]))
                link(nc.vector.tensor_tensor(sc[:], sc[:], per_token(one[:, 2, :]), ALU.mult))
                link(nc.vector.memset(g8[:], -1.0))
                link(nc.vector.tensor_reduce(g8[:, :, 0:4], sc[:].rearrange("p q (g s) -> p q g s", s=2), AX, ALU.max))
                top(g8)
                g4 = iota[:, 0:4].unsqueeze(1).to_broadcast([P, NQ, 4])
                for s, dst in ((0, ma), (1, mb)):
                    link(nc.vector.tensor_tensor(dst[:, :, 0:4], g4, ixf[:, :, s].unsqueeze(2).to_broadcast([P, NQ, 4]),
                                                 ALU.is_equal))
                link(nc.vector.tensor_tensor(tmp[:, :, 0:4], ma[:, :, 0:4], mb[:, :, 0:4], ALU.add))
                for s in range(2):
                    ins = nc.vector.tensor_tensor(lg[:].rearrange("p q (g s) -> p q g s", s=2)[:, :, :, s],
                                                  sc[:].rearrange("p q (g s) -> p q g s", s=2)[:, :, :, s],
                                                  tmp[:, :, 0:4], ALU.mult)
                link(ins)
                top(lg)
                link(nc.vector.tensor_tensor(one[:, 0, :], mx[:, :, 0], mx[:, :, 1], ALU.add))
                link(nc.vector.reciprocal(one[:, 1, :], one[:, 0, :]))
                for s in range(2):
                    ins = nc.vector.tensor_tensor(m["p01"][:, s, :], mx[:, :, s], one[:, 1, :], ALU.mult)
                link(ins)

            link(nc.vector.tensor_tensor(lg[:], per_expert(iota[:, 0:E]), per_token(ixf[:, :, 0]), ALU.is_equal))
            link(nc.vector.tensor_tensor(mb[:], per_expert(iota[:, 0:E]), per_token(ixf[:, :, 1]), ALU.is_equal))
            link(nc.vector.tensor_tensor(ma[:], lg[:], mb[:], ALU.add))
            for e in range(E):
                ins = nc.vector.tensor_tensor_scan(tmp[:, :, e], ones_row, ma[:, :, e], 0.0, ALU.mult, ALU.add)
            link(ins)
            link(nc.vector.tensor_copy(cnt[:, 3, :], tmp[:, NQ - 1, :]))
            nc.vector.tensor_tensor(mp[:], tmp[:], ma[:], ALU.subtract).then_inc(sem["marks"], 1)
            dve.wait_ge(sem["rank"], 1)
            K = TOK // TS
            link(nc.vector.tensor_copy(cnt[:, 0, :], ps[:, 6, 0:E]))
            link(nc.vector.tensor_scalar(steps[:, 0:K], iota[:, 0:K], float(TS), None, ALU.mult))
            link(nc.vector.tensor_tensor(big[:, 0:E * K].rearrange("p (e k) -> p e k", e=E),
                                         cnt[:, 0, :].unsqueeze(2).to_broadcast([P, E, K]),
                                         steps[:, 0:K].unsqueeze(1).to_broadcast([P, E, K]), ALU.is_gt))
            link(nc.vector.tensor_reduce(cnt[:, 1, :], big[:, 0:E * K].rearrange("p (e k) -> p e k", e=E), AX, ALU.add))
            link(nc.vector.tensor_tensor_scan(cnt[:, 2, :], m["ones"][:, 0:E], cnt[:, 1, :], 0.0, ALU.mult, ALU.add))
            link(nc.vector.tensor_tensor(cnt[:, 3, :], cnt[:, 2, :], cnt[:, 1, :], ALU.subtract))
            link(nc.vector.tensor_scalar(cnt[:, 3, :], cnt[:, 3, :], float(TS), None, ALU.mult))
            link(nc.vector.tensor_tensor(big[:].rearrange("p (k e) -> p k e", e=E),
                                         cnt[:, 2, :].unsqueeze(1).to_broadcast([P, KT, E]),
                                         iota[:, 0:KT].unsqueeze(2).to_broadcast([P, KT, E]), ALU.is_le))
            link(nc.vector.tensor_reduce(tef[:], big[:].rearrange("p (k e) -> p k e", e=E), AX, ALU.add))
            link(nc.vector.tensor_scalar(tef[:], tef[:], float(E - 1), None, ALU.min))
            link(nc.vector.tensor_copy(m["tile_e"][:], tef[:]))
            link(nc.vector.tensor_tensor(sc[:], ps[:, 5, 0:NQ * E].rearrange("p (q e) -> p q e", e=E),
                                         per_expert(cnt[:, 3, :]), ALU.add))
            for s, mark in ((0, lg), (1, mb)):
                link(nc.vector.tensor_tensor(tmp[:], mark[:], sc[:], ALU.mult))
                link(nc.vector.tensor_reduce(one[:, 2 + s, :], tmp[:], AX, ALU.add))
                link(nc.vector.tensor_copy(m["slots"][:, s, :], one[:, 2 + s, :]))
            nc.vector.engine_nop().then_inc(sem["slots"], 1)

        @block.gpsimd
        def _(pool):
            pool.wait_ge(sem["slots"], 1)
            pool.wait_ge(sem["rows_a"], NQ // 2)
            pool.wait_ge(sem["rows_d"], NQ // 2)
            for q in range(NQ):
                for s in range(2):
                    nc.gpsimd.indirect_dma_start(
                        out=m["xs"], out_offset=bass.IndirectOffsetOnAxis(ap=m["slots"][:, s, q:q + 1], axis=0),
                        in_=rows[:, q, :], in_offset=None).then_inc(s_sent[s], 16)
            for s in range(2):
                pool.wait_ge(s_sent[s], 16 * NQ)


def experts(nc, m, L, w1, w2, F, gated):
    ps, ident = m["ps"], m["ident"]
    FB = F // P
    HB = FB // 2 if gated else FB
    with ExitStack() as ctx:
        new = ctx.enter_context(semaphores(nc))
        def sb(name, shape, dt=F32):
            return ctx.enter_context(nc.sbuf_tensor(f"{L}_{name}", shape, dt))

        def sems(name, n=2):
            return [new(f"{L}_{name}{k}") for k in range(n)]

        s_x, s_w1, s_w2, s_y = sems("x"), sems("w1"), sems("w2"), sems("y")
        sem = {k: new(f"{L}_{k}") for k in
               "turned xt hid act up out yev".split()}
        w1_t = sb("w1", [P, 2, 2, F])
        w2_t = sb("w2", [P, 2, HB, D])
        xr = sb("xr", [P, 2, HALVES, D])
        xT = sb("xT", [P, 2, 2, TS])
        hT = sb("hT", [P, 2, HB, TS])
        gl = sb("gl", [P, 2, HB, TS]) if gated else None
        yt = sb("yt", [P, 2, HALVES, D])
        xs_v = m["xs"].rearrange("(k h p) d -> k p h d", h=HALVES, p=P)
        ys_v = m["ys"].rearrange("(k h p) d -> k p h d", h=HALVES, p=P)
        block = ctx.enter_context(nc.Block())
        NBK = FB // 2
        SBK = NBK // 2 if gated else NBK

        def loop(eng, body):
            body(0, 0)
            body(1, 1)
            with eng.Fori(1, (KT - 1) // 2) as p:
                body(2 * p, 0)
                body(2 * p + 1, 1)
            for k in range(2 * ((KT - 1) // 2), KT):
                body(k, k % 2)

        def times(k, r):
            return k // 2 + 1 if isinstance(k, int) else (k - r) // 2 + 1

        @block.sync
        def _(sp):
            def load(k, r):
                wait(sp, sem["turned"], k - 1)
                sp.dma_start(xr[:, r, :, :], xs_v[bass.ds(k, 1)].rearrange("k p h d -> p (k h) d")
                             if not isinstance(k, int) else xs_v[k]).then_inc(s_x[r], 16)
                e = nc.sync.value_load(m["tile_e"][0:1, bass.ds(k, 1)], min_val=0, max_val=E - 1)
                wait(sp, sem["hid"], (k - 1) * NBK)
                sp.dma_start(w1_t[:, r, :, :].rearrange("p i f -> p (i f)"),
                             w1[bass.ds(e, 1)].rearrange("e p f -> (e p) f")).then_inc(s_w1[r], 16)
                wait(sp, sem["out"], k - 1)
                sp.dma_start(w2_t[:, r, :, :].rearrange("p b d -> p (b d)"),
                             w2[bass.ds(e, 1)].rearrange("e p f -> (e p) f")).then_inc(s_w2[r], 16)

            def store(k, r):
                sp.wait_ge(sem["yev"], k + 1)
                sp.dma_start(ys_v[bass.ds(k, 1)].rearrange("k p h d -> p (k h) d")
                             if not isinstance(k, int) else ys_v[k], yt[:, r, :, :]).then_inc(s_y[r], 16)

            load(0, 0)
            load(1, 1)
            with sp.Fori(0, (KT - 3) // 2) as p:
                for r in range(2):
                    store(2 * p + r, r)
                    load(2 * p + r + 2, r)
            for k in range(2 * ((KT - 3) // 2), KT):
                store(k, k % 2)
                if k + 2 < KT:
                    load(k + 2, k % 2)
            for r in range(2):
                sp.wait_ge(s_y[r], 16 * ((KT - r + 1) // 2))

        @block.tensor
        def _(pe):
            def turn(k, r):
                pe.wait_ge(s_x[r], 16 * times(k, r))
                wait(pe, sem["xt"], k)
                for h in range(HALVES):
                    for i in range(2):
                        mm = nc.tensor.transpose(ps[:, 6, i * TS + h * P:i * TS + (h + 1) * P],
                                                 xr[:, r, h, i * P:(i + 1) * P], ident[:])
                mm.then_inc(sem["turned"], 1)

            def body(k, r):
                pe.wait_ge(sem["xt"], k + 1)
                pe.wait_ge(s_w1[r], 16 * times(k, r))
                for b in range(NBK):
                    wait(pe, sem["act" if b < SBK else "up"], (k - 1) * SBK + b % SBK + 1)
                    for f in (2 * b, 2 * b + 1):
                        for i in range(2):
                            mm = nc.tensor.matmul(ps[:, b, (f % 2) * TS:(f % 2 + 1) * TS],
                                                  w1_t[:, r, i, f * P:(f + 1) * P], xT[:, r, i, :],
                                                  start=(i == 0), stop=(i == 1))
                    mm.then_inc(sem["hid"], 1)
                if not (isinstance(k, int) and k == KT - 1):
                    turn(k + 1, 1 - r)
                pe.wait_ge(s_w2[r], 16 * times(k, r))
                wait(pe, sem["yev"], k)
                pe.wait_ge(sem["up" if gated else "act"], (k + 1) * SBK)
                for h in range(HALVES):
                    for f in range(HB):
                        mm = nc.tensor.matmul(ps[:, 7, h * D:(h + 1) * D], hT[:, r, f, h * P:(h + 1) * P],
                                              w2_t[:, r, f, :], start=(f == 0), stop=(f == HB - 1))
                mm.then_inc(sem["out"], 1)

            turn(0, 0)
            loop(pe, body)

        @block.scalar
        def _(act):
            def body(k, r):
                wait(act, sem["out"], k - 1)
                for b in range(NBK):
                    act.wait_ge(sem["hid"], k * NBK + b + 1)
                    src = ps[:, b, 0:2 * TS]
                    if not gated:
                        nc.scalar.activation(hT[:, r, 2 * b:2 * b + 2, :].rearrange("p b t -> p (b t)"), src, ACT.Gelu
                                             ).then_inc(sem["act"], 1)
                    elif b < NBK // 2:
                        nc.scalar.activation(gl[:, r, 2 * b:2 * b + 2, :].rearrange("p b t -> p (b t)"), src, ACT.Silu
                                             ).then_inc(sem["act"], 1)

            loop(act, body)

        @block.vector
        def _(dve):
            def move_x(k, r):
                dve.wait_ge(sem["turned"], k + 1)
                wait(dve, sem["hid"], (k - 1) * NBK)
                nc.vector.tensor_copy(xT[:, r, :, :].rearrange("p i t -> p (i t)"), ps[:, 6, 0:2 * TS]
                                      ).then_inc(sem["xt"], 1)

            def body(k, r):
                if gated:
                    for b in range(NBK // 2, NBK):
                        dve.wait_ge(sem["hid"], k * NBK + b + 1)
                        dve.wait_ge(sem["act"], k * SBK + b - SBK + 1)
                        if b == NBK // 2:
                            wait(dve, sem["out"], k - 1)
                        c = 2 * b - HB
                        nc.vector.tensor_tensor(hT[:, r, c:c + 2, :].rearrange("p b t -> p (b t)"),
                                                gl[:, r, c:c + 2, :].rearrange("p b t -> p (b t)"),
                                                ps[:, b, 0:2 * TS], ALU.mult).then_inc(sem["up"], 1)
                if not (isinstance(k, int) and k == KT - 1):
                    move_x(k + 1, 1 - r)
                dve.wait_ge(sem["out"], k + 1)
                if not (isinstance(k, int) and k < 2):
                    dve.wait_ge(s_y[r], 16 * (times(k, r) - 1))
                nc.vector.tensor_copy(yt[:, r, :, :].rearrange("p h d -> p (h d)"), ps[:, 7, 0:HALVES * D]
                                      ).then_inc(sem["yev"], 1)

            move_x(0, 0)
            loop(dve, body)


def combine(nc, m, L):
    X, ps = m["X"], m["ps"]
    NB = 4
    with ExitStack() as ctx:
        new = ctx.enter_context(semaphores(nc))
        got = ctx.enter_context(nc.sbuf_tensor(f"{L}_got", [P, NB, 2, D], F32))
        mix = ctx.enter_context(nc.sbuf_tensor(f"{L}_mix", [P, NB, 2, D], F32))
        s_got = [new(f"{L}_got{k}") for k in range(NB)]
        sem = {k: new(f"{L}_{k}") for k in "scaled mixed turned added".split()}
        block = ctx.enter_context(nc.Block())

        @block.gpsimd
        def _(pool):
            for q in range(NQ):
                wait(pool, sem["mixed"], q - NB + 1)
                for s in range(2):
                    nc.gpsimd.indirect_dma_start(
                        out=got[:, q % NB, s, :], out_offset=None, in_=m["ys"],
                        in_offset=bass.IndirectOffsetOnAxis(ap=m["slots"][:, s, q:q + 1], axis=0)
                        ).then_inc(s_got[q % NB], 16)

        @block.scalar
        def _(act):
            for q in range(NQ):
                act.wait_ge(s_got[q % NB], 32 * (q // NB + 1))
                wait(act, sem["mixed"], q - NB + 1)
                nc.scalar.activation(mix[:, q % NB, 0, :], got[:, q % NB, 0, :], ACT.Copy,
                                     scale=m["p01"][:, 0, q:q + 1]).then_inc(sem["scaled"], 1)

        @block.vector
        def _(dve):
            for q in range(NQ + 1):
                if q < NQ:
                    dve.wait_ge(sem["scaled"], q + 1)
                    wait(dve, sem["turned"], q - NB + 1)
                    nc.vector.scalar_tensor_tensor(out=mix[:, q % NB, 1, :], in0=got[:, q % NB, 1, :],
                                                   scalar=m["p01"][:, 1, q:q + 1], in1=mix[:, q % NB, 0, :],
                                                   op0=ALU.mult, op1=ALU.add).then_inc(sem["mixed"], 1)
                if q > 0:
                    b = q - 1
                    dve.wait_ge(sem["turned"], b + 1)
                    x = X[:, :, b * P:(b + 1) * P]
                    nc.vector.tensor_tensor(x, x, ps[:, b % 4, 0:D].rearrange("p (i t) -> p i t", i=2), ALU.add
                                            ).then_inc(sem["added"], 1)

        @block.tensor
        def _(pe):
            for q in range(NQ):
                pe.wait_ge(sem["mixed"], q + 1)
                wait(pe, sem["added"], q - 3)
                for i in range(2):
                    mm = nc.tensor.transpose(ps[:, q % 4, i * P:(i + 1) * P], mix[:, q % NB, 1, i * P:(i + 1) * P],
                                             m["ident"][:])
                mm.then_inc(sem["turned"], 1)


def program(nc, inputs, out):
    with ExitStack() as ctx:
        def sb(name, shape, dt=F32):
            return ctx.enter_context(nc.sbuf_tensor(name, shape, dt))

        m = {
            "ps": ctx.enter_context(nc.psum_tensor("ps", [P, 8, 512], F32)),
            "X": sb("X", [P, 2, TOK]),
            "Xn": sb("Xn", [P, 2, TOK]),
            "ident": sb("ident", [P, P]),
            "ones": sb("ones", [P, P]),
            "ones_c": sb("ones_c", [P, P]),
            "sel": sb("sel", [BC, 2 * N, P], BF16),
            "mask": sb("mask", [P, 2]),
            "tri": sb("tri", [P, P]),
            "iota": sb("iota", [P, 64]),
            "slots": sb("slots", [P, 2, NQ], U32),
            "p01": sb("p01", [P, 2, NQ]),
            "tile_e": sb("tile_e", [P, KT], mybir.dt.int32),
            "xs": nc.dram_tensor("slot_rows", (KT * TS, D), F32, kind="Internal").ap(),
            "ys": nc.dram_tensor("slot_results", (KT * TS, D), F32, kind="Internal").ap(),
        }
        wp = sb("wp", [P, 2, PACKW])
        zero = sb("zero", [P, 2048])
        gates = sb("gates", [P, 2, 2 * E])
        s_load = [ctx.enter_context(nc.semaphore(f"load{k}")) for k in range(10)]
        s_zero = ctx.enter_context(nc.semaphore("zeroed"))
        s_one = ctx.enter_context(nc.semaphore("one"))
        s_out = ctx.enter_context(nc.semaphore("stored"))

        with nc.sbuf_tensor("sel_f", [BC, 2 * N, P], F32) as sel_f, nc.Block() as block:
            @block.sync
            def _(eng):
                loads = [(m["X"][:], inputs["x"]), (m["ident"][:], inputs["ident"]), (sel_f[:], inputs["sel"]),
                         (m["mask"][:], inputs["mask"]), (wp[:, 0, :], inputs["pack0"]), (wp[:, 1, :], inputs["pack1"]),
                         (m["tri"][:], inputs["tri"]), (m["iota"][:], inputs["iota"]), (gates[:, 0, :], inputs["gate0"]),
                         (gates[:, 1, :], inputs["gate1"])]
                for s, (dst, src) in zip(s_load, loads):
                    eng.dma_start(dst, src).then_inc(s, 16)
                eng.wait_ge(s_one, 3)
                rows = 2048 // D * P
                for a in range(0, KT * TS, rows):
                    b = min(a + rows, KT * TS)
                    eng.dma_start(m["xs"][a:b, :].rearrange("(p r) d -> p (r d)", p=P), zero[:, 0:(b - a) // P * D]
                                  ).then_inc(s_zero, 16)
                for s in s_load:
                    eng.wait_ge(s, 16)
                eng.wait_ge(s_zero, 16 * -(-KT * TS // rows))

            @block.vector
            def _(eng):
                nc.vector.memset(zero[:], 0.0).then_inc(s_one, 1)
                nc.vector.memset(m["ones"][:], 1.0).then_inc(s_one, 1)
                nc.vector.memset(m["ones_c"][:], 1.0 / 256).then_inc(s_one, 1)
                eng.wait_ge(s_load[2], 16)
                nc.vector.tensor_copy(m["sel"][:], sel_f[:]).then_inc(s_one, 1)

        for layer in range(LAYERS):
            layer_norm(nc, m, f"L{layer}c", 1e-6)
            mamba(nc, m, f"L{layer}", wp[:, layer, :])
            if STAGES <= 2 * layer + 1:
                break
            layer_norm(nc, m, f"L{layer}t", 1e-5)
            route(nc, m, f"L{layer}r", gates[:, layer, :], layer == 1)
            experts(nc, m, f"L{layer}e", inputs[f"up{layer}"], inputs[f"down{layer}"], 1024, layer == 1)
            combine(nc, m, f"L{layer}s")
            if STAGES <= 2 * layer + 2:
                break

        with nc.Block() as block:
            @block.sync
            def _(eng):
                eng.dma_start(out, m["X"][:]).then_inc(s_out, 16)
                eng.wait_ge(s_out, 16)


LAYERS = 2
STAGES = 4


def pack(np, g, j2):
    a = np.zeros((P, PACKW), np.float32)

    def put(name, v, r0=0, c0=0):
        a[r0:r0 + v.shape[0], PACK[name][0] + c0:PACK[name][0] + c0 + v.shape[1]] = v

    in_t = g("in_proj_w").T
    for j in range(2):
        put("in", in_t[:, :P], 64 * j, P * j)
        put("in", in_t[:, P:], 64 * j, 2 * P + P * j)
        put("out", g("out_proj_w").T, 0, P * j + 64 * j)
    put("tok", g("global_token").reshape(64, 1))
    put("bc", np.tile(g("x_proj_w")[4:].T, (1, 3)))
    put("xdt", g("x_proj_w")[:4])
    put("dtw", g("dt_proj_w").T)
    put("conv_w", g("conv_w"))
    put("conv_b", g("conv_b").reshape(P, 1))
    put("dt_b", g("dt_proj_b").reshape(P, 1))
    put("D", g("D").reshape(P, 1))
    put("A", g("A_log"))
    return a


def host_arrays(np, inputs):
    x = np.asarray(inputs["x"]).reshape(BATCH, 64, 2, 2, PIX)
    arrays = {"x": np.ascontiguousarray(x.transpose(3, 1, 2, 0, 4)).reshape(P, 2, TOK)}
    for l in range(2):
        arrays[f"pack{l}"] = pack(np, lambda k: np.asarray(inputs[f"L{l}_conv_{k}"]), 2)
    arrays["ident"] = np.eye(P, dtype=np.float32)
    sel = np.zeros((BC, 2 * N, P), np.float32)
    for r in range(BC):
        sel[r, r % 32, :] = 1
    arrays["sel"] = sel
    mask = np.zeros((P, 2), np.float32)
    mask[32:, 0] = -1
    mask[64:, 1] = -1
    arrays["mask"] = mask
    arrays["tri"] = np.triu(np.ones((P, P), np.float32), 1)
    arrays["iota"] = np.tile(np.arange(64, dtype=np.float32), (P, 1))

    def chans_first(w):
        w = w.reshape(w.shape[:-1] + (64, 2, 2))
        n = w.ndim
        return np.ascontiguousarray(w.transpose(tuple(range(n - 4)) + (n - 1, n - 3, n - 2, n - 4)))

    for l, (up, down) in enumerate((("w1", "w2"), ("w13_weight", "w2_weight"))):
        arrays[f"gate{l}"] = chans_first(np.asarray(inputs[f"L{l}_ffn_gate_w"])).reshape(P, 2 * E)
        arrays[f"up{l}"] = chans_first(np.asarray(inputs[f"L{l}_ffn_{up}"])).reshape(E, P, -1)
        w2 = np.asarray(inputs[f"L{l}_ffn_{down}"])
        w2 = w2.reshape(E, 64, 2, 2, -1, P).transpose(0, 5, 4, 2, 3, 1)
        arrays[f"down{l}"] = np.ascontiguousarray(w2).reshape(E, P, -1)
    return arrays


def kernel(**inputs):
    import numpy as np
    import concourse.bacc as bacc
    from concourse.bass_utils import run_bass_kernel_spmd

    nc = bacc.Bacc("TRN2", target_bir_lowering=False, num_devices=1)
    arrays = host_arrays(np, inputs)
    aps = {k: nc.dram_tensor(f"in_{k}", a.shape, mybir.dt.from_np(a.dtype), kind="ExternalInput").ap()
           for k, a in arrays.items()}
    out = nc.dram_tensor("out", (P, 2, TOK), F32, kind="ExternalOutput").ap()
    program(nc, aps, out)
    r = run_bass_kernel_spmd(nc, [{f"in_{k}": a for k, a in arrays.items()}], core_ids=[0])
    y = r.results[0]["out"].reshape(2, 64, 2, BATCH, PIX)
    return np.ascontiguousarray(y.transpose(3, 1, 2, 0, 4)).reshape(BATCH, 256, SIDE, SIDE)
```

```python
from contextlib import ExitStack, contextmanager

import concourse.bass as bass
from concourse import mybir

F32 = mybir.dt.float32
BF16 = mybir.dt.bfloat16
U32 = mybir.dt.uint32
ALU = mybir.AluOpType
ACT = mybir.ActivationFunctionType
AX = mybir.AxisListType.X

P = 128
BATCH, SIDE = 4, 24
PIX = SIDE * SIDE
TOK = BATCH * PIX
ROWS = 4
PT = ROWS * SIDE
T = 4 * PT
NT = TOK // PT
TPB = PIX // PT
N = 16
TAPS = 4
E = 8
NDA, NDBU, NHC = 8, 4, 8
NBP = 4
LEAD, LAG = 3, 3
A0, A1 = 4, 11
D_GATE, D_SPLIT, D_RES = 4, 2, 7
P0, P1 = 6, 9
CN = 4
PAD = 2
IMG = PAD + 2 * PIX
EXP_LN, LN, SILU = "natural_log_exp_and_others", "natural_log", "silu_and_others"
BC = 96

PACK = {}
_at = 0
for _name, _w in (("in_u", 5 * P), ("taps", 5 * P), ("in_z", 2 * P), ("bc", BC), ("out", 2 * P), ("conv_b", 1), ("dt_b", 1), ("D", 1),
                  ("A", N), ("tok", 1), ("xdt", 128), ("dtw", 128)):
    PACK[_name] = (_at, _at + _w)
    _at += _w
PACKW = _at


@contextmanager
def semaphores(nc):
    made = []

    def new(name):
        made.append(nc.alloc_semaphore(name))
        return made[-1]

    yield new
    nc.clear_and_free_semaphores(made)
    nc.all_engine_barrier()


def wait(eng, sem, count):
    if isinstance(count, int) and count <= 0:
        return
    eng.wait_ge(sem, count)


def tile_pairs(eng, body):
    body(0)
    with eng.Fori(1, NT // 2 - 1) as p:
        body(p)
    body(NT // 2 - 1)


def layer_norm(nc, m, L, eps, tok=None):
    X, ps, ones = m["X"], m["ps"], m["ones_c"]
    NB = 2 * BATCH
    W = TOK // NB
    seq = tok is not None

    def block_of(q):
        if seq:
            a = (q // 2) * IMG + PAD + (q % 2) * 2 * W
            return m["Xn"][:, a:a + 2 * W].rearrange("p (h i w) -> p i h w", i=2, w=SIDE)
        return m["Xn"][:, 0:2 * TOK].rearrange("p (i t) -> p i t", i=2)[:, :, q * W:(q + 1) * W].rearrange(
            "p i (h w) -> p i h w", w=SIDE)

    def rows(v):
        return v.rearrange("p (h w) -> p h w", w=SIDE)

    def both(v):
        return rows(v).unsqueeze(1).to_broadcast([P, 2, W // SIDE, SIDE])

    with ExitStack() as ctx:
        new = ctx.enter_context(semaphores(nc))
        sem = {k: new(f"{L}_{k}") for k in ("mean", "cent", "sq", "var", "ln", "rstd", "norm")}
        sq = ctx.enter_context(nc.sbuf_tensor(f"{L}_sq", [P, 2, 2, W], F32))
        rs = ctx.enter_context(nc.sbuf_tensor(f"{L}_rs", [P, 2, 2, W], F32))
        block = ctx.enter_context(nc.Block())

        @block.tensor
        def _(pe):
            for q in range(NB + 1):
                if q < NB:
                    wait(pe, sem["cent"], q - 1)
                    for i in range(2):
                        mm = nc.tensor.matmul(ps[:, q % 2, 0:W], ones[:], X[:, i, q * W:(q + 1) * W],
                                              start=(i == 0), stop=(i == 1))
                    mm.then_inc(sem["mean"], 1)
                if q > 0:
                    b = q - 1
                    pe.wait_ge(sem["sq"], 2 * b + 2)
                    wait(pe, sem["ln"], b - 1)
                    for i in range(2):
                        mm = nc.tensor.matmul(ps[:, 2 + b % 2, 0:W], ones[:], sq[:, b % 2, i, :],
                                              start=(i == 0), stop=(i == 1))
                    mm.then_inc(sem["var"], 1)

        @block.vector
        def _(dve):
            if seq:
                for b in range(BATCH):
                    nc.vector.memset(m["Xn"][:, b * IMG:b * IMG + 1], 0.0)
                    nc.vector.tensor_copy(m["Xn"][:, b * IMG + 1:b * IMG + PAD], tok)
            for q in range(NB + 1):
                if q < NB:
                    dve.wait_ge(sem["mean"], q + 1)
                    nc.vector.tensor_tensor(block_of(q), X[:, :, q * W:(q + 1) * W].rearrange(
                        "p i (h w) -> p i h w", w=SIDE), both(ps[:, q % 2, 0:W]), ALU.subtract
                        ).then_inc(sem["cent"], 1)
                if q > 0:
                    b = q - 1
                    dve.wait_ge(sem["rstd"], b + 1)
                    nc.vector.tensor_tensor(block_of(b), block_of(b), both(rs[:, b % 2, 0, :]), ALU.mult
                                            ).then_inc(sem["norm"], 1)

        @block.scalar
        def _(act):
            nc.scalar.preload_act_table_set(EXP_LN)
            for q in range(NB + 1):
                if q < NB:
                    act.wait_ge(sem["cent"], q + 1)
                    wait(act, sem["var"], q - 1)
                    for i in range(2):
                        nc.scalar.activation(rows(sq[:, q % 2, i, :]), block_of(q)[:, i], ACT.Square
                                             ).then_inc(sem["sq"], 1)
                if q > 0:
                    b = q - 1
                    act.wait_ge(sem["var"], b + 1)
                    wait(act, sem["norm"], b - 1)
                    nc.scalar.activation(rs[:, b % 2, 1, :], ps[:, 2 + b % 2, 0:W], ACT.Ln, bias=eps
                                         ).then_inc(sem["ln"], 1)
                    act.wait_ge(sem["ln"], b + 1)
                    nc.scalar.activation(rs[:, b % 2, 0, :], rs[:, b % 2, 1, :], ACT.Exp, scale=-0.5
                                         ).then_inc(sem["rstd"], 1)


def softplus_steps(nc, act, pool, sem, s, ps, bias, u, dt, w, k):
    def absolute():
        nc.scalar.activation(s["a"], ps, ACT.Abs, bias=bias).then_inc(sem["abs"], 1)

    def relu():
        nc.scalar.activation(s["r"], ps, ACT.Relu, bias=bias).then_inc(sem["relu"], 1)

    def decayed():
        act.wait_ge(sem["abs"], k + 1)
        nc.scalar.activation(s["e"], s["a"], ACT.Exp, scale=-1.0).then_inc(sem["e"], 1)

    def plus_one():
        act.wait_ge(sem["e"], k + 1)
        nc.scalar.activation(s["f"], s["e"], ACT.Identity, bias=1.0).then_inc(sem["f"], 1)

    def minus_one():
        act.wait_ge(sem["f"], k + 1)
        nc.scalar.activation(s["g"], s["f"], ACT.Identity, bias=-1.0).then_inc(sem["g"], 1)

    def log():
        nc.scalar.activation(s["l"], s["f"], ACT.Ln).then_inc(sem["l"], 1)

    def lost():
        pool.wait_ge(sem["g"], k + 1)
        nc.gpsimd.tensor_tensor(s["a"], s["e"], s["g"], ALU.subtract).then_inc(sem["sum"], 1)

    def add_log():
        pool.wait_ge(sem["l"], k + 1)
        pool.wait_ge(sem["sum"], 3 * k + 1)
        nc.gpsimd.tensor_tensor(s["e"], s["a"], s["l"], ALU.add).then_inc(sem["sum"], 1)

    def add_relu():
        pool.wait_ge(sem["relu"], k + 1)
        pool.wait_ge(sem["sum"], 3 * k + 2)
        nc.gpsimd.tensor_tensor(dt, s["e"], s["r"], ALU.add).then_inc(sem["sum"], 1)

    def times_u():
        pool.wait_ge(sem["sum"], 3 * k + 3)
        nc.gpsimd.tensor_tensor(w, dt, u, ALU.mult).then_inc(sem["w"], 1)

    return (absolute, relu, decayed, plus_one, minus_one, log), (lost, add_log, add_relu, times_u)


def mamba(nc, m, L, wp):
    X, Xn, ps, ident = m["X"], m["Xn"], m["ps"], m["ident"]

    def par(name, rows=P):
        a, b = PACK[name]
        return wp[0:rows, a:b]

    w_z = par("in_z").rearrange("p (j d) -> p j d", j=2)
    w_out = par("out").rearrange("p (j c) -> p j c", j=2)
    FOLDS = ((0, 1, 0), (1, 1, 1), (2, 0, 0), (3, 0, 1), (4, 0, 2))

    with ExitStack() as ctx:
        new = ctx.enter_context(semaphores(nc))

        def sb(name, shape, dt=F32):
            return ctx.enter_context(nc.sbuf_tensor(f"{L}_{name}", shape, dt))

        sem = {k: new(f"{L}_{k}") for k in
               "u_in z_in u zs xp abs relu e f g l sum w hi r1 mid parts b dbu da scan carry hc y yz out res".split()}
        tsem = {k: new(f"{L}_tok_{k}") for k in ("abs", "relu", "e", "f", "g", "l", "sum", "w")}
        s_tok, s_fold, s_negA = new(f"{L}_tok"), new(f"{L}_fold"), new(f"{L}_negA")
        s_cst = [new(f"{L}_c_stored{r}") for r in range(2)]
        s_cld = [[new(f"{L}_c_spread{r}{k}") for k in range(N // CN)] for r in range(2)]

        fold = sb("fold", [P, 5, P])
        diagD = sb("diagD", [P, P])
        negA = sb("negA", [P, 2, N])
        w_dt = sb("w_dt", [P, P])
        carry = sb("carry", [P, 2, N])
        tok = sb("tok", [P, 16])
        ubc = sb("ubc", [P, P])
        u = sb("u", [P, 2, T])
        zs = sb("zs", [P, 2, T])
        sp = {k: sb("sp_" + k, [P, T]) for k in "arefgl"}
        dt = sb("dt", [P, 2, T])
        w = sb("w", [P, 2, T])
        hi = sb("hi", [P, T], BF16)
        mid = sb("mid", [P, T], BF16)
        r1 = sb("r1", [P, T])
        parts = sb("parts", [P, 2, T], BF16)
        da = sb("da", [P, NDA, T])
        dbu = sb("dbu", [P, NDBU, T])
        h = sb("h", [P, N, T])
        crep = sb("crep", [P, 2, N, T])
        hc = sb("hc", [P, NHC, T])
        yz = sb("yz", [P, T])
        c_rows = m["c_rows"]

        def bank(k, w=T):
            return ps[:, k, 0:w]

        def b_ps(n):
            return bank((0, 1, 3, 4)[n % NBP])

        ua_ps, zb_ps = bank(6), bank(7)
        y_ps = (bank(2), bank(5))

        def js(v):
            return v.rearrange("p (s j) -> p j s", j=2)

        def column(t, img, back):
            return Xn[:, bass.ds(t * (T // 2) + img * PAD + (PAD - back), T // 2)]

        block = ctx.enter_context(nc.Block())

        @block.tensor
        def _(pe):
            def u_in(t, img, which):
                if 0 in which:
                    wait(pe, sem["relu"], t)
                for k in which:
                    g, j, back = FOLDS[k]
                    mm = nc.tensor.matmul(ua_ps[:, j * (T // 2):(j + 1) * (T // 2)], fold[:, g, :],
                                          column(t, img, back), start=(k in (0, 2)), stop=(k in (1, 4)))
                if 4 in which:
                    mm.then_inc(sem["u_in"], 1)

            def z_in(t, img):
                wait(pe, sem["res"], t - 1)
                if not (isinstance(t, int) and t == 0):
                    pe.wait_ge(sem["r1"], t + 1)
                for j in range(2):
                    mm = nc.tensor.matmul(zb_ps[:, j * (T // 2):(j + 1) * (T // 2)], w_z[:, j, :],
                                          column(t, img, 0), start=True, stop=True)
                mm.then_inc(sem["z_in"], 1)

            def project_bc(t, r):
                pe.wait_ge(sem["u"], t + 1)
                wait(pe, sem["zs"], max(t, 1) if isinstance(t, int) else t)
                nc.tensor.matmul(zb_ps[0:BC, :], par("bc"), u[:, r, :], start=True, stop=True).then_inc(sem["xp"], 1)

            def project_dt(t, r):
                pe.wait_ge(sem["u"], t + 1)
                nc.tensor.matmul(ua_ps, w_dt[:], u[:, r, :], start=True, stop=True).then_inc(sem["xp"], 1)

            def spread_b(t, r, n):
                g = t * N + n
                wait(pe, sem["dbu"], g - NBP + 1)
                if n == 0:
                    pe.wait_ge(sem["parts"], t + 1)
                nc.tensor.matmul(b_ps(n), m["sel"][:, n, :], parts[0:BC, r, :], start=True, stop=True
                                 ).then_inc(sem["b"], 1)

            def skip(t, r):
                wait(pe, sem["yz"], t - 1)
                nc.tensor.matmul(y_ps[r], diagD[:], u[:, r, :], start=True, stop=False)

            def sum_y(t, r, n):
                pe.wait_ge(sem["hc"], t * N + n + 1)
                nc.tensor.matmul(y_ps[r], ident[:], hc[:, n % NHC, :], start=False, stop=(n == N - 1)
                                 ).then_inc(sem["y"], 1)

            def project_out(t):
                pe.wait_ge(sem["yz"], t + 1)
                for j in range(2):
                    mm = nc.tensor.matmul(zb_ps[:, 0:T // 2], w_out[:, j, :], js(yz[:])[:, j, :],
                                          start=(j == 0), stop=(j == 1))
                mm.then_inc(sem["out"], 1)

            nc.tensor.matmul(bank(0, P), par("xdt", 4), par("dtw", 4), start=True, stop=True).then_inc(s_tok, 1)
            pe.wait_ge(s_fold, 2)
            nc.tensor.matmul(bank(1, 1), fold[:, 0, :], par("tok"), start=True, stop=True).then_inc(s_tok, 1)
            u_in(0, 0, range(5))
            z_in(0, 0)
            pe.wait_ge(s_tok, 5)
            nc.tensor.matmul(bank(4, 1), w_dt[:], tok[:, 0:1], start=True, stop=True).then_inc(s_tok, 1)
            nc.tensor.matmul(bank(5, N), ubc[:], par("bc")[:, 0:N], start=True, stop=True).then_inc(s_tok, 1)
            project_bc(0, 0)
            project_dt(0, 0)
            u_in(1, 0, range(5))
            for n in range(LEAD):
                spread_b(0, 0, n)
            pe.wait_ge(tsem["relu"], 1)

            def tile(t, r, img1, img2, more):
                first = isinstance(t, int) and t == 0
                for n in range(N):
                    if n + LEAD < N:
                        spread_b(t, r, n + LEAD)
                    elif more:
                        spread_b(t + 1, 1 - r, n + LEAD - N)
                    if n >= LAG:
                        if n == LAG:
                            skip(t, r)
                        sum_y(t, r, n - LAG)
                    elif not first:
                        sum_y(t - 1, 1 - r, N - LAG + n)
                    if more:
                        if n == 0:
                            project_bc(t + 1, 1 - r)
                        if n == 1:
                            project_dt(t + 1, 1 - r)
                    if more == 2 and 4 <= n <= 6:
                        u_in(t + 2, img2, ((0, 1), (2, 3), (4,))[n - 4])
                    if n == 6 and not first:
                        if more:
                            pe.wait_ge(sem["r1"], t + 2)
                        project_out(t - 1)
                    if n == 8 and more:
                        z_in(t + 1, img1)

            def pair(p):
                last = isinstance(p, int) and p == NT // 2 - 1
                tile(2 * p, 0, p // (TPB // 2), (p + 1) // (TPB // 2), 1 if last else 2)
                tile(2 * p + 1, 1, (p + 1) // (TPB // 2), (p + 1) // (TPB // 2), 0 if last else 2)

            tile_pairs(pe, pair)
            for n in range(N - LAG, N):
                sum_y(NT - 1, 1, n)
            pe.wait_ge(sem["res"], NT - 1)
            project_out(NT - 1)

        @block.scalar
        def _(act):
            def steps(t, r):
                return softplus_steps(nc, act, None, sem, {k: v[:] for k, v in sp.items()}, ua_ps, par("dt_b"),
                                      None, None, None, t)[0]

            def silu_u(t, r):
                act.wait_ge(sem["u_in"], t + 1)
                wait(act, sem["y"], (t - 2) * N + 1)
                nc.scalar.activation(js(u[:, r, :]), ua_ps.rearrange("p (j s) -> p j s", j=2), ACT.Silu,
                                     bias=par("conv_b")).then_inc(sem["u"], 1)

            def silu_z(t, r):
                act.wait_ge(sem["z_in"], t + 1)
                wait(act, sem["yz"], t - 1)
                nc.scalar.activation(js(zs[:, r, :]), zb_ps.rearrange("p (j s) -> p j s", j=2), ACT.Silu
                                     ).then_inc(sem["zs"], 1)

            def b_high(t):
                act.wait_ge(sem["xp"], 2 * t + 1)
                wait(act, sem["r1"], t)
                nc.scalar.copy(hi[0:BC, :], zb_ps[0:BC, :]).then_inc(sem["hi"], 1)

            def b_mid(t):
                act.wait_ge(sem["r1"], t + 1)
                wait(act, sem["parts"], t)
                nc.scalar.copy(mid[0:BC, :], r1[0:BC, :]).then_inc(sem["mid"], 1)

            def dt_head(t, r):
                act.wait_ge(sem["xp"], 2 * t + 2)
                wait(act, sem["w"], t)
                steps(t, r)[0]()
                steps(t, r)[1]()

            def decay(t, r, n):
                g = t * N + n
                if n == 0:
                    act.wait_ge(sem["sum"], 3 * t + 3)
                wait(act, sem["scan"], g - NDA + 1)
                nc.scalar.activation(da[:, n % NDA, :], dt[:, r, :], ACT.Exp, scale=negA[:, 0, n:n + 1]
                                     ).then_inc(sem["da"], 1)

            nc.scalar.preload_act_table_set(EXP_LN)
            nc.scalar.activation(negA[:, 1, :], par("A"), ACT.Exp).then_inc(s_negA, 1)
            act.wait_ge(s_negA, 1)
            nc.scalar.mul(negA[:, 0, :], negA[:, 1, :], -1.0).then_inc(s_negA, 1)
            act.wait_ge(s_tok, 2)
            nc.scalar.copy(w_dt[:], bank(0, P)).then_inc(s_tok, 1)
            nc.scalar.preload_act_table_set(SILU)
            nc.scalar.activation(tok[:, 0:1], bank(1, 1), ACT.Silu, bias=par("conv_b")).then_inc(s_tok, 1)
            silu_u(0, 0)
            silu_z(0, 0)
            nc.scalar.preload_act_table_set(EXP_LN)
            b_high(0)
            dt_head(0, 0)
            for step in steps(0, 0)[2:5]:
                step()
            b_mid(0)
            act.wait_ge(s_tok, 7)
            of_tok = softplus_steps(nc, act, None, tsem, {k: tok[:, 2 + q:3 + q] for q, k in enumerate("arefgl")},
                                    bank(4, 1), par("dt_b"), None, None, None, 0)[0]
            for step in of_tok[0:5]:
                step()
            nc.scalar.preload_act_table_set(LN)
            steps(0, 0)[5]()
            of_tok[5]()
            nc.scalar.preload_act_table_set(SILU)
            silu_u(1, 1)
            nc.scalar.preload_act_table_set(EXP_LN)
            act.wait_ge(s_negA, 2)

            def tile(t, r, more):
                for n in range(N):
                    decay(t, r, n)
                    if not more:
                        continue
                    if n == A0:
                        b_high(t + 1)
                    if n == A0 + 1:
                        dt_head(t + 1, 1 - r)
                        steps(t + 1, r)[2]()
                    if n == A0 + 2:
                        b_mid(t + 1)
                        steps(t + 1, r)[3]()
                    if n == A0 + 3:
                        steps(t + 1, r)[4]()
                    if n == A1:
                        nc.scalar.preload_act_table_set(LN)
                        steps(t + 1, r)[5]()
                        nc.scalar.preload_act_table_set(SILU)
                        if more == 2:
                            silu_u(t + 2, r)
                        silu_z(t + 1, 1 - r)
                        nc.scalar.preload_act_table_set(EXP_LN)

            def pair(p):
                last = isinstance(p, int) and p == NT // 2 - 1
                tile(2 * p, 0, 1 if last else 2)
                tile(2 * p + 1, 1, 0 if last else 2)

            tile_pairs(act, pair)

        @block.vector
        def _(dve):
            def split_one(t, r, before):
                wait(dve, s_cst[1 - r], 16 * before)
                dve.wait_ge(sem["hi"], t + 1)
                wait(dve, sem["parts"], t)
                nc.vector.scalar_tensor_tensor(out=r1[0:BC, :], in0=hi[0:BC, :], scalar=m["mask"][0:BC, 0:1],
                                               in1=zb_ps[0:BC, :], op0=ALU.mult, op1=ALU.add
                                               ).then_inc(sem["r1"], 1)

            def split_two(t, r):
                dve.wait_ge(sem["mid"], t + 1)
                wait(dve, sem["b"], (t - 1) * N)
                nc.vector.scalar_tensor_tensor(out=parts[0:BC, r, :], in0=mid[0:BC, :], scalar=m["mask"][0:BC, 1:2],
                                               in1=r1[0:BC, :], op0=ALU.mult, op1=ALU.add
                                               ).then_inc(sem["parts"], 1)

            def times_b(t, r, n):
                g = t * N + n
                dve.wait_ge(sem["b"], g + 1)
                if n == 0:
                    dve.wait_ge(sem["w"], t + 1)
                wait(dve, sem["scan"], g - NDBU + 1)
                nc.vector.tensor_tensor(dbu[:, n % NDBU, :], w[:, r, :], b_ps(n), ALU.mult).then_inc(sem["dbu"], 1)

            def scan(t, n, slot):
                g = t * N + n
                dve.wait_ge(sem["da"], g + 1)
                dve.wait_ge(sem["dbu"], g + 1)
                wait(dve, sem["hc"], g - N + 1)
                first = h[:, n, T - 1:T] if slot is None else carry[:, slot, n:n + 1] if isinstance(slot, int) \
                    else carry[:, bass.ds(slot, 1), n:n + 1].rearrange("p a n -> p (a n)")
                nc.vector.tensor_tensor_scan(h[:, n, :], da[:, n % NDA, :], dbu[:, n % NDBU, :], first, ALU.mult, ALU.add
                                             ).then_inc(sem["scan"], 1)

            def gate(t, r):
                dve.wait_ge(sem["y"], t * N + N)
                dve.wait_ge(sem["zs"], t + 1)
                wait(dve, sem["out"], t)
                nc.vector.tensor_tensor(yz[:], zs[:, r, :], y_ps[r], ALU.mult).then_inc(sem["yz"], 1)

            def residual(t):
                dve.wait_ge(sem["out"], t + 1)
                x = X[:, :, bass.ds(t * PT, PT)].rearrange("p i (h w) -> p i h w", w=SIDE)
                nc.vector.tensor_tensor(x, x, zb_ps[:, 0:T // 2].rearrange("p (h i w) -> p i h w", i=2, w=SIDE), ALU.add
                                        ).then_inc(sem["res"], 1)

            nc.vector.tensor_tensor(fold[:].rearrange("p g d -> p (g d)"), par("in_u"), par("taps"), ALU.mult
                                    ).then_inc(s_fold, 1)
            nc.vector.tensor_scalar(diagD[:], ident[:], par("D"), None, ALU.mult).then_inc(s_fold, 1)
            dve.wait_ge(s_tok, 4)
            nc.vector.tensor_scalar(ubc[:], m["ones"][:], tok[:, 0:1], None, ALU.mult).then_inc(s_tok, 1)
            split_one(0, 0, 0)
            split_two(0, 0)
            times_b(0, 0, 0)
            dve.wait_ge(s_tok, 7)
            dve.wait_ge(tsem["w"], 1)
            nc.vector.tensor_scalar(carry[:, 0, :], bank(5, N), tok[:, 9:10], None, ALU.mult).then_inc(s_tok, 1)
            dve.wait_ge(s_tok, 8)

            def tile(t, r, p, slot, last):
                for n in range(N):
                    if n + 1 < N:
                        times_b(t, r, n + 1)
                    elif not last:
                        times_b(t + 1, 1 - r, 0)
                    scan(t, n, slot)
                    if n == D_GATE and not (isinstance(t, int) and t == 0):
                        gate(t - 1, 1 - r)
                    if n == D_SPLIT and not last:
                        split_one(t + 1, 1 - r, p + 1)
                    if n == D_SPLIT + 2 and not last:
                        split_two(t + 1, 1 - r)
                    if n == D_RES and not (isinstance(t, int) and t == 0):
                        residual(t - 1)

            def pair(p):
                tile(2 * p, 0, p, (p % (TPB // 2) + 1) // 2, False)
                last = isinstance(p, int) and p == NT // 2 - 1
                tile(2 * p + 1, 1, p, None, last)
                if not last:
                    dve.wait_ge(sem["scan"], (2 * p + 2) * N)
                    nc.vector.tensor_copy(carry[:, 1, :], h[:, :, T - 1]).then_inc(sem["carry"], 1)
                    dve.wait_ge(sem["carry"], p + 1)

            tile_pairs(dve, pair)
            gate(NT - 1, 1)
            residual(NT - 1)

        @block.gpsimd
        def _(pool):
            def steps(t, r):
                return softplus_steps(nc, None, pool, sem, {k: v[:] for k, v in sp.items()}, None, None,
                                      u[:, r, :], dt[:, r, :], w[:, r, :], t)[1]

            def times_c(t, r, p, n):
                g = t * N + n
                if n % CN == 0:
                    pool.wait_ge(s_cld[r][n // CN], 16 * (p + 1))
                wait(pool, sem["y"], g - NHC + 1)
                pool.wait_ge(sem["scan"], g + 1)
                nc.gpsimd.tensor_tensor(hc[:, n % NHC, :], h[:, n, :], crep[:, r, n, :], ALU.mult
                                        ).then_inc(sem["hc"], 1)

            for step in steps(0, 0):
                step()
            for step in softplus_steps(nc, None, pool, tsem, {k: tok[:, 2 + q:3 + q] for q, k in enumerate("arefgl")},
                                       None, None, tok[:, 0:1], tok[:, 8:9], tok[:, 9:10], 0)[1]:
                step()

            def tile(t, r, p, last):
                for n in range(N):
                    times_c(t, r, p, n)
                    if not last:
                        if n == P0:
                            steps(t + 1, 1 - r)[0]()
                        if n == P1:
                            steps(t + 1, 1 - r)[1]()
                        if n == P1 + 1:
                            wait(pool, sem["da"], t * N)
                            steps(t + 1, 1 - r)[2]()
                        if n == P1 + 2:
                            wait(pool, sem["dbu"], t * N)
                            steps(t + 1, 1 - r)[3]()

            def pair(p):
                tile(2 * p, 0, p, False)
                tile(2 * p + 1, 1, p, isinstance(p, int) and p == NT // 2 - 1)

            tile_pairs(pool, pair)

        @block.sync
        def _(sp_):
            def count(v):
                return v if isinstance(v, int) else sp_.to_reg(v)

            def spread_c(t, r, p):
                spread, stored, split = count(16 * p), count(16 * (p + 1)), count(t + 1)
                used = [count((t - 2) * N + (k + 1) * CN) for k in range(N // CN)]
                sp_.wait_ge(sem["r1"], split)
                for k in range(N // CN):
                    wait(sp_, s_cld[r][k], spread)
                sp_.dma_start(c_rows[r], r1[N:2 * N, :]).then_inc(s_cst[r], 16)
                sp_.wait_ge(s_cst[r], stored)
                for k in range(N // CN):
                    wait(sp_, sem["hc"], used[k])
                    src = c_rows[r, k * CN:(k + 1) * CN, :].rearrange("n t -> (n t)").unsqueeze(0).to_broadcast([P, CN * T])
                    sp_.dma_start(crep[:, r, k * CN:(k + 1) * CN, :].rearrange("p n t -> p (n t)"), src
                                  ).then_inc(s_cld[r][k], 16)

            def pair(p):
                spread_c(2 * p, 0, p)
                spread_c(2 * p + 1, 1, p)

            tile_pairs(sp_, pair)


TS = 256
KT = (2 * TOK + E * (TS - 1)) // TS
NQ = TOK // P
D = 256
HALVES = TS // P


class Chain:

    def __init__(self, eng, sem):
        self.eng, self.sem, self.n = eng, sem, 0

    def __call__(self, ins):
        self.n += 1
        ins.then_inc(self.sem, 1)
        self.eng.wait_ge(self.sem, self.n)


def route(nc, m, L, gate, grouped):
    ps, iota = m["ps"], m["iota"]
    Xn = m["Xn"][:, 0:2 * TOK].rearrange("p (i t) -> p i t", i=2)
    with ExitStack() as ctx:
        new = ctx.enter_context(semaphores(nc))
        def sb(name, shape, dt=F32):
            return ctx.enter_context(nc.sbuf_tensor(f"{L}_{name}", shape, dt))

        sem = {k: new(f"{L}_{k}") for k in
               "logit turned rows_a rows_d expo ask_e marks rank chain slots".split()}
        s_sent = [new(f"{L}_sent{k}") for k in range(2)]
        rows = sb("rows", [P, NQ, D])
        lg, mx, ixf, ma, mb, sc, mp, tmp = (sb(k, [P, NQ, E]) for k in ("lg", "mx", "ixf", "ma", "mb", "sc", "mp", "tmp"))
        ix = sb("ix", [P, NQ, E], U32)
        g8 = sb("g8", [P, NQ, E])
        one = sb("one", [P, 4, NQ])
        cnt = sb("cnt", [P, 4, E])
        steps = sb("steps", [P, 16])
        big = sb("big", [P, KT * E])
        tef = sb("tef", [P, KT])
        ones_row = m["ones"][:, 0:NQ]
        block = ctx.enter_context(nc.Block())

        def per_token(v):
            return v.unsqueeze(2).to_broadcast([P, NQ, E])

        def per_expert(v):
            return v.unsqueeze(1).to_broadcast([P, NQ, E])

        flat = "p q e -> p (q e)"

        @block.tensor
        def _(pe):
            for q in range(NQ):
                for i in range(2):
                    mm = nc.tensor.matmul(ps[:, 0, q * E:(q + 1) * E], Xn[:, i, q * P:(q + 1) * P],
                                          gate[:, i * E:(i + 1) * E], start=(i == 0), stop=(i == 1))
            mm.then_inc(sem["logit"], 1)
            for q in range(NQ):
                b = 1 + q % 4
                wait(pe, sem["rows_d"] if q % 2 else sem["rows_a"], (q - 4) // 2 + 1 if q >= 4 else 0)
                for i in range(2):
                    mm = nc.tensor.transpose(ps[:, b, i * P:(i + 1) * P], Xn[:, i, q * P:(q + 1) * P], m["ident"][:])
                mm.then_inc(sem["turned"], 1)
            pe.wait_ge(sem["marks"], 1)
            nc.tensor.matmul(ps[:, 5, 0:NQ * E], m["tri"][:], ma[:].rearrange(flat), start=True, stop=False)
            nc.tensor.matmul(ps[:, 5, 0:NQ * E], m["ones"][:], mp[:].rearrange(flat), start=False, stop=True)
            nc.tensor.matmul(ps[:, 6, 0:E], m["ones"][:], cnt[:, 3, :], start=True, stop=True).then_inc(sem["rank"], 1)

        @block.scalar
        def _(act):
            for q in range(0, NQ, 2):
                act.wait_ge(sem["turned"], q + 1)
                nc.scalar.copy(rows[:, q, :], ps[:, 1 + q % 4, 0:D]).then_inc(sem["rows_a"], 1)
            act.wait_ge(sem["ask_e"], 1)
            if grouped:
                nc.scalar.activation(sc[:], sc[:], ACT.Exp).then_inc(sem["expo"], 1)
            else:
                nc.scalar.activation(one[:, 1, :], one[:, 0, :], ACT.Exp).then_inc(sem["expo"], 1)

        @block.vector
        def _(dve):
            link = Chain(dve, sem["chain"])
            for q in range(1, NQ, 2):
                dve.wait_ge(sem["turned"], q + 1)
                nc.vector.tensor_copy(rows[:, q, :], ps[:, 1 + q % 4, 0:D]).then_inc(sem["rows_d"], 1)
            dve.wait_ge(sem["logit"], 1)
            link(nc.vector.tensor_copy(lg[:].rearrange(flat), ps[:, 0, 0:NQ * E]))

            def top(values):
                for q in range(NQ):
                    ins = nc.vector.max(mx[:, q, :], values[:, q, :])
                link(ins)
                for q in range(NQ):
                    ins = nc.vector.max_index(ix[:, q, :], mx[:, q, :], values[:, q, :])
                link(ins)
                link(nc.vector.tensor_copy(ixf[:], ix[:]))

            if not grouped:
                top(lg)
                nc.vector.tensor_tensor(one[:, 0, :], mx[:, :, 1], mx[:, :, 0], ALU.subtract).then_inc(sem["ask_e"], 1)
                dve.wait_ge(sem["expo"], 1)
                link(nc.vector.tensor_scalar(one[:, 2, :], one[:, 1, :], 1.0, None, ALU.add))
                link(nc.vector.reciprocal(m["p01"][:, 0, :], one[:, 2, :]))
                link(nc.vector.tensor_tensor(m["p01"][:, 1, :], one[:, 1, :], m["p01"][:, 0, :], ALU.mult))
            else:
                link(nc.vector.tensor_reduce(one[:, 0, :], lg[:], AX, ALU.max))
                nc.vector.tensor_tensor(sc[:], lg[:], per_token(one[:, 0, :]), ALU.subtract).then_inc(sem["ask_e"], 1)
                dve.wait_ge(sem["expo"], 1)
                link(nc.vector.tensor_reduce(one[:, 1, :], sc[:], AX, ALU.add))
                link(nc.vector.reciprocal(one[:, 2, :], one[:, 1, :]))
                link(nc.vector.tensor_tensor(sc[:], sc[:], per_token(one[:, 2, :]), ALU.mult))
                link(nc.vector.memset(g8[:], -1.0))
                link(nc.vector.tensor_reduce(g8[:, :, 0:4], sc[:].rearrange("p q (g s) -> p q g s", s=2), AX, ALU.max))
                top(g8)
                g4 = iota[:, 0:4].unsqueeze(1).to_broadcast([P, NQ, 4])
                for s, dst in ((0, ma), (1, mb)):
                    link(nc.vector.tensor_tensor(dst[:, :, 0:4], g4, ixf[:, :, s].unsqueeze(2).to_broadcast([P, NQ, 4]),
                                                 ALU.is_equal))
                link(nc.vector.tensor_tensor(tmp[:, :, 0:4], ma[:, :, 0:4], mb[:, :, 0:4], ALU.add))
                for s in range(2):
                    ins = nc.vector.tensor_tensor(lg[:].rearrange("p q (g s) -> p q g s", s=2)[:, :, :, s],
                                                  sc[:].rearrange("p q (g s) -> p q g s", s=2)[:, :, :, s],
                                                  tmp[:, :, 0:4], ALU.mult)
                link(ins)
                top(lg)
                link(nc.vector.tensor_tensor(one[:, 0, :], mx[:, :, 0], mx[:, :, 1], ALU.add))
                link(nc.vector.reciprocal(one[:, 1, :], one[:, 0, :]))
                for s in range(2):
                    ins = nc.vector.tensor_tensor(m["p01"][:, s, :], mx[:, :, s], one[:, 1, :], ALU.mult)
                link(ins)

            link(nc.vector.tensor_tensor(lg[:], per_expert(iota[:, 0:E]), per_token(ixf[:, :, 0]), ALU.is_equal))
            link(nc.vector.tensor_tensor(mb[:], per_expert(iota[:, 0:E]), per_token(ixf[:, :, 1]), ALU.is_equal))
            link(nc.vector.tensor_tensor(ma[:], lg[:], mb[:], ALU.add))
            for e in range(E):
                ins = nc.vector.tensor_tensor_scan(tmp[:, :, e], ones_row, ma[:, :, e], 0.0, ALU.mult, ALU.add)
            link(ins)
            link(nc.vector.tensor_copy(cnt[:, 3, :], tmp[:, NQ - 1, :]))
            nc.vector.tensor_tensor(mp[:], tmp[:], ma[:], ALU.subtract).then_inc(sem["marks"], 1)
            dve.wait_ge(sem["rank"], 1)
            K = TOK // TS
            link(nc.vector.tensor_copy(cnt[:, 0, :], ps[:, 6, 0:E]))
            link(nc.vector.tensor_scalar(steps[:, 0:K], iota[:, 0:K], float(TS), None, ALU.mult))
            link(nc.vector.tensor_tensor(big[:, 0:E * K].rearrange("p (e k) -> p e k", e=E),
                                         cnt[:, 0, :].unsqueeze(2).to_broadcast([P, E, K]),
                                         steps[:, 0:K].unsqueeze(1).to_broadcast([P, E, K]), ALU.is_gt))
            link(nc.vector.tensor_reduce(cnt[:, 1, :], big[:, 0:E * K].rearrange("p (e k) -> p e k", e=E), AX, ALU.add))
            link(nc.vector.tensor_tensor_scan(cnt[:, 2, :], m["ones"][:, 0:E], cnt[:, 1, :], 0.0, ALU.mult, ALU.add))
            link(nc.vector.tensor_tensor(cnt[:, 3, :], cnt[:, 2, :], cnt[:, 1, :], ALU.subtract))
            link(nc.vector.tensor_scalar(cnt[:, 3, :], cnt[:, 3, :], float(TS), None, ALU.mult))
            link(nc.vector.tensor_tensor(big[:].rearrange("p (k e) -> p k e", e=E),
                                         cnt[:, 2, :].unsqueeze(1).to_broadcast([P, KT, E]),
                                         iota[:, 0:KT].unsqueeze(2).to_broadcast([P, KT, E]), ALU.is_le))
            link(nc.vector.tensor_reduce(tef[:], big[:].rearrange("p (k e) -> p k e", e=E), AX, ALU.add))
            link(nc.vector.tensor_scalar(tef[:], tef[:], float(E - 1), None, ALU.min))
            link(nc.vector.tensor_copy(m["tile_e"][:], tef[:]))
            link(nc.vector.tensor_tensor(sc[:], ps[:, 5, 0:NQ * E].rearrange("p (q e) -> p q e", e=E),
                                         per_expert(cnt[:, 3, :]), ALU.add))
            for s, mark in ((0, lg), (1, mb)):
                link(nc.vector.tensor_tensor(tmp[:], mark[:], sc[:], ALU.mult))
                link(nc.vector.tensor_reduce(one[:, 2 + s, :], tmp[:], AX, ALU.add))
                link(nc.vector.tensor_copy(m["slots"][:, s, :], one[:, 2 + s, :]))
            nc.vector.engine_nop().then_inc(sem["slots"], 1)

        @block.gpsimd
        def _(pool):
            pool.wait_ge(sem["slots"], 1)
            pool.wait_ge(sem["rows_a"], NQ // 2)
            pool.wait_ge(sem["rows_d"], NQ // 2)
            for q in range(NQ):
                for s in range(2):
                    nc.gpsimd.indirect_dma_start(
                        out=m["xs"], out_offset=bass.IndirectOffsetOnAxis(ap=m["slots"][:, s, q:q + 1], axis=0),
                        in_=rows[:, q, :], in_offset=None).then_inc(s_sent[s], 16)
            for s in range(2):
                pool.wait_ge(s_sent[s], 16 * NQ)


def experts(nc, m, L, w1, w2, F, gated):
    ps, ident = m["ps"], m["ident"]
    FB = F // P
    HB = FB // 2 if gated else FB
    with ExitStack() as ctx:
        new = ctx.enter_context(semaphores(nc))
        def sb(name, shape, dt=F32):
            return ctx.enter_context(nc.sbuf_tensor(f"{L}_{name}", shape, dt))

        def sems(name, n=2):
            return [new(f"{L}_{name}{k}") for k in range(n)]

        s_x, s_w1, s_w2, s_y = sems("x"), sems("w1"), sems("w2"), sems("y")
        sem = {k: new(f"{L}_{k}") for k in
               "turned xt hid act up out yev".split()}
        w1_t = sb("w1", [P, 2, 2, F])
        w2_t = sb("w2", [P, 2, HB, D])
        xr = sb("xr", [P, 2, HALVES, D])
        xT = sb("xT", [P, 2, 2, TS])
        hT = sb("hT", [P, 2, HB, TS])
        gl = sb("gl", [P, 2, HB, TS]) if gated else None
        yt = sb("yt", [P, 2, HALVES, D])
        xs_v = m["xs"].rearrange("(k h p) d -> k p h d", h=HALVES, p=P)
        ys_v = m["ys"].rearrange("(k h p) d -> k p h d", h=HALVES, p=P)
        block = ctx.enter_context(nc.Block())
        NBK = FB // 2
        SBK = NBK // 2 if gated else NBK

        def loop(eng, body):
            body(0, 0)
            body(1, 1)
            with eng.Fori(1, (KT - 1) // 2) as p:
                body(2 * p, 0)
                body(2 * p + 1, 1)
            for k in range(2 * ((KT - 1) // 2), KT):
                body(k, k % 2)

        def times(k, r):
            return k // 2 + 1 if isinstance(k, int) else (k - r) // 2 + 1

        @block.sync
        def _(sp):
            def load(k, r):
                wait(sp, sem["turned"], k - 1)
                sp.dma_start(xr[:, r, :, :], xs_v[bass.ds(k, 1)].rearrange("k p h d -> p (k h) d")
                             if not isinstance(k, int) else xs_v[k]).then_inc(s_x[r], 16)
                e = nc.sync.value_load(m["tile_e"][0:1, bass.ds(k, 1)], min_val=0, max_val=E - 1)
                wait(sp, sem["hid"], (k - 1) * NBK)
                sp.dma_start(w1_t[:, r, :, :].rearrange("p i f -> p (i f)"),
                             w1[bass.ds(e, 1)].rearrange("e p f -> (e p) f")).then_inc(s_w1[r], 16)
                wait(sp, sem["out"], k - 1)
                sp.dma_start(w2_t[:, r, :, :].rearrange("p b d -> p (b d)"),
                             w2[bass.ds(e, 1)].rearrange("e p f -> (e p) f")).then_inc(s_w2[r], 16)

            def store(k, r):
                sp.wait_ge(sem["yev"], k + 1)
                sp.dma_start(ys_v[bass.ds(k, 1)].rearrange("k p h d -> p (k h) d")
                             if not isinstance(k, int) else ys_v[k], yt[:, r, :, :]).then_inc(s_y[r], 16)

            load(0, 0)
            load(1, 1)
            with sp.Fori(0, (KT - 3) // 2) as p:
                for r in range(2):
                    store(2 * p + r, r)
                    load(2 * p + r + 2, r)
            for k in range(2 * ((KT - 3) // 2), KT):
                store(k, k % 2)
                if k + 2 < KT:
                    load(k + 2, k % 2)
            for r in range(2):
                sp.wait_ge(s_y[r], 16 * ((KT - r + 1) // 2))

        @block.tensor
        def _(pe):
            def turn(k, r):
                pe.wait_ge(s_x[r], 16 * times(k, r))
                wait(pe, sem["xt"], k)
                for h in range(HALVES):
                    for i in range(2):
                        mm = nc.tensor.transpose(ps[:, 6, i * TS + h * P:i * TS + (h + 1) * P],
                                                 xr[:, r, h, i * P:(i + 1) * P], ident[:])
                mm.then_inc(sem["turned"], 1)

            def body(k, r):
                pe.wait_ge(sem["xt"], k + 1)
                pe.wait_ge(s_w1[r], 16 * times(k, r))
                for b in range(NBK):
                    wait(pe, sem["act" if b < SBK else "up"], (k - 1) * SBK + b % SBK + 1)
                    for f in (2 * b, 2 * b + 1):
                        for i in range(2):
                            mm = nc.tensor.matmul(ps[:, b, (f % 2) * TS:(f % 2 + 1) * TS],
                                                  w1_t[:, r, i, f * P:(f + 1) * P], xT[:, r, i, :],
                                                  start=(i == 0), stop=(i == 1))
                    mm.then_inc(sem["hid"], 1)
                if not (isinstance(k, int) and k == KT - 1):
                    turn(k + 1, 1 - r)
                pe.wait_ge(s_w2[r], 16 * times(k, r))
                wait(pe, sem["yev"], k)
                pe.wait_ge(sem["up" if gated else "act"], (k + 1) * SBK)
                for h in range(HALVES):
                    for f in range(HB):
                        mm = nc.tensor.matmul(ps[:, 7, h * D:(h + 1) * D], hT[:, r, f, h * P:(h + 1) * P],
                                              w2_t[:, r, f, :], start=(f == 0), stop=(f == HB - 1))
                mm.then_inc(sem["out"], 1)

            turn(0, 0)
            loop(pe, body)

        @block.scalar
        def _(act):
            def body(k, r):
                wait(act, sem["out"], k - 1)
                for b in range(NBK):
                    act.wait_ge(sem["hid"], k * NBK + b + 1)
                    src = ps[:, b, 0:2 * TS]
                    if not gated:
                        nc.scalar.activation(hT[:, r, 2 * b:2 * b + 2, :].rearrange("p b t -> p (b t)"), src, ACT.Gelu
                                             ).then_inc(sem["act"], 1)
                    elif b < NBK // 2:
                        nc.scalar.activation(gl[:, r, 2 * b:2 * b + 2, :].rearrange("p b t -> p (b t)"), src, ACT.Silu
                                             ).then_inc(sem["act"], 1)

            loop(act, body)

        @block.vector
        def _(dve):
            def move_x(k, r):
                dve.wait_ge(sem["turned"], k + 1)
                wait(dve, sem["hid"], (k - 1) * NBK)
                nc.vector.tensor_copy(xT[:, r, :, :].rearrange("p i t -> p (i t)"), ps[:, 6, 0:2 * TS]
                                      ).then_inc(sem["xt"], 1)

            def body(k, r):
                if gated:
                    for b in range(NBK // 2, NBK):
                        dve.wait_ge(sem["hid"], k * NBK + b + 1)
                        dve.wait_ge(sem["act"], k * SBK + b - SBK + 1)
                        if b == NBK // 2:
                            wait(dve, sem["out"], k - 1)
                        c = 2 * b - HB
                        nc.vector.tensor_tensor(hT[:, r, c:c + 2, :].rearrange("p b t -> p (b t)"),
                                                gl[:, r, c:c + 2, :].rearrange("p b t -> p (b t)"),
                                                ps[:, b, 0:2 * TS], ALU.mult).then_inc(sem["up"], 1)
                if not (isinstance(k, int) and k == KT - 1):
                    move_x(k + 1, 1 - r)
                dve.wait_ge(sem["out"], k + 1)
                if not (isinstance(k, int) and k < 2):
                    dve.wait_ge(s_y[r], 16 * (times(k, r) - 1))
                nc.vector.tensor_copy(yt[:, r, :, :].rearrange("p h d -> p (h d)"), ps[:, 7, 0:HALVES * D]
                                      ).then_inc(sem["yev"], 1)

            move_x(0, 0)
            loop(dve, body)


def combine(nc, m, L):
    X, ps = m["X"], m["ps"]
    NB = 4
    with ExitStack() as ctx:
        new = ctx.enter_context(semaphores(nc))
        got = ctx.enter_context(nc.sbuf_tensor(f"{L}_got", [P, NB, 2, D], F32))
        mix = ctx.enter_context(nc.sbuf_tensor(f"{L}_mix", [P, NB, 2, D], F32))
        s_got = [new(f"{L}_got{k}") for k in range(NB)]
        sem = {k: new(f"{L}_{k}") for k in "scaled mixed turned added".split()}
        block = ctx.enter_context(nc.Block())

        @block.gpsimd
        def _(pool):
            for q in range(NQ):
                wait(pool, sem["mixed"], q - NB + 1)
                for s in range(2):
                    nc.gpsimd.indirect_dma_start(
                        out=got[:, q % NB, s, :], out_offset=None, in_=m["ys"],
                        in_offset=bass.IndirectOffsetOnAxis(ap=m["slots"][:, s, q:q + 1], axis=0)
                        ).then_inc(s_got[q % NB], 16)

        @block.scalar
        def _(act):
            for q in range(NQ):
                act.wait_ge(s_got[q % NB], 32 * (q // NB + 1))
                wait(act, sem["mixed"], q - NB + 1)
                nc.scalar.activation(mix[:, q % NB, 0, :], got[:, q % NB, 0, :], ACT.Copy,
                                     scale=m["p01"][:, 0, q:q + 1]).then_inc(sem["scaled"], 1)

        @block.vector
        def _(dve):
            for q in range(NQ + 1):
                if q < NQ:
                    dve.wait_ge(sem["scaled"], q + 1)
                    wait(dve, sem["turned"], q - NB + 1)
                    nc.vector.scalar_tensor_tensor(out=mix[:, q % NB, 1, :], in0=got[:, q % NB, 1, :],
                                                   scalar=m["p01"][:, 1, q:q + 1], in1=mix[:, q % NB, 0, :],
                                                   op0=ALU.mult, op1=ALU.add).then_inc(sem["mixed"], 1)
                if q > 0:
                    b = q - 1
                    dve.wait_ge(sem["turned"], b + 1)
                    x = X[:, :, b * P:(b + 1) * P]
                    nc.vector.tensor_tensor(x, x, ps[:, b % 4, 0:D].rearrange("p (i t) -> p i t", i=2), ALU.add
                                            ).then_inc(sem["added"], 1)

        @block.tensor
        def _(pe):
            for q in range(NQ):
                pe.wait_ge(sem["mixed"], q + 1)
                wait(pe, sem["added"], q - 3)
                for i in range(2):
                    mm = nc.tensor.transpose(ps[:, q % 4, i * P:(i + 1) * P], mix[:, q % NB, 1, i * P:(i + 1) * P],
                                             m["ident"][:])
                mm.then_inc(sem["turned"], 1)


def program(nc, inputs, out):
    with ExitStack() as ctx:
        def sb(name, shape, dt=F32):
            return ctx.enter_context(nc.sbuf_tensor(name, shape, dt))

        m = {
            "ps": ctx.enter_context(nc.psum_tensor("ps", [P, 8, 512], F32)),
            "X": sb("X", [P, 2, TOK]),
            "Xn": sb("Xn", [P, BATCH * IMG]),
            "ident": sb("ident", [P, P]),
            "ones": sb("ones", [P, P]),
            "ones_c": sb("ones_c", [P, P]),
            "sel": sb("sel", [BC, 2 * N, P], BF16),
            "mask": sb("mask", [P, 2]),
            "tri": sb("tri", [P, P]),
            "iota": sb("iota", [P, 64]),
            "slots": sb("slots", [P, 2, NQ], U32),
            "p01": sb("p01", [P, 2, NQ]),
            "tile_e": sb("tile_e", [P, KT], mybir.dt.int32),
            "xs": nc.dram_tensor("slot_rows", (KT * TS, D), F32, kind="Internal").ap(),
            "c_rows": nc.dram_tensor("c_rows", (2, N, T), F32, kind="Internal").ap(),
            "ys": nc.dram_tensor("slot_results", (KT * TS, D), F32, kind="Internal").ap(),
        }
        wp = sb("wp", [P, 2, PACKW])
        zero = sb("zero", [P, 2048])
        gates = sb("gates", [P, 2, 2 * E])
        s_load = [ctx.enter_context(nc.semaphore(f"load{k}")) for k in range(10)]
        s_zero = ctx.enter_context(nc.semaphore("zeroed"))
        s_one = ctx.enter_context(nc.semaphore("one"))
        s_out = ctx.enter_context(nc.semaphore("stored"))

        with nc.sbuf_tensor("sel_f", [BC, 2 * N, P], F32) as sel_f, nc.Block() as block:
            @block.sync
            def _(eng):
                loads = [(m["X"][:], inputs["x"]), (m["ident"][:], inputs["ident"]), (sel_f[:], inputs["sel"]),
                         (m["mask"][:], inputs["mask"]), (wp[:, 0, :], inputs["pack0"]), (wp[:, 1, :], inputs["pack1"]),
                         (m["tri"][:], inputs["tri"]), (m["iota"][:], inputs["iota"]), (gates[:, 0, :], inputs["gate0"]),
                         (gates[:, 1, :], inputs["gate1"])]
                for s, (dst, src) in zip(s_load, loads):
                    eng.dma_start(dst, src).then_inc(s, 16)
                eng.wait_ge(s_one, 3)
                rows = 2048 // D * P
                for a in range(0, KT * TS, rows):
                    b = min(a + rows, KT * TS)
                    eng.dma_start(m["xs"][a:b, :].rearrange("(p r) d -> p (r d)", p=P), zero[:, 0:(b - a) // P * D]
                                  ).then_inc(s_zero, 16)
                for s in s_load:
                    eng.wait_ge(s, 16)
                eng.wait_ge(s_zero, 16 * -(-KT * TS // rows))

            @block.vector
            def _(eng):
                nc.vector.memset(zero[:], 0.0).then_inc(s_one, 1)
                nc.vector.memset(m["ones"][:], 1.0).then_inc(s_one, 1)
                nc.vector.memset(m["ones_c"][:], 1.0 / 256).then_inc(s_one, 1)
                eng.wait_ge(s_load[2], 16)
                nc.vector.tensor_copy(m["sel"][:], sel_f[:]).then_inc(s_one, 1)

        for layer in range(LAYERS):
            a, b = PACK["tok"]
            layer_norm(nc, m, f"L{layer}c", 1e-6, wp[:, layer, a:b])
            mamba(nc, m, f"L{layer}", wp[:, layer, :])
            if STAGES <= 2 * layer + 1:
                break
            layer_norm(nc, m, f"L{layer}t", 1e-5)
            route(nc, m, f"L{layer}r", gates[:, layer, :], layer == 1)
            experts(nc, m, f"L{layer}e", inputs[f"up{layer}"], inputs[f"down{layer}"], 1024, layer == 1)
            combine(nc, m, f"L{layer}s")
            if STAGES <= 2 * layer + 2:
                break

        with nc.Block() as block:
            @block.sync
            def _(eng):
                eng.dma_start(out, m["X"][:]).then_inc(s_out, 16)
                eng.wait_ge(s_out, 16)


LAYERS = 2
STAGES = 4


def pack(np, g):
    a = np.zeros((P, PACKW), np.float32)

    def put(name, v, r0=0, c0=0):
        a[r0:r0 + v.shape[0], PACK[name][0] + c0:PACK[name][0] + c0 + v.shape[1]] = v

    in_t = g("in_proj_w").T
    for k, taps in enumerate(((2, 3), (0, 1), (3, None), (1, 2), (None, 0))):
        for j, tap in enumerate(taps):
            if tap is not None:
                put("in_u", in_t[:, :P], 64 * j, P * k)
                put("taps", np.tile(g("conv_w")[:, tap], (64, 1)), 64 * j, P * k)
    for j in range(2):
        put("in_z", in_t[:, P:], 64 * j, P * j)
        put("out", g("out_proj_w").T, 0, P * j + 64 * j)
    put("tok", g("global_token").reshape(64, 1), 64)
    put("bc", np.tile(g("x_proj_w")[4:].T, (1, 3)))
    put("xdt", g("x_proj_w")[:4])
    put("dtw", g("dt_proj_w").T)
    put("conv_b", g("conv_b").reshape(P, 1))
    put("dt_b", g("dt_proj_b").reshape(P, 1))
    put("D", g("D").reshape(P, 1))
    put("A", g("A_log"))
    return a


def host_arrays(np, inputs):
    x = np.asarray(inputs["x"]).reshape(BATCH, 64, 2, 2, PIX)
    arrays = {"x": np.ascontiguousarray(x.transpose(3, 1, 2, 0, 4)).reshape(P, 2, TOK)}
    for l in range(2):
        arrays[f"pack{l}"] = pack(np, lambda k: np.asarray(inputs[f"L{l}_conv_{k}"]))
    arrays["ident"] = np.eye(P, dtype=np.float32)
    sel = np.zeros((BC, 2 * N, P), np.float32)
    for r in range(BC):
        sel[r, r % 32, :] = 1
    arrays["sel"] = sel
    mask = np.zeros((P, 2), np.float32)
    mask[32:, 0] = -1
    mask[64:, 1] = -1
    arrays["mask"] = mask
    arrays["tri"] = np.triu(np.ones((P, P), np.float32), 1)
    arrays["iota"] = np.tile(np.arange(64, dtype=np.float32), (P, 1))

    def chans_first(w):
        w = w.reshape(w.shape[:-1] + (64, 2, 2))
        n = w.ndim
        return np.ascontiguousarray(w.transpose(tuple(range(n - 4)) + (n - 1, n - 3, n - 2, n - 4)))

    for l, (up, down) in enumerate((("w1", "w2"), ("w13_weight", "w2_weight"))):
        arrays[f"gate{l}"] = chans_first(np.asarray(inputs[f"L{l}_ffn_gate_w"])).reshape(P, 2 * E)
        arrays[f"up{l}"] = chans_first(np.asarray(inputs[f"L{l}_ffn_{up}"])).reshape(E, P, -1)
        w2 = np.asarray(inputs[f"L{l}_ffn_{down}"])
        w2 = w2.reshape(E, 64, 2, 2, -1, P).transpose(0, 5, 4, 2, 3, 1)
        arrays[f"down{l}"] = np.ascontiguousarray(w2).reshape(E, P, -1)
    return arrays


def kernel(**inputs):
    import numpy as np
    import concourse.bacc as bacc
    from concourse.bass_utils import run_bass_kernel_spmd

    nc = bacc.Bacc("TRN2", target_bir_lowering=False, num_devices=1)
    arrays = host_arrays(np, inputs)
    aps = {k: nc.dram_tensor(f"in_{k}", a.shape, mybir.dt.from_np(a.dtype), kind="ExternalInput").ap()
           for k, a in arrays.items()}
    out = nc.dram_tensor("out", (P, 2, TOK), F32, kind="ExternalOutput").ap()
    program(nc, aps, out)
    r = run_bass_kernel_spmd(nc, [{f"in_{k}": a for k, a in arrays.items()}], core_ids=[0])
    y = r.results[0]["out"].reshape(2, 64, 2, BATCH, PIX)
    return np.ascontiguousarray(y.transpose(3, 1, 2, 0, 4)).reshape(BATCH, 256, SIDE, SIDE)
```

```python
from contextlib import ExitStack, contextmanager

import concourse.bass as bass
from concourse import mybir

F32 = mybir.dt.float32
BF16 = mybir.dt.bfloat16
U32 = mybir.dt.uint32
ALU = mybir.AluOpType
ACT = mybir.ActivationFunctionType
AX = mybir.AxisListType.X

P = 128
BATCH, SIDE = 4, 24
PIX = SIDE * SIDE
TOK = BATCH * PIX
ROWS = 4
PT = ROWS * SIDE
T = 4 * PT
NT = TOK // PT
TPB = PIX // PT
N = 16
TAPS = 4
E = 8
NDA, NDBU, NHC = 8, 4, 8
NBP = 4
LEAD, LAG = 3, 3
A0, A1 = 4, 11
D_GATE, D_SPLIT, D_RES = 4, 2, 7
P0, P1 = 6, 9
CN = 4
PAD = 2
IMG = PAD + 2 * PIX
EXP_LN, LN, SILU = "natural_log_exp_and_others", "natural_log", "silu_and_others"
BC = 96

PACK = {}
_at = 0
for _name, _w in (("in_u", 5 * P), ("taps", 5 * P), ("in_z", 2 * P), ("bc", BC), ("out", 2 * P), ("conv_b", 1), ("dt_b", 1), ("D", 1),
                  ("A", N), ("tok", 1), ("xdt", 128), ("dtw", 128)):
    PACK[_name] = (_at, _at + _w)
    _at += _w
PACKW = _at


@contextmanager
def semaphores(nc):
    made = []

    def new(name):
        made.append(nc.alloc_semaphore(name))
        return made[-1]

    yield new
    nc.clear_and_free_semaphores(made)
    nc.all_engine_barrier()


def wait(eng, sem, count):
    if isinstance(count, int) and count <= 0:
        return
    eng.wait_ge(sem, count)


def tile_pairs(eng, body):
    body(0)
    with eng.Fori(1, NT // 2 - 1) as p:
        body(p)
    body(NT // 2 - 1)


def layer_norm(nc, m, L, eps, tok=None, tok_in=None, loads=(), x_in=None, settled=(), cast=None):
    X, ps, ones = m["X"], m["ps"], m["ones_c"]
    seq = tok is not None
    NB = 2 * BATCH if seq else 6
    W = TOK // NB
    IN = SIDE if seq else P

    def block_of(q):
        if seq:
            a = (q // 2) * IMG + PAD + (q % 2) * 2 * W
            return m["Xn"][:, a:a + 2 * W].rearrange("p (h i w) -> p i h w", i=2, w=SIDE)
        return m["Xn"][:, q * 2 * W:(q + 1) * 2 * W].rearrange("p (g i t) -> p i g t", i=2, t=P)

    def rows(v):
        return v.rearrange("p (h w) -> p h w", w=IN)

    def both(v):
        return rows(v).unsqueeze(1).to_broadcast([P, 2, W // IN, IN])

    with ExitStack() as ctx:
        new = ctx.enter_context(semaphores(nc))
        sem = {k: new(f"{L}_{k}") for k in ("mean", "cent", "sq", "var", "ln", "rstd", "norm")}
        sq = ctx.enter_context(nc.sbuf_tensor(f"{L}_sq", [P, 2, 2, W], F32))
        rs = ctx.enter_context(nc.sbuf_tensor(f"{L}_rs", [P, 3, W], F32))
        block = ctx.enter_context(nc.Block())

        @block.sync
        def _(sp):
            for dst, src, s in loads:
                sp.dma_start(dst, src).then_inc(s, 16)
            for s in settled:
                sp.wait_ge(s, 16)

        if cast:
            @block.gpsimd
            def _(pool):
                pool.wait_ge(cast[2], 16)
                nc.gpsimd.tensor_copy(cast[0], cast[1])

        @block.tensor
        def _(pe):
            for q in range(NB + 1):
                if q < NB:
                    wait(pe, sem["cent"], q - 1)
                    if x_in and q % 2 == 0:
                        pe.wait_ge(x_in[q // 2], 16)
                    for i in range(2):
                        mm = nc.tensor.matmul(ps[:, q % 2, 0:W], ones[:], X[:, i, q * W:(q + 1) * W],
                                              start=(i == 0), stop=(i == 1))
                    mm.then_inc(sem["mean"], 1)
                if q > 0:
                    b = q - 1
                    pe.wait_ge(sem["sq"], 2 * b + 2)
                    wait(pe, sem["ln"], b - 1)
                    for i in range(2):
                        mm = nc.tensor.matmul(ps[:, 2 + b % 2, 0:W], ones[:], sq[:, b % 2, i, :],
                                              start=(i == 0), stop=(i == 1))
                    mm.then_inc(sem["var"], 1)

        @block.vector
        def _(dve):
            if seq:
                dve.wait_ge(tok_in, 16)
                for b in range(BATCH):
                    nc.vector.memset(m["Xn"][:, b * IMG:b * IMG + 1], 0.0)
                    nc.vector.tensor_copy(m["Xn"][:, b * IMG + 1:b * IMG + PAD], tok)
            for q in range(NB + 2):
                if q < NB:
                    if x_in and q % 2 == 0:
                        dve.wait_ge(x_in[q // 2], 16)
                    dve.wait_ge(sem["mean"], q + 1)
                    nc.vector.tensor_tensor(block_of(q), X[:, :, q * W:(q + 1) * W].rearrange(
                        "p i (h w) -> p i h w", w=IN), both(ps[:, q % 2, 0:W]), ALU.subtract
                        ).then_inc(sem["cent"], 1)
                if q > 1:
                    b = q - 2
                    dve.wait_ge(sem["rstd"], b + 1)
                    nc.vector.tensor_tensor(block_of(b), block_of(b), both(rs[:, b % 3, :]), ALU.mult
                                            ).then_inc(sem["norm"], 1)

        @block.scalar
        def _(act):
            nc.scalar.preload_act_table_set(EXP_LN)
            for q in range(NB + 1):
                if q < NB:
                    act.wait_ge(sem["cent"], q + 1)
                    wait(act, sem["var"], q - 1)
                    for i in range(2):
                        nc.scalar.activation(rows(sq[:, q % 2, i, :]), block_of(q)[:, i], ACT.Square
                                             ).then_inc(sem["sq"], 1)
                if q > 0:
                    b = q - 1
                    act.wait_ge(sem["var"], b + 1)
                    wait(act, sem["norm"], b - 2)
                    nc.scalar.activation(rs[:, b % 3, :], ps[:, 2 + b % 2, 0:W], ACT.Ln, bias=eps
                                         ).then_inc(sem["ln"], 1)
                    act.wait_ge(sem["ln"], b + 1)
                    nc.scalar.activation(rs[:, b % 3, :], rs[:, b % 3, :], ACT.Exp, scale=-0.5
                                         ).then_inc(sem["rstd"], 1)


def softplus_steps(nc, act, pool, sem, s, ps, bias, u, dt, w, k):
    def absolute():
        nc.scalar.activation(s["a"], ps, ACT.Abs, bias=bias).then_inc(sem["abs"], 1)

    def relu():
        nc.scalar.activation(s["r"], ps, ACT.Relu, bias=bias).then_inc(sem["relu"], 1)

    def decayed():
        act.wait_ge(sem["abs"], k + 1)
        nc.scalar.activation(s["e"], s["a"], ACT.Exp, scale=-1.0).then_inc(sem["e"], 1)

    def plus_one():
        act.wait_ge(sem["e"], k + 1)
        nc.scalar.activation(s["f"], s["e"], ACT.Identity, bias=1.0).then_inc(sem["f"], 1)

    def minus_one():
        act.wait_ge(sem["f"], k + 1)
        nc.scalar.activation(s["g"], s["f"], ACT.Identity, bias=-1.0).then_inc(sem["g"], 1)

    def log():
        nc.scalar.activation(s["l"], s["f"], ACT.Ln).then_inc(sem["l"], 1)

    def lost():
        pool.wait_ge(sem["g"], k + 1)
        nc.gpsimd.tensor_tensor(s["a"], s["e"], s["g"], ALU.subtract).then_inc(sem["sum"], 1)

    def add_log():
        pool.wait_ge(sem["l"], k + 1)
        pool.wait_ge(sem["sum"], 3 * k + 1)
        nc.gpsimd.tensor_tensor(s["e"], s["a"], s["l"], ALU.add).then_inc(sem["sum"], 1)

    def add_relu():
        pool.wait_ge(sem["relu"], k + 1)
        pool.wait_ge(sem["sum"], 3 * k + 2)
        nc.gpsimd.tensor_tensor(dt, s["e"], s["r"], ALU.add).then_inc(sem["sum"], 1)

    def times_u():
        pool.wait_ge(sem["sum"], 3 * k + 3)
        nc.gpsimd.tensor_tensor(w, dt, u, ALU.mult).then_inc(sem["w"], 1)

    return (absolute, relu, decayed, plus_one, minus_one, log), (lost, add_log, add_relu, times_u)


def mamba(nc, m, L, wp):
    X, Xn, ps, ident = m["X"], m["Xn"], m["ps"], m["ident"]

    def par(name, rows=P):
        a, b = PACK[name]
        return wp[0:rows, a:b]

    w_z = par("in_z").rearrange("p (j d) -> p j d", j=2)
    w_out = par("out").rearrange("p (j c) -> p j c", j=2)
    FOLDS = ((0, 1, 0), (1, 1, 1), (2, 0, 0), (3, 0, 1), (4, 0, 2))

    with ExitStack() as ctx:
        new = ctx.enter_context(semaphores(nc))

        def sb(name, shape, dt=F32):
            return ctx.enter_context(nc.sbuf_tensor(f"{L}_{name}", shape, dt))

        sem = {k: new(f"{L}_{k}") for k in
               "u_in z_in u zs xp abs relu e f g l sum w hi r1 mid parts b dbu da scan carry hc y yz out res".split()}
        tsem = {k: new(f"{L}_tok_{k}") for k in ("abs", "relu", "e", "f", "g", "l", "sum", "w")}
        s_tok, s_fold, s_negA = new(f"{L}_tok"), new(f"{L}_fold"), new(f"{L}_negA")
        s_cst = [new(f"{L}_c_stored{r}") for r in range(2)]
        s_cld = [[new(f"{L}_c_spread{r}{k}") for k in range(N // CN)] for r in range(2)]

        fold = sb("fold", [P, 5, P])
        diagD = sb("diagD", [P, P])
        negA = sb("negA", [P, 2, N])
        w_dt = sb("w_dt", [P, P])
        carry = sb("carry", [P, 2, N])
        tok = sb("tok", [P, 16])
        ubc = sb("ubc", [P, P])
        u = sb("u", [P, 2, T])
        zs = sb("zs", [P, 2, T])
        sp = {k: sb("sp_" + k, [P, T]) for k in "arefgl"}
        dt = sb("dt", [P, 2, T])
        w = sb("w", [P, 2, T])
        hi = sb("hi", [P, T], BF16)
        mid = sb("mid", [P, T], BF16)
        r1 = sb("r1", [P, T])
        parts = sb("parts", [P, 2, T], BF16)
        da = sb("da", [P, NDA, T])
        dbu = sb("dbu", [P, NDBU, T])
        h = sb("h", [P, N, T])
        crep = sb("crep", [P, 2, N, T])
        hc = sb("hc", [P, NHC, T])
        yz = sb("yz", [P, T])
        c_rows = m["c_rows"]

        def bank(k, w=T):
            return ps[:, k, 0:w]

        def b_ps(n):
            return bank((0, 1, 3, 4)[n % NBP])

        ua_ps, zb_ps = bank(6), bank(7)
        y_ps = (bank(2), bank(5))

        def js(v):
            return v.rearrange("p (s j) -> p j s", j=2)

        def column(t, img, back):
            return Xn[:, bass.ds(t * (T // 2) + img * PAD + (PAD - back), T // 2)]

        block = ctx.enter_context(nc.Block())

        @block.tensor
        def _(pe):
            def u_in(t, img, which):
                if 0 in which:
                    wait(pe, sem["relu"], t)
                for k in which:
                    g, j, back = FOLDS[k]
                    mm = nc.tensor.matmul(ua_ps[:, j * (T // 2):(j + 1) * (T // 2)], fold[:, g, :],
                                          column(t, img, back), start=(k in (0, 2)), stop=(k in (1, 4)))
                if 4 in which:
                    mm.then_inc(sem["u_in"], 1)

            def z_in(t, img):
                wait(pe, sem["res"], t - 1)
                if not (isinstance(t, int) and t == 0):
                    pe.wait_ge(sem["r1"], t + 1)
                for j in range(2):
                    mm = nc.tensor.matmul(zb_ps[:, j * (T // 2):(j + 1) * (T // 2)], w_z[:, j, :],
                                          column(t, img, 0), start=True, stop=True)
                mm.then_inc(sem["z_in"], 1)

            def project_bc(t, r):
                pe.wait_ge(sem["u"], t + 1)
                wait(pe, sem["zs"], max(t, 1) if isinstance(t, int) else t)
                nc.tensor.matmul(zb_ps[0:BC, :], par("bc"), u[:, r, :], start=True, stop=True).then_inc(sem["xp"], 1)

            def project_dt(t, r):
                pe.wait_ge(sem["u"], t + 1)
                nc.tensor.matmul(ua_ps, w_dt[:], u[:, r, :], start=True, stop=True).then_inc(sem["xp"], 1)

            def spread_b(t, r, n):
                g = t * N + n
                wait(pe, sem["dbu"], g - NBP + 1)
                if n == 0:
                    pe.wait_ge(sem["parts"], t + 1)
                nc.tensor.matmul(b_ps(n), m["sel"][:, n, :], parts[0:BC, r, :], start=True, stop=True
                                 ).then_inc(sem["b"], 1)

            def skip(t, r):
                wait(pe, sem["yz"], t - 1)
                nc.tensor.matmul(y_ps[r], diagD[:], u[:, r, :], start=True, stop=False)

            def sum_y(t, r, n):
                pe.wait_ge(sem["hc"], t * N + n + 1)
                nc.tensor.matmul(y_ps[r], ident[:], hc[:, n % NHC, :], start=False, stop=(n == N - 1)
                                 ).then_inc(sem["y"], 1)

            def project_out(t):
                pe.wait_ge(sem["yz"], t + 1)
                for j in range(2):
                    mm = nc.tensor.matmul(zb_ps[:, 0:T // 2], w_out[:, j, :], js(yz[:])[:, j, :],
                                          start=(j == 0), stop=(j == 1))
                mm.then_inc(sem["out"], 1)

            nc.tensor.matmul(bank(0, P), par("xdt", 4), par("dtw", 4), start=True, stop=True).then_inc(s_tok, 1)
            pe.wait_ge(s_fold, 2)
            nc.tensor.matmul(bank(1, 1), fold[:, 0, :], par("tok"), start=True, stop=True).then_inc(s_tok, 1)
            u_in(0, 0, range(5))
            z_in(0, 0)
            pe.wait_ge(s_tok, 5)
            nc.tensor.matmul(bank(4, 1), w_dt[:], tok[:, 0:1], start=True, stop=True).then_inc(s_tok, 1)
            nc.tensor.matmul(bank(5, N), ubc[:], par("bc")[:, 0:N], start=True, stop=True).then_inc(s_tok, 1)
            project_bc(0, 0)
            project_dt(0, 0)
            u_in(1, 0, range(5))
            for n in range(LEAD):
                spread_b(0, 0, n)
            pe.wait_ge(tsem["relu"], 1)

            def tile(t, r, img1, img2, more):
                first = isinstance(t, int) and t == 0
                for n in range(N):
                    if n + LEAD < N:
                        spread_b(t, r, n + LEAD)
                    elif more:
                        spread_b(t + 1, 1 - r, n + LEAD - N)
                    if n >= LAG:
                        if n == LAG:
                            skip(t, r)
                        sum_y(t, r, n - LAG)
                    elif not first:
                        sum_y(t - 1, 1 - r, N - LAG + n)
                    if more:
                        if n == 0:
                            project_bc(t + 1, 1 - r)
                        if n == 1:
                            project_dt(t + 1, 1 - r)
                    if more == 2 and 4 <= n <= 6:
                        u_in(t + 2, img2, ((0, 1), (2, 3), (4,))[n - 4])
                    if n == 6 and not first:
                        if more:
                            pe.wait_ge(sem["r1"], t + 2)
                        project_out(t - 1)
                    if n == 8 and more:
                        z_in(t + 1, img1)

            def pair(p):
                last = isinstance(p, int) and p == NT // 2 - 1
                tile(2 * p, 0, p // (TPB // 2), (p + 1) // (TPB // 2), 1 if last else 2)
                tile(2 * p + 1, 1, (p + 1) // (TPB // 2), (p + 1) // (TPB // 2), 0 if last else 2)

            tile_pairs(pe, pair)
            for n in range(N - LAG, N):
                sum_y(NT - 1, 1, n)
            pe.wait_ge(sem["res"], NT - 1)
            project_out(NT - 1)

        @block.scalar
        def _(act):
            def steps(t, r):
                return softplus_steps(nc, act, None, sem, {k: v[:] for k, v in sp.items()}, ua_ps, par("dt_b"),
                                      None, None, None, t)[0]

            def silu_u(t, r):
                act.wait_ge(sem["u_in"], t + 1)
                wait(act, sem["y"], (t - 2) * N + 1)
                nc.scalar.activation(js(u[:, r, :]), ua_ps.rearrange("p (j s) -> p j s", j=2), ACT.Silu,
                                     bias=par("conv_b")).then_inc(sem["u"], 1)

            def silu_z(t, r):
                act.wait_ge(sem["z_in"], t + 1)
                wait(act, sem["yz"], t - 1)
                nc.scalar.activation(js(zs[:, r, :]), zb_ps.rearrange("p (j s) -> p j s", j=2), ACT.Silu
                                     ).then_inc(sem["zs"], 1)

            def b_high(t):
                act.wait_ge(sem["xp"], 2 * t + 1)
                wait(act, sem["r1"], t)
                nc.scalar.copy(hi[0:BC, :], zb_ps[0:BC, :]).then_inc(sem["hi"], 1)

            def b_mid(t):
                act.wait_ge(sem["r1"], t + 1)
                wait(act, sem["parts"], t)
                nc.scalar.copy(mid[0:BC, :], r1[0:BC, :]).then_inc(sem["mid"], 1)

            def dt_head(t, r):
                act.wait_ge(sem["xp"], 2 * t + 2)
                wait(act, sem["w"], t)
                steps(t, r)[0]()
                steps(t, r)[1]()

            def decay(t, r, n):
                g = t * N + n
                if n == 0:
                    act.wait_ge(sem["sum"], 3 * t + 3)
                wait(act, sem["scan"], g - NDA + 1)
                nc.scalar.activation(da[:, n % NDA, :], dt[:, r, :], ACT.Exp, scale=negA[:, 0, n:n + 1]
                                     ).then_inc(sem["da"], 1)

            nc.scalar.preload_act_table_set(EXP_LN)
            nc.scalar.activation(negA[:, 1, :], par("A"), ACT.Exp).then_inc(s_negA, 1)
            act.wait_ge(s_negA, 1)
            nc.scalar.mul(negA[:, 0, :], negA[:, 1, :], -1.0).then_inc(s_negA, 1)
            act.wait_ge(s_tok, 2)
            nc.scalar.copy(w_dt[:], bank(0, P)).then_inc(s_tok, 1)
            nc.scalar.preload_act_table_set(SILU)
            nc.scalar.activation(tok[:, 0:1], bank(1, 1), ACT.Silu, bias=par("conv_b")).then_inc(s_tok, 1)
            silu_u(0, 0)
            silu_z(0, 0)
            nc.scalar.preload_act_table_set(EXP_LN)
            b_high(0)
            dt_head(0, 0)
            for step in steps(0, 0)[2:5]:
                step()
            b_mid(0)
            act.wait_ge(s_tok, 7)
            of_tok = softplus_steps(nc, act, None, tsem, {k: tok[:, 2 + q:3 + q] for q, k in enumerate("arefgl")},
                                    bank(4, 1), par("dt_b"), None, None, None, 0)[0]
            for step in of_tok[0:5]:
                step()
            nc.scalar.preload_act_table_set(LN)
            steps(0, 0)[5]()
            of_tok[5]()
            nc.scalar.preload_act_table_set(SILU)
            silu_u(1, 1)
            nc.scalar.preload_act_table_set(EXP_LN)
            act.wait_ge(s_negA, 2)

            def tile(t, r, more):
                for n in range(N):
                    decay(t, r, n)
                    if not more:
                        continue
                    if n == A0:
                        b_high(t + 1)
                    if n == A0 + 1:
                        dt_head(t + 1, 1 - r)
                        steps(t + 1, r)[2]()
                    if n == A0 + 2:
                        b_mid(t + 1)
                        steps(t + 1, r)[3]()
                    if n == A0 + 3:
                        steps(t + 1, r)[4]()
                    if n == A1:
                        nc.scalar.preload_act_table_set(LN)
                        steps(t + 1, r)[5]()
                        nc.scalar.preload_act_table_set(SILU)
                        if more == 2:
                            silu_u(t + 2, r)
                        silu_z(t + 1, 1 - r)
                        nc.scalar.preload_act_table_set(EXP_LN)

            def pair(p):
                last = isinstance(p, int) and p == NT // 2 - 1
                tile(2 * p, 0, 1 if last else 2)
                tile(2 * p + 1, 1, 0 if last else 2)

            tile_pairs(act, pair)

        @block.vector
        def _(dve):
            def split_one(t, r, before):
                wait(dve, s_cst[1 - r], 16 * before)
                dve.wait_ge(sem["hi"], t + 1)
                wait(dve, sem["parts"], t)
                nc.vector.scalar_tensor_tensor(out=r1[0:BC, :], in0=hi[0:BC, :], scalar=m["mask"][0:BC, 0:1],
                                               in1=zb_ps[0:BC, :], op0=ALU.mult, op1=ALU.add
                                               ).then_inc(sem["r1"], 1)

            def split_two(t, r):
                dve.wait_ge(sem["mid"], t + 1)
                wait(dve, sem["b"], (t - 1) * N)
                nc.vector.scalar_tensor_tensor(out=parts[0:BC, r, :], in0=mid[0:BC, :], scalar=m["mask"][0:BC, 1:2],
                                               in1=r1[0:BC, :], op0=ALU.mult, op1=ALU.add
                                               ).then_inc(sem["parts"], 1)

            def times_b(t, r, n):
                g = t * N + n
                dve.wait_ge(sem["b"], g + 1)
                if n == 0:
                    dve.wait_ge(sem["w"], t + 1)
                wait(dve, sem["scan"], g - NDBU + 1)
                nc.vector.tensor_tensor(dbu[:, n % NDBU, :], w[:, r, :], b_ps(n), ALU.mult).then_inc(sem["dbu"], 1)

            def scan(t, n, slot):
                g = t * N + n
                dve.wait_ge(sem["da"], g + 1)
                dve.wait_ge(sem["dbu"], g + 1)
                wait(dve, sem["hc"], g - N + 1)
                first = h[:, n, T - 1:T] if slot is None else carry[:, slot, n:n + 1] if isinstance(slot, int) \
                    else carry[:, bass.ds(slot, 1), n:n + 1].rearrange("p a n -> p (a n)")
                nc.vector.tensor_tensor_scan(h[:, n, :], da[:, n % NDA, :], dbu[:, n % NDBU, :], first, ALU.mult, ALU.add
                                             ).then_inc(sem["scan"], 1)

            def gate(t, r):
                dve.wait_ge(sem["y"], t * N + N)
                dve.wait_ge(sem["zs"], t + 1)
                wait(dve, sem["out"], t)
                nc.vector.tensor_tensor(yz[:], zs[:, r, :], y_ps[r], ALU.mult).then_inc(sem["yz"], 1)

            def residual(t):
                dve.wait_ge(sem["out"], t + 1)
                x = X[:, :, bass.ds(t * PT, PT)].rearrange("p i (h w) -> p i h w", w=SIDE)
                nc.vector.tensor_tensor(x, x, zb_ps[:, 0:T // 2].rearrange("p (h i w) -> p i h w", i=2, w=SIDE), ALU.add
                                        ).then_inc(sem["res"], 1)

            nc.vector.tensor_tensor(fold[:].rearrange("p g d -> p (g d)"), par("in_u"), par("taps"), ALU.mult
                                    ).then_inc(s_fold, 1)
            nc.vector.tensor_scalar(diagD[:], ident[:], par("D"), None, ALU.mult).then_inc(s_fold, 1)
            dve.wait_ge(s_tok, 4)
            nc.vector.tensor_scalar(ubc[:], m["ones"][:], tok[:, 0:1], None, ALU.mult).then_inc(s_tok, 1)
            split_one(0, 0, 0)
            split_two(0, 0)
            times_b(0, 0, 0)
            dve.wait_ge(s_tok, 7)
            dve.wait_ge(tsem["w"], 1)
            nc.vector.tensor_scalar(carry[:, 0, :], bank(5, N), tok[:, 9:10], None, ALU.mult).then_inc(s_tok, 1)
            dve.wait_ge(s_tok, 8)

            def tile(t, r, p, slot, last):
                for n in range(N):
                    if n + 1 < N:
                        times_b(t, r, n + 1)
                    elif not last:
                        times_b(t + 1, 1 - r, 0)
                    scan(t, n, slot)
                    if n == D_GATE and not (isinstance(t, int) and t == 0):
                        gate(t - 1, 1 - r)
                    if n == D_SPLIT and not last:
                        split_one(t + 1, 1 - r, p + 1)
                    if n == D_SPLIT + 2 and not last:
                        split_two(t + 1, 1 - r)
                    if n == D_RES and not (isinstance(t, int) and t == 0):
                        residual(t - 1)

            def pair(p):
                tile(2 * p, 0, p, (p % (TPB // 2) + 1) // 2, False)
                last = isinstance(p, int) and p == NT // 2 - 1
                tile(2 * p + 1, 1, p, None, last)
                if not last:
                    dve.wait_ge(sem["scan"], (2 * p + 2) * N)
                    nc.vector.tensor_copy(carry[:, 1, :], h[:, :, T - 1]).then_inc(sem["carry"], 1)
                    dve.wait_ge(sem["carry"], p + 1)

            tile_pairs(dve, pair)
            gate(NT - 1, 1)
            residual(NT - 1)

        @block.gpsimd
        def _(pool):
            def steps(t, r):
                return softplus_steps(nc, None, pool, sem, {k: v[:] for k, v in sp.items()}, None, None,
                                      u[:, r, :], dt[:, r, :], w[:, r, :], t)[1]

            def times_c(t, r, p, n):
                g = t * N + n
                if n % CN == 0:
                    pool.wait_ge(s_cld[r][n // CN], 16 * (p + 1))
                wait(pool, sem["y"], g - NHC + 1)
                pool.wait_ge(sem["scan"], g + 1)
                nc.gpsimd.tensor_tensor(hc[:, n % NHC, :], h[:, n, :], crep[:, r, n, :], ALU.mult
                                        ).then_inc(sem["hc"], 1)

            for step in steps(0, 0):
                step()
            for step in softplus_steps(nc, None, pool, tsem, {k: tok[:, 2 + q:3 + q] for q, k in enumerate("arefgl")},
                                       None, None, tok[:, 0:1], tok[:, 8:9], tok[:, 9:10], 0)[1]:
                step()

            def tile(t, r, p, last):
                for n in range(N):
                    times_c(t, r, p, n)
                    if not last:
                        if n == P0:
                            steps(t + 1, 1 - r)[0]()
                        if n == P1:
                            steps(t + 1, 1 - r)[1]()
                        if n == P1 + 1:
                            wait(pool, sem["da"], t * N)
                            steps(t + 1, 1 - r)[2]()
                        if n == P1 + 2:
                            wait(pool, sem["dbu"], t * N)
                            steps(t + 1, 1 - r)[3]()

            def pair(p):
                tile(2 * p, 0, p, False)
                tile(2 * p + 1, 1, p, isinstance(p, int) and p == NT // 2 - 1)

            tile_pairs(pool, pair)

        @block.sync
        def _(sp_):
            def count(v):
                return v if isinstance(v, int) else sp_.to_reg(v)

            def spread_c(t, r, p):
                spread, stored, split = count(16 * p), count(16 * (p + 1)), count(t + 1)
                used = [count((t - 2) * N + (k + 1) * CN) for k in range(N // CN)]
                sp_.wait_ge(sem["r1"], split)
                for k in range(N // CN):
                    wait(sp_, s_cld[r][k], spread)
                sp_.dma_start(c_rows[r], r1[N:2 * N, :]).then_inc(s_cst[r], 16)
                sp_.wait_ge(s_cst[r], stored)
                for k in range(N // CN):
                    wait(sp_, sem["hc"], used[k])
                    src = c_rows[r, k * CN:(k + 1) * CN, :].rearrange("n t -> (n t)").unsqueeze(0).to_broadcast([P, CN * T])
                    sp_.dma_start(crep[:, r, k * CN:(k + 1) * CN, :].rearrange("p n t -> p (n t)"), src
                                  ).then_inc(s_cld[r][k], 16)

            def pair(p):
                spread_c(2 * p, 0, p)
                spread_c(2 * p + 1, 1, p)

            tile_pairs(sp_, pair)


TS = 128
KT = (2 * TOK + E * (TS - 1)) // TS
NQ = TOK // P
D = 256
KD = (KT + 1) // 2


class Chain:

    def __init__(self, eng, sem):
        self.eng, self.sem, self.n = eng, sem, 0

    def __call__(self, ins):
        self.n += 1
        ins.then_inc(self.sem, 1)
        self.eng.wait_ge(self.sem, self.n)


def route(nc, m, L, gate, grouped):
    ps, iota = m["ps"], m["iota"]
    Xn = m["Xn"][:, 0:2 * TOK].rearrange("p (q i t) -> p q i t", i=2, t=P)
    rows = m["Xn"][:, 0:2 * TOK].rearrange("p (q d) -> p q d", d=D)
    with ExitStack() as ctx:
        new = ctx.enter_context(semaphores(nc))
        def sb(name, shape, dt=F32):
            return ctx.enter_context(nc.sbuf_tensor(f"{L}_{name}", shape, dt))

        sem = {k: new(f"{L}_{k}") for k in
               "turned rows_a rows_d expo ask_e marks rank chain match map".split()}
        s_sent = new(f"{L}_sent")
        lg, mx, ixf, ma, mb, sc, mp, tmp = (sb(k, [P, NQ, E]) for k in ("lg", "mx", "ixf", "ma", "mb", "sc", "mp", "tmp"))
        ix = sb("ix", [P, NQ, E], U32)
        g8 = sb("g8", [P, NQ, E])
        lg2 = sb("lg2", [P, 2, NQ, E])
        one = sb("one", [P, 4, NQ])
        cnt = sb("cnt", [P, 4, E])
        steps = sb("steps", [P, TOK // TS])
        big = sb("big", [P, 2 * KD * E])
        tef = sb("tef", [P, 2 * KD])
        slot = sb("slot", [P, 2, NQ], U32)
        part = sb("part", [P, 2, 2, NQ], U32)
        partf = sb("partf", [P, 2, 2 * NQ])
        at_p = sb("at_p", [P, 2 * NQ, P], BF16)
        at_k = sb("at_k", [P, 2 * NQ, KT], BF16)
        who = sb("who", [P, 2 * NQ, 2, KT], BF16)
        back = sb("back", [P, 4, KT])
        ones_row = m["ones"][:, 0:NQ]
        block = ctx.enter_context(nc.Block())

        def per_token(v):
            return v.unsqueeze(2).to_broadcast([P, NQ, E])

        def per_expert(v):
            return v.unsqueeze(1).to_broadcast([P, NQ, E])

        flat = "p q e -> p (q e)"

        def made(q):
            return ps[:, 1 + q % 4, 0:2 * (P + E)].rearrange("p (i c) -> p i c", i=2)

        @block.tensor
        def _(pe):
            for q in range(NQ):
                b = 1 + q % 4
                wait(pe, sem["rows_d"] if q % 2 else sem["rows_a"], (q - 4) // 2 + 1 if q >= 4 else 0)
                for i in range(2):
                    mm = nc.tensor.matmul(ps[:, b, i * (P + E):(i + 1) * (P + E)], Xn[:, q, i, :], gate[:, i, :],
                                          start=True, stop=True)
                mm.then_inc(sem["turned"], 1)
            pe.wait_ge(sem["marks"], 1)
            nc.tensor.matmul(ps[:, 5, 0:NQ * E], m["tri"][:], ma[:].rearrange(flat), start=True, stop=False)
            nc.tensor.matmul(ps[:, 5, 0:NQ * E], m["ones"][:], mp[:].rearrange(flat), start=False, stop=True)
            nc.tensor.matmul(ps[:, 6, 0:E], m["ones"][:], cnt[:, 3, :], start=True, stop=True).then_inc(sem["rank"], 1)
            pe.wait_ge(sem["match"], 1)
            for c in range(2 * NQ):
                mm = nc.tensor.matmul(ps[:, 7, 0:2 * KT], at_p[:, c, :], who[:, c].rearrange("p a k -> p (a k)"),
                                      start=(c == 0), stop=(c == 2 * NQ - 1))
            mm.then_inc(sem["map"], 1)

        @block.scalar
        def _(act):
            for q in range(0, NQ, 2):
                act.wait_ge(sem["turned"], q + 1)
                nc.scalar.copy(lg2[:, :, q, :], made(q)[:, :, P:P + E])
                nc.scalar.copy(rows[:, q, :].rearrange("p (i t) -> p i t", i=2), made(q)[:, :, 0:P]
                               ).then_inc(sem["rows_a"], 1)
            act.wait_ge(sem["ask_e"], 1)
            if grouped:
                nc.scalar.activation(sc[:], sc[:], ACT.Exp).then_inc(sem["expo"], 1)
            else:
                nc.scalar.activation(one[:, 1, :], one[:, 0, :], ACT.Exp).then_inc(sem["expo"], 1)

        @block.vector
        def _(dve):
            link = Chain(dve, sem["chain"])
            for q in range(1, NQ, 2):
                dve.wait_ge(sem["turned"], q + 1)
                nc.vector.tensor_copy(lg2[:, :, q, :], made(q)[:, :, P:P + E])
                nc.vector.tensor_copy(rows[:, q, :].rearrange("p (i t) -> p i t", i=2), made(q)[:, :, 0:P]
                                      ).then_inc(sem["rows_d"], 1)
            dve.wait_ge(sem["rows_a"], NQ // 2)
            dve.wait_ge(sem["rows_d"], NQ // 2)
            link(nc.vector.tensor_tensor(lg[:], lg2[:, 0], lg2[:, 1], ALU.add))

            def top(values):
                for q in range(NQ):
                    ins = nc.vector.max(mx[:, q, :], values[:, q, :])
                link(ins)
                for q in range(NQ):
                    ins = nc.vector.max_index(ix[:, q, :], mx[:, q, :], values[:, q, :])
                link(ins)
                link(nc.vector.tensor_copy(ixf[:], ix[:]))

            if not grouped:
                top(lg)
                nc.vector.tensor_tensor(one[:, 0, :], mx[:, :, 1], mx[:, :, 0], ALU.subtract).then_inc(sem["ask_e"], 1)
                dve.wait_ge(sem["expo"], 1)
                link(nc.vector.tensor_scalar(one[:, 2, :], one[:, 1, :], 1.0, None, ALU.add))
                link(nc.vector.reciprocal(m["p01"][:, 0, :], one[:, 2, :]))
                link(nc.vector.tensor_tensor(m["p01"][:, 1, :], one[:, 1, :], m["p01"][:, 0, :], ALU.mult))
            else:
                link(nc.vector.tensor_reduce(one[:, 0, :], lg[:], AX, ALU.max))
                nc.vector.tensor_tensor(sc[:], lg[:], per_token(one[:, 0, :]), ALU.subtract).then_inc(sem["ask_e"], 1)
                dve.wait_ge(sem["expo"], 1)
                link(nc.vector.tensor_reduce(one[:, 1, :], sc[:], AX, ALU.add))
                link(nc.vector.reciprocal(one[:, 2, :], one[:, 1, :]))
                link(nc.vector.tensor_tensor(sc[:], sc[:], per_token(one[:, 2, :]), ALU.mult))
                link(nc.vector.memset(g8[:], -1.0))
                link(nc.vector.tensor_reduce(g8[:, :, 0:4], sc[:].rearrange("p q (g s) -> p q g s", s=2), AX, ALU.max))
                top(g8)
                g4 = iota[:, 0:4].unsqueeze(1).to_broadcast([P, NQ, 4])
                for s, dst in ((0, ma), (1, mb)):
                    link(nc.vector.tensor_tensor(dst[:, :, 0:4], g4, ixf[:, :, s].unsqueeze(2).to_broadcast([P, NQ, 4]),
                                                 ALU.is_equal))
                link(nc.vector.tensor_tensor(tmp[:, :, 0:4], ma[:, :, 0:4], mb[:, :, 0:4], ALU.add))
                for s in range(2):
                    ins = nc.vector.tensor_tensor(lg[:].rearrange("p q (g s) -> p q g s", s=2)[:, :, :, s],
                                                  sc[:].rearrange("p q (g s) -> p q g s", s=2)[:, :, :, s],
                                                  tmp[:, :, 0:4], ALU.mult)
                link(ins)
                top(lg)
                link(nc.vector.tensor_tensor(one[:, 0, :], mx[:, :, 0], mx[:, :, 1], ALU.add))
                link(nc.vector.reciprocal(one[:, 1, :], one[:, 0, :]))
                for s in range(2):
                    ins = nc.vector.tensor_tensor(m["p01"][:, s, :], mx[:, :, s], one[:, 1, :], ALU.mult)
                link(ins)

            link(nc.vector.tensor_tensor(lg[:], per_expert(iota[:, 0:E]), per_token(ixf[:, :, 0]), ALU.is_equal))
            link(nc.vector.tensor_tensor(mb[:], per_expert(iota[:, 0:E]), per_token(ixf[:, :, 1]), ALU.is_equal))
            link(nc.vector.tensor_tensor(ma[:], lg[:], mb[:], ALU.add))
            for e in range(E):
                ins = nc.vector.tensor_tensor_scan(tmp[:, :, e], ones_row, ma[:, :, e], 0.0, ALU.mult, ALU.add)
            link(ins)
            link(nc.vector.tensor_copy(cnt[:, 3, :], tmp[:, NQ - 1, :]))
            nc.vector.tensor_tensor(mp[:], tmp[:], ma[:], ALU.subtract).then_inc(sem["marks"], 1)
            dve.wait_ge(sem["rank"], 1)
            K = TOK // TS
            link(nc.vector.tensor_copy(cnt[:, 0, :], ps[:, 6, 0:E]))
            link(nc.vector.tensor_scalar(steps[:, 0:K], iota[:, 0:K], float(TS), None, ALU.mult))
            link(nc.vector.tensor_tensor(big[:, 0:E * K].rearrange("p (e k) -> p e k", e=E),
                                         cnt[:, 0, :].unsqueeze(2).to_broadcast([P, E, K]),
                                         steps[:, 0:K].unsqueeze(1).to_broadcast([P, E, K]), ALU.is_gt))
            link(nc.vector.tensor_reduce(cnt[:, 1, :], big[:, 0:E * K].rearrange("p (e k) -> p e k", e=E), AX, ALU.add))
            link(nc.vector.tensor_tensor_scan(cnt[:, 2, :], m["ones"][:, 0:E], cnt[:, 1, :], 0.0, ALU.mult, ALU.add))
            link(nc.vector.tensor_tensor(cnt[:, 3, :], cnt[:, 2, :], cnt[:, 1, :], ALU.subtract))
            link(nc.vector.tensor_scalar(cnt[:, 3, :], cnt[:, 3, :], float(TS), None, ALU.mult))
            link(nc.vector.tensor_tensor(big[:].rearrange("p (k e) -> p k e", e=E),
                                         cnt[:, 2, :].unsqueeze(1).to_broadcast([P, 2 * KD, E]),
                                         iota[:, 0:2 * KD].unsqueeze(2).to_broadcast([P, 2 * KD, E]), ALU.is_le))
            link(nc.vector.tensor_reduce(tef[:], big[:].rearrange("p (k e) -> p k e", e=E), AX, ALU.add))
            link(nc.vector.tensor_scalar(tef[:], tef[:], float(E - 1), None, ALU.min))
            link(nc.vector.tensor_copy(m["tile_e"][:], tef[:]))
            link(nc.vector.tensor_tensor(sc[:], ps[:, 5, 0:NQ * E].rearrange("p (q e) -> p q e", e=E),
                                         per_expert(cnt[:, 3, :]), ALU.add))
            for s, mark in ((0, lg), (1, mb)):
                link(nc.vector.tensor_tensor(tmp[:], mark[:], sc[:], ALU.mult))
                link(nc.vector.tensor_reduce(one[:, 2 + s, :], tmp[:], AX, ALU.add))
                link(nc.vector.tensor_copy(slot[:, s, :], one[:, 2 + s, :]))
            link(nc.vector.tensor_scalar(part[:, 0], slot[:], 7, None, ALU.logical_shift_right))
            link(nc.vector.tensor_scalar(part[:, 1], slot[:], P - 1, None, ALU.bitwise_and))
            link(nc.vector.tensor_copy(partf[:].rearrange("p a c -> p (a c)"), part[:].rearrange("p a s q -> p (a s q)")))
            C2 = 2 * NQ
            nc.vector.tensor_tensor(at_p[:], iota[:].unsqueeze(1).to_broadcast([P, C2, P]),
                                    partf[:, 1, :].unsqueeze(2).to_broadcast([P, C2, P]), ALU.is_equal)
            link(nc.vector.tensor_tensor(at_k[:], iota[:, 0:KT].unsqueeze(1).to_broadcast([P, C2, KT]),
                                         partf[:, 0, :].unsqueeze(2).to_broadcast([P, C2, KT]), ALU.is_equal))
            nc.vector.tensor_tensor(who[:, :, 0, :], at_k[:], iota[:, 1:C2 + 1].unsqueeze(2).to_broadcast([P, C2, KT]), ALU.mult)
            nc.vector.tensor_scalar(who[:, :, 1, :], at_k[:], m["row"][:], None, ALU.mult).then_inc(sem["match"], 1)
            dve.wait_ge(sem["map"], 1)
            link(nc.vector.tensor_copy(back[:, 3, :], ps[:, 7, KT:2 * KT]))
            link(nc.vector.scalar_tensor_tensor(out=back[:, 0, :], in0=ps[:, 7, 0:KT], scalar=float(P), in1=back[:, 3, :],
                                                op0=ALU.mult, op1=ALU.add))
            link(nc.vector.tensor_scalar(back[:, 1, :], back[:, 0, :], 0.5, None, ALU.is_lt))
            link(nc.vector.tensor_tensor(back[:, 1, :], back[:, 1, :], m["spare"][:], ALU.mult))
            link(nc.vector.tensor_scalar(back[:, 0, :], back[:, 0, :], float(-P), None, ALU.add))
            link(nc.vector.tensor_tensor(m["give"][:], back[:, 1, :], back[:, 0, :], ALU.add))
            link(nc.vector.tensor_scalar(back[:, 2, :], back[:, 0, :], float(TOK), None, ALU.is_ge))
            link(nc.vector.tensor_scalar(back[:, 2, :], back[:, 2, :], float(-TOK), None, ALU.mult))
            link(nc.vector.tensor_tensor(back[:, 2, :], back[:, 2, :], back[:, 0, :], ALU.add))
            link(nc.vector.tensor_scalar(m["take"][:], back[:, 2, :], 0.0, None, ALU.max))

        @block.sync
        def _(sp):
            G = 6
            for q in range(0, NQ, G):
                sp.wait_ge(sem["rows_a"], (q + G) // 2)
                sp.wait_ge(sem["rows_d"], (q + G) // 2)
                sp.dma_start(m["tok_rows"][q * P:(q + G) * P, :].rearrange("(q p) d -> p q d", p=P), rows[:, q:q + G, :]
                             ).then_inc(s_sent, 16)
            sp.wait_ge(s_sent, 16 * (NQ // G))


def experts(nc, m, L, w1, w2, loaded, F, gated):
    ps, ident = m["ps"], m["ident"]
    FB = F // P
    HB = FB // 2 if gated else FB
    BF = 4
    NBH = FB // BF
    NBK = 2 * NBH
    AB = 1 if gated else NBH
    with ExitStack() as ctx:
        new = ctx.enter_context(semaphores(nc))
        def sb(name, shape, dt=F32):
            return ctx.enter_context(nc.sbuf_tensor(f"{L}_{name}", shape, dt))

        def sems(name, n=2):
            return [new(f"{L}_{name}{k}") for k in range(n)]

        s_x, s_y = sems("x"), sems("y")
        sem = {k: new(f"{L}_{k}") for k in
               "turned xt staged hid act up out yev take give".split()}
        xr = sb("xr", [P, 2, 2, D])
        xT = sb("xT", [P, 2, 2, 2, TS])
        hT = sb("hT", [P, 2, 2, HB, TS])
        gl = sb("gl", [P, 2, 2, HB, TS]) if gated else None
        yt = sb("yt", [P, 2, 2, D])
        w1_t = m["Xn"][:, 0:4 * F].rearrange("p (h i f) -> p h i f", h=2, i=2)
        rows_of = {k: sb(k, [P, 2, 2], U32) for k in ("take", "give")}
        done = {k: sb(f"{k}_done", [P, 2, 2]) for k in rows_of}
        block = ctx.enter_context(nc.Block())

        def tiles(k):
            return KT % 2 if isinstance(k, int) and k == KD - 1 and KT % 2 else 2

        def loop(eng, body):
            body(0, 0)
            body(1, 1)
            with eng.Fori(1, (KD - 1) // 2) as p:
                body(2 * p, 0)
                body(2 * p + 1, 1)
            for k in range(2 * ((KD - 1) // 2), KD):
                body(k, k % 2)

        def times(k, r):
            return k // 2 + 1 if isinstance(k, int) else (k - r) // 2 + 1

        @block.gpsimd
        def _(pool):
            def carry_wait(name, step, r):
                nc.gpsimd.tensor_tensor(done[name][:, step, r:r + 1], m["ones"][:, 0:1], m["ones"][:, 1:2], ALU.mult)

            def index(name, k, r):
                copy, n = rows_of[name], tiles(k)
                src = m[name][:, bass.ds(2 * k, n)]
                carry_wait(name, 0, r)
                nc.gpsimd.tensor_copy(copy[:, r, 0:n], src).then_inc(sem[name], 1)
                pool.wait_ge(sem[name], k + 1)
                carry_wait(name, 1, r)
                return [bass.IndirectOffsetOnAxis(ap=copy[:, r, h:h + 1], axis=0) for h in range(n)]

            def load(k, r):
                wait(pool, sem["turned"], k - 1)
                for h, rows in enumerate(index("take", k, r)):
                    nc.gpsimd.indirect_dma_start(out=xr[:, r, h, :], out_offset=None, in_=m["tok_rows"], in_offset=rows).then_inc(s_x[r], 16)

            def store(k, r):
                pool.wait_ge(sem["yev"], k + 1)
                for h, rows in enumerate(index("give", k, r)):
                    nc.gpsimd.indirect_dma_start(out=m["ys"], out_offset=rows, in_=yt[:, r, h, :],
                                                 in_offset=None).then_inc(s_y[r], 16)

            load(0, 0)
            load(1, 1)
            with pool.Fori(0, (KD - 3) // 2) as p:
                for r in range(2):
                    load(2 * p + r + 2, r)
                    store(2 * p + r, r)
            for k in range(2 * ((KD - 3) // 2), KD):
                if k + 2 < KD:
                    load(k + 2, k % 2)
                store(k, k % 2)
            for r in range(2):
                pool.wait_ge(s_y[r], 16 * sum(tiles(k) for k in range(r, KD, 2)))

        @block.tensor
        def _(pe):
            def turn(k, r):
                pe.wait_ge(s_x[r], 32 * (times(k, r) - 1) + 16 * tiles(k))
                wait(pe, sem["xt"], k)
                for h in range(tiles(k)):
                    for i in range(2):
                        mm = nc.tensor.transpose(ps[:, 6, (2 * i + h) * P:(2 * i + h + 1) * P],
                                                 xr[:, r, h, i * P:(i + 1) * P], ident[:])
                mm.then_inc(sem["turned"], 1)

            def body(k, r):
                e = [pe.value_load(m["tile_e"][0:1, bass.ds(2 * k + h, 1)], min_val=0, max_val=E - 1)
                     for h in range(tiles(k))]
                pe.wait_ge(sem["xt"], k + 1)
                for h in range(tiles(k)):
                    pe.wait_ge(sem["staged"], 2 * k + h + 1)
                    for b in range(NBH):
                        if gated:
                            wait(pe, sem["up" if b else "act"], (k - 1) * 2 + h + 1)
                        else:
                            wait(pe, sem["act"], (k - 1) * NBK + h * NBH + b + 1)
                        for f in range(BF * b, BF * (b + 1)):
                            for i in range(2):
                                mm = nc.tensor.matmul(
                                    ps[:, h * NBH + b, (f % BF) * TS:(f % BF + 1) * TS],
                                    w1_t[:, h, i, f * P:(f + 1) * P],
                                    xT[:, r, i, h, :], start=(i == 0), stop=(i == 1))
                        mm.then_inc(sem["hid"], 1)
                if not (isinstance(k, int) and k == KD - 1):
                    turn(k + 1, 1 - r)
                wait(pe, sem["yev"], k)
                for h in range(tiles(k)):
                    if gated:
                        pe.wait_ge(sem["up"], 2 * k + h + 1)
                    else:
                        pe.wait_ge(sem["act"], k * NBK + (h + 1) * NBH)
                    for f in range(HB):
                        mm = nc.tensor.matmul(ps[:, 7, h * D:(h + 1) * D], hT[:, r, h, f, :],
                                              w2[:, bass.ds(e[h], 1), f, :].rearrange("p e d -> p (e d)"),
                                              start=(f == 0), stop=(f == HB - 1))
                mm.then_inc(sem["out"], 1)

            turn(0, 0)
            for s in loaded[1::2]:
                pe.wait_ge(s, 16)
            loop(pe, body)

        @block.scalar
        def _(act):
            def body(k, r):
                wait(act, sem["out"], k - 1)
                for h in range(tiles(k)):
                    for b in range(AB):
                        act.wait_ge(sem["hid"], k * NBK + h * NBH + b + 1)
                        dst = (gl if gated else hT)[:, r, h, BF * b:BF * (b + 1), :].rearrange("p b t -> p (b t)")
                        nc.scalar.activation(dst, ps[:, h * NBH + b, :], ACT.Silu if gated else ACT.Gelu
                                             ).then_inc(sem["act"], 1)

            loop(act, body)

        @block.vector
        def _(dve):
            def move_x(k, r):
                dve.wait_ge(sem["turned"], k + 1)
                wait(dve, sem["hid"], (k - 1) * NBK)
                nc.vector.tensor_copy(xT[:, r].rearrange("p i h t -> p (i h t)"), ps[:, 6, :]
                                      ).then_inc(sem["xt"], 1)

            def stage(k, h):
                e = dve.value_load(m["tile_e"][0:1, bass.ds(2 * k + h, 1)], min_val=0, max_val=E - 1)
                wait(dve, sem["hid"], (k - 1) * NBK + (h + 1) * NBH)
                nc.vector.tensor_copy(w1_t[:, h].rearrange("p i f -> p (i f)"),
                                      w1[:, bass.ds(e, 1)].rearrange("p e i f -> p (e i f)")).then_inc(sem["staged"], 1)

            def body(k, r):
                n = tiles(k)
                more = tiles(k + 1) if not (isinstance(k, int) and k == KD - 1) else 0
                for h in range(2):
                    if gated and h < n:
                        dve.wait_ge(sem["hid"], k * NBK + h * NBH + 2)
                        dve.wait_ge(sem["act"], 2 * k + h + 1)
                        if h == 0:
                            wait(dve, sem["out"], k - 1)
                        nc.vector.tensor_tensor(hT[:, r, h].rearrange("p b t -> p (b t)"),
                                                gl[:, r, h].rearrange("p b t -> p (b t)"),
                                                ps[:, h * NBH + 1, :], ALU.mult).then_inc(sem["up"], 1)
                    if h < more:
                        stage(k + 1, h)
                if more:
                    move_x(k + 1, 1 - r)
                dve.wait_ge(sem["out"], k + 1)
                if not (isinstance(k, int) and k < 2):
                    dve.wait_ge(s_y[r], 32 * (times(k, r) - 1))
                nc.vector.tensor_copy(yt[:, r, 0:n, :].rearrange("p h d -> p (h d)"), ps[:, 7, 0:n * D]
                                      ).then_inc(sem["yev"], 1)

            move_x(0, 0)
            for s in loaded[0::2]:
                dve.wait_ge(s, 16)
            for h in range(2):
                stage(0, h)
            loop(dve, body)


def combine(nc, m, L, out=None):
    X, ps = m["X"], m["ps"]
    NB, G = 4, 6
    with ExitStack() as ctx:
        new = ctx.enter_context(semaphores(nc))
        got = ctx.enter_context(nc.sbuf_tensor(f"{L}_got", [P, NB, 2, D], F32))
        mix = ctx.enter_context(nc.sbuf_tensor(f"{L}_mix", [P, NB, 2, D], F32))
        s_got = [new(f"{L}_got{k}") for k in range(NB)]
        s_out = new(f"{L}_stored")
        sem = {k: new(f"{L}_{k}") for k in "scaled mixed turned added".split()}
        block = ctx.enter_context(nc.Block())

        @block.sync
        def _(sp):
            ys = m["ys"][0:2 * TOK, :].rearrange("(s q p) d -> q p s d", s=2, p=P)
            for q in range(NQ):
                wait(sp, sem["mixed"], q - NB + 1)
                sp.dma_start(got[:, q % NB, :, :], ys[q]).then_inc(s_got[q % NB], 16)
            if out is not None:
                for q in range(0, NQ, G):
                    sp.wait_ge(sem["added"], q + G)
                    sp.dma_start(out[:, :, q * P:(q + G) * P], X[:, :, q * P:(q + G) * P]).then_inc(s_out, 16)
                sp.wait_ge(s_out, 16 * (NQ // G))

        @block.scalar
        def _(act):
            for q in range(NQ):
                act.wait_ge(s_got[q % NB], 16 * (q // NB + 1))
                wait(act, sem["mixed"], q - NB + 1)
                nc.scalar.activation(mix[:, q % NB, 0, :], got[:, q % NB, 0, :], ACT.Copy,
                                     scale=m["p01"][:, 0, q:q + 1]).then_inc(sem["scaled"], 1)

        @block.vector
        def _(dve):
            for q in range(NQ + 1):
                if q < NQ:
                    dve.wait_ge(sem["scaled"], q + 1)
                    wait(dve, sem["turned"], q - NB + 1)
                    nc.vector.scalar_tensor_tensor(out=mix[:, q % NB, 1, :], in0=got[:, q % NB, 1, :],
                                                   scalar=m["p01"][:, 1, q:q + 1], in1=mix[:, q % NB, 0, :],
                                                   op0=ALU.mult, op1=ALU.add).then_inc(sem["mixed"], 1)
                if q > 0:
                    b = q - 1
                    dve.wait_ge(sem["turned"], b + 1)
                    x = X[:, :, b * P:(b + 1) * P]
                    nc.vector.tensor_tensor(x, x, ps[:, b % 4, 0:D].rearrange("p (i t) -> p i t", i=2), ALU.add
                                            ).then_inc(sem["added"], 1)

        @block.tensor
        def _(pe):
            for q in range(NQ):
                pe.wait_ge(sem["mixed"], q + 1)
                wait(pe, sem["added"], q - 3)
                for i in range(2):
                    mm = nc.tensor.transpose(ps[:, q % 4, i * P:(i + 1) * P], mix[:, q % NB, 1, i * P:(i + 1) * P],
                                             m["ident"][:])
                mm.then_inc(sem["turned"], 1)


def program(nc, inputs, out):
    with ExitStack() as ctx:
        def sb(name, shape, dt=F32):
            return ctx.enter_context(nc.sbuf_tensor(name, shape, dt))

        m = {
            "ps": ctx.enter_context(nc.psum_tensor("ps", [P, 8, 512], F32)),
            "X": sb("X", [P, 2, TOK]),
            "Xn": sb("Xn", [P, BATCH * IMG]),
            "ident": sb("ident", [P, P]),
            "ones": sb("ones", [P, P]),
            "ones_c": sb("ones_c", [P, P]),
            "sel": sb("sel", [BC, N, P], BF16),
            "mask": sb("mask", [P, 2]),
            "tri": sb("tri", [P, P]),
            "iota": sb("iota", [P, P]),
            "row": sb("row", [P, 1]),
            "spare": sb("spare", [P, KT]),
            "take": sb("take", [P, KT]),
            "give": sb("give", [P, KT]),
            "p01": sb("p01", [P, 2, NQ]),
            "tile_e": sb("tile_e", [P, 2 * KD], mybir.dt.int32),
            "tok_rows": nc.dram_tensor("tok_rows", (TOK, D), F32, kind="Internal").ap(),
            "c_rows": nc.dram_tensor("c_rows", (2, N, T), F32, kind="Internal").ap(),
            "ys": nc.dram_tensor("results", (2 * TOK + KT * TS, D), F32, kind="Internal").ap(),
        }
        gates = sb("gates", [P, 2, 2, P + E])
        s_const = {k: ctx.enter_context(nc.semaphore(f"const_{k}")) for k in
                   "ident sel mask tri iota gate0 gate1 row spare".split()}
        s_x = [ctx.enter_context(nc.semaphore(f"x{k}")) for k in range(BATCH)]
        s_one = ctx.enter_context(nc.semaphore("one"))

        with nc.Block() as block:
            @block.vector
            def _(eng):
                nc.vector.memset(m["ones"][:], 1.0).then_inc(s_one, 1)
                nc.vector.memset(m["ones_c"][:], 1.0 / 256).then_inc(s_one, 1)

        first = ExitStack()
        a, b = PACK["tok"]
        for layer, gated in enumerate((False, True)):
            with nc.sbuf_tensor(f"L{layer}_wp", [P, PACKW], F32) as wp, semaphores(nc) as new:
                tok_in = new(f"L{layer}_pack")
                loads = [(wp[:], inputs[f"pack{layer}"], tok_in)]
                if layer == 0:
                    sel_f = first.enter_context(nc.sbuf_tensor("sel_f", [BC, N, P], F32))
                    by_image = [(m["X"][:, :, k * PIX:(k + 1) * PIX], inputs["x"][:, :, k * PIX:(k + 1) * PIX], s_x[k])
                                for k in range(BATCH)]
                    rest = [(m["ident"][:], "ident"), (sel_f[:], "sel"), (m["mask"][:], "mask"), (m["tri"][:], "tri"),
                            (m["iota"][:], "iota"), (gates[:, 0], "gate0"), (gates[:, 1], "gate1"),
                            (m["row"][:], "row"), (m["spare"][:], "spare")]
                    loads = by_image[0:1] + loads + by_image[1:] + [(dst, inputs[k], s_const[k]) for dst, k in rest]
                    layer_norm(nc, m, "L0c", 1e-6, wp[:, a:b], tok_in, loads, s_x,
                               [s_const[k] for _, k in rest], (m["sel"][:], sel_f[:], s_const["sel"]))
                    first.close()
                else:
                    layer_norm(nc, m, f"L{layer}c", 1e-6, wp[:, a:b], tok_in, loads)
                mamba(nc, m, f"L{layer}", wp)
            F = 1024
            HB = F // P // (2 if gated else 1)
            with semaphores(nc) as new, nc.sbuf_tensor(f"L{layer}_w1", [P, E, 2, F], F32) as w1, \
                    nc.sbuf_tensor(f"L{layer}_w2", [P, E, HB, D], F32) as w2:
                loaded = [new(f"L{layer}_w{k}") for k in range(2 * E)]
                loads = [(w1[:, e].rearrange("p i f -> p (i f)"), inputs[f"up{layer}"][e], loaded[2 * e]) for e in range(E)] \
                    + [(w2[:, e].rearrange("p b d -> p (b d)"), inputs[f"down{layer}"][e], loaded[2 * e + 1]) for e in range(E)]
                layer_norm(nc, m, f"L{layer}t", 1e-5, loads=loads)
                route(nc, m, f"L{layer}r", gates[:, layer], gated)
                experts(nc, m, f"L{layer}e", w1, w2, loaded, F, gated)
            combine(nc, m, f"L{layer}s", out if layer == 1 else None)


def pack(np, g):
    a = np.zeros((P, PACKW), np.float32)

    def put(name, v, r0=0, c0=0):
        a[r0:r0 + v.shape[0], PACK[name][0] + c0:PACK[name][0] + c0 + v.shape[1]] = v

    in_t = g("in_proj_w").T
    for k, taps in enumerate(((2, 3), (0, 1), (3, None), (1, 2), (None, 0))):
        for j, tap in enumerate(taps):
            if tap is not None:
                put("in_u", in_t[:, :P], 64 * j, P * k)
                put("taps", np.tile(g("conv_w")[:, tap], (64, 1)), 64 * j, P * k)
    for j in range(2):
        put("in_z", in_t[:, P:], 64 * j, P * j)
        put("out", g("out_proj_w").T, 0, P * j + 64 * j)
    put("tok", g("global_token").reshape(64, 1), 64)
    put("bc", np.tile(g("x_proj_w")[4:].T, (1, 3)))
    put("xdt", g("x_proj_w")[:4])
    put("dtw", g("dt_proj_w").T)
    put("conv_b", g("conv_b").reshape(P, 1))
    put("dt_b", g("dt_proj_b").reshape(P, 1))
    put("D", g("D").reshape(P, 1))
    put("A", g("A_log"))
    return a


def host_arrays(np, inputs):
    x = np.asarray(inputs["x"]).reshape(BATCH, 64, 2, 2, PIX)
    arrays = {"x": np.ascontiguousarray(x.transpose(3, 1, 2, 0, 4)).reshape(P, 2, TOK)}
    for l in range(2):
        arrays[f"pack{l}"] = pack(np, lambda k: np.asarray(inputs[f"L{l}_conv_{k}"]))
    arrays["ident"] = np.eye(P, dtype=np.float32)
    sel = np.zeros((BC, N, P), np.float32)
    for r in range(BC):
        if r % 32 < N:
            sel[r, r % 32, :] = 1
    arrays["sel"] = sel
    mask = np.zeros((P, 2), np.float32)
    mask[32:, 0] = -1
    mask[64:, 1] = -1
    arrays["mask"] = mask
    arrays["tri"] = np.triu(np.ones((P, P), np.float32), 1)
    arrays["iota"] = np.tile(np.arange(P, dtype=np.float32), (P, 1))
    arrays["row"] = np.arange(P, dtype=np.float32).reshape(P, 1)
    arrays["spare"] = arrays["row"] + np.arange(KT, dtype=np.float32) * np.float32(TS) + np.float32(2 * TOK + P)

    def chans_first(w):
        w = w.reshape(w.shape[:-1] + (64, 2, 2))
        n = w.ndim
        return np.ascontiguousarray(w.transpose(tuple(range(n - 4)) + (n - 1, n - 3, n - 2, n - 4)))

    for l, (up, down) in enumerate((("w1", "w2"), ("w13_weight", "w2_weight"))):
        gate = chans_first(np.asarray(inputs[f"L{l}_ffn_gate_w"])).reshape(P, 2, E)
        arrays[f"gate{l}"] = np.concatenate([np.stack([arrays["ident"]] * 2, 1), gate], 2)
        arrays[f"up{l}"] = chans_first(np.asarray(inputs[f"L{l}_ffn_{up}"])).reshape(E, P, -1)
        w2 = np.asarray(inputs[f"L{l}_ffn_{down}"])
        w2 = w2.reshape(E, 64, 2, 2, -1, P).transpose(0, 5, 4, 2, 3, 1)
        arrays[f"down{l}"] = np.ascontiguousarray(w2).reshape(E, P, -1)
    return arrays


def kernel(**inputs):
    import numpy as np
    import concourse.bacc as bacc
    from concourse.bass_utils import run_bass_kernel_spmd

    nc = bacc.Bacc("TRN2", target_bir_lowering=False, num_devices=1)
    arrays = host_arrays(np, inputs)
    aps = {k: nc.dram_tensor(f"in_{k}", a.shape, mybir.dt.from_np(a.dtype), kind="ExternalInput").ap()
           for k, a in arrays.items()}
    out = nc.dram_tensor("out", (P, 2, TOK), F32, kind="ExternalOutput").ap()
    program(nc, aps, out)
    r = run_bass_kernel_spmd(nc, [{f"in_{k}": a for k, a in arrays.items()}], core_ids=[0])
    y = r.results[0]["out"].reshape(2, 64, 2, BATCH, PIX)
    return np.ascontiguousarray(y.transpose(3, 1, 2, 0, 4)).reshape(BATCH, 256, SIDE, SIDE)
```
